# Optimizing a Trainium2 kernel written in Bass

```python
import numpy as np
import jax
import jax.numpy as jnp

def _softmax(x, axis=-1):
    return jax.nn.softmax(x, axis=axis)

def _gelu(x):
    return jax.nn.gelu(x, approximate=True)

def _silu(x):
    return jax.nn.silu(x)

def _sigmoid(x):
    return jax.nn.sigmoid(x)

def _layernorm(x, axis=-1, eps=1e-05):
    m = jnp.mean(x, axis=axis, keepdims=True)
    v = jnp.var(x, axis=axis, keepdims=True)
    return (x - m) / jnp.sqrt(v + eps)

def _scatter_add(tgt, idx, src, axis=0):
    return tgt.at[idx].add(src)

def _segment_sum(src, seg, n):
    return jax.ops.segment_sum(src, seg, n)
kernel_name = 'mk_gnn_resnorm_d4_gnn_r32_5a0b48'

def setup_inputs(seed: int=0):
    np.random.seed(seed)
    _w = jnp.asarray

    def _rec_inputs():
        import jax
        import jax.numpy as jnp
        _gk = jax.random.key(seed)
        x = -0.0005121 + 1.001 * jax.random.normal(jax.random.fold_in(_gk, 1), (3125, 64), jnp.float32)
        _s = jax.random.randint(jax.random.fold_in(_gk, 2), (25000,), 0, 3125, jnp.int32)
        _d = jax.random.randint(jax.random.fold_in(_gk, 3), (25000,), 0, 3125, jnp.int32)
        _loop = jnp.arange(3125, dtype=jnp.int32)
        src = jnp.concatenate([_s, _d, _loop])
        dst = jnp.concatenate([_d, _s, _loop])
        _o = jnp.argsort(dst, stable=True)
        src = src[_o]
        dst = dst[_o]
        edge_attr_64 = -0.000129727 + 1.00004 * jax.random.normal(jax.random.fold_in(_gk, 12), (53125, 64), jnp.float32)
        edge_weight = 0.000452788 + 0.999756 * jax.random.normal(jax.random.fold_in(_gk, 14), (53125,), jnp.float32)
        edge_weight_n2 = 0.000452788 + 0.999756 * jax.random.normal(jax.random.fold_in(_gk, 15), (53125,), jnp.float32)
        return (x, src, dst, edge_attr_64, edge_weight, edge_weight_n2)
    x, src, dst, edge_attr_64, edge_weight, edge_weight_n2 = _rec_inputs()

    def _L0_gnn_setup():
        import jax, jax.numpy as jnp
        import numpy as np
        N_NODES = 50000
        N_EDGES = 25000
        IN_CH, HID_CH, OUT_CH, HEADS = (64, 32, 64, 8)
        NEG_SLOPE = 0.2

        def _gat_conv(x, src, dst, W, a_s, a_d, b, heads, out_ch, concat):
            n = x.shape[0]
            h = (x @ W).reshape(n, heads, out_ch)
            al_s = jnp.einsum('nhc,hc->nh', h, a_s)
            al_d = jnp.einsum('nhc,hc->nh', h, a_d)
            e = jax.nn.leaky_relu(al_s[src] + al_d[dst], NEG_SLOPE)
            m = jax.ops.segment_max(e, dst, num_segments=n)
            m = jnp.where(jnp.isfinite(m), m, 0.0)
            ex = jnp.exp(e - m[dst])
            denom = jax.ops.segment_sum(ex, dst, num_segments=n)
            alpha = ex / (denom[dst] + 1e-16)
            msg = h[src] * alpha[:, :, None]
            out = jax.ops.segment_sum(msg, dst, num_segments=n)
            out = out.reshape(n, heads * out_ch) if concat else out.mean(axis=1)
            return out + b
        key = jax.random.key(seed)
        ks = jax.random.split(key, 12)
        x = jax.random.normal(ks[0], (N_NODES, IN_CH), dtype=jnp.float32)
        src = jax.random.randint(ks[1], (N_EDGES,), 0, N_NODES)
        dst = jax.random.randint(ks[2], (N_EDGES,), 0, N_NODES)
        edge_index = jnp.stack([src, dst]).astype(jnp.int64)
        g1 = 1.0 / np.sqrt(IN_CH)
        g2 = 1.0 / np.sqrt(HID_CH * HEADS)
        W1 = jax.random.normal(ks[3], (IN_CH, HEADS * HID_CH), dtype=jnp.float32) * g1
        a1_src = jax.random.normal(ks[4], (HEADS, HID_CH), dtype=jnp.float32) * g1
        a1_dst = jax.random.normal(ks[5], (HEADS, HID_CH), dtype=jnp.float32) * g1
        b1 = jnp.zeros((HEADS * HID_CH,), dtype=jnp.float32)
        W2 = jax.random.normal(ks[6], (HEADS * HID_CH, OUT_CH), dtype=jnp.float32) * g2
        a2_src = jax.random.normal(ks[7], (1, OUT_CH), dtype=jnp.float32) * g2
        a2_dst = jax.random.normal(ks[8], (1, OUT_CH), dtype=jnp.float32) * g2
        b2 = jnp.zeros((OUT_CH,), dtype=jnp.float32)
        return {'x': x, 'edge_index': edge_index, 'W1': W1, 'a1_src': a1_src, 'a1_dst': a1_dst, 'b1': b1, 'W2': W2, 'a2_src': a2_src, 'a2_dst': a2_dst, 'b2': b2}
    _L0_gnn_all = _L0_gnn_setup()
    _L0_gnn_in = {k: v for k, v in _L0_gnn_all.items() if k in ('W1', 'a1_src', 'a1_dst', 'b1', 'W2', 'a2_src', 'a2_dst', 'b2')}
    del _L0_gnn_all

    def _L1_gnn_setup():
        import jax, jax.numpy as jnp
        import numpy as np
        LOG2 = float(np.log(2.0))

        def ssp(x):
            return jax.nn.softplus(x) - LOG2
        V, E, F, EIN, H = (50000, 25000, 64, 64, 64)
        key = jax.random.key(seed)
        ks = jax.random.split(key, 16)

        def lin(k, out_d, in_d):
            bound = 1.0 / np.sqrt(in_d)
            k1, k2 = jax.random.split(k)
            W = jax.random.uniform(k1, (out_d, in_d), jnp.float32, -bound, bound)
            b = jax.random.uniform(k2, (out_d,), jnp.float32, -bound, bound)
            return (W, b)
        Wn, bn = lin(ks[0], H, F)
        We1, be1 = lin(ks[1], H, EIN)
        We2, be2 = lin(ks[2], H, H)
        Wc, bc = lin(ks[3], F, H)
        Wp, bp = lin(ks[4], F, F)
        return {'node_feats_in': jax.random.normal(ks[5], (V, F), jnp.float32), 'edge_feats': jax.random.normal(ks[6], (E, EIN), jnp.float32), 'src': jax.random.randint(ks[7], (E,), 0, V, jnp.int32), 'dst': jax.random.randint(ks[8], (E,), 0, V, jnp.int32), 'Wn': Wn, 'bn': bn, 'We1': We1, 'be1': be1, 'We2': We2, 'be2': be2, 'Wc': Wc, 'bc': bc, 'Wp': Wp, 'bp': bp}
    _L1_gnn_all = _L1_gnn_setup()
    _L1_gnn_in = {k: v for k, v in _L1_gnn_all.items() if k in ('Wn', 'bn', 'We1', 'be1', 'We2', 'be2', 'Wc', 'bc', 'Wp', 'bp')}
    del _L1_gnn_all

    def _L2_gnn_setup():
        import jax, jax.numpy as jnp
        import numpy as np
        N, E, D, H, C = (50000, 25000, 64, 2, 64)

        def _transformer_conv(x, src, dst, wq, bq, wk, bk, wv, bv, ws, bs):
            n = x.shape[0]
            q = (x @ wq + bq).reshape(n, H, C)
            k = (x @ wk + bk).reshape(n, H, C)
            v = (x @ wv + bv).reshape(n, H, C)
            qi = q[dst]
            kj = k[src]
            vj = v[src]
            alpha = jnp.einsum('ehc,ehc->eh', qi, kj) / jnp.sqrt(jnp.asarray(C, x.dtype))
            amax = jax.ops.segment_max(alpha, dst, num_segments=n)
            amax = jnp.where(jnp.isfinite(amax), amax, 0.0)
            ex = jnp.exp(alpha - amax[dst])
            denom = jax.ops.segment_sum(ex, dst, num_segments=n)
            a = ex / (denom[dst] + 1e-16)
            out = jax.ops.segment_sum(a[:, :, None] * vj, dst, num_segments=n)
            out = out.mean(axis=1)
            return out + x @ ws + bs
        key = jax.random.key(seed)
        ks = jax.random.split(key, 20)
        x = jax.random.normal(ks[0], (N, D), dtype=jnp.float32)
        edge_index = jax.random.randint(ks[1], (2, E), 0, N, dtype=jnp.int64)
        s = 1.0 / np.sqrt(D)

        def lin(k, din, dout):
            return jax.random.uniform(k, (din, dout), jnp.float32, -s, s)
        inp = {'x': x, 'edge_index': edge_index}
        i = 2
        for l, din in ((1, D), (2, C)):
            for nm, dout in (('wq', H * C), ('wk', H * C), ('wv', H * C), ('ws', C)):
                inp[f'l{l}_{nm}'] = lin(ks[i], din, dout)
                i += 1
                inp[f"l{l}_{nm.replace('w', 'b')}"] = jnp.zeros((dout,), jnp.float32)
        return inp
    _L2_gnn_all = _L2_gnn_setup()
    _L2_gnn_in = {k: v for k, v in _L2_gnn_all.items() if k in ('l1_wq', 'l1_bq', 'l1_wk', 'l1_bk', 'l1_wv', 'l1_bv', 'l1_ws', 'l1_bs', 'l2_wq', 'l2_bq', 'l2_wk', 'l2_bk', 'l2_wv', 'l2_bv', 'l2_ws', 'l2_bs')}
    del _L2_gnn_all

    def _L3_gnn_setup():
        import jax, jax.numpy as jnp
        import numpy as np
        N = 3125
        E = 50000
        D_IN = 64
        D_OUT = 64

        def _spmm(w, src, dst, h, n):
            return jax.ops.segment_sum(w[:, None] * h[src], dst, num_segments=n)
        key = jax.random.key(seed)
        ks = jax.random.split(key, 12)
        stdv = 1.0 / np.sqrt(D_OUT)
        inp = {'x': jax.random.normal(ks[0], (N, D_IN), dtype=jnp.float32), 'w_low': jax.random.uniform(ks[1], (E,), dtype=jnp.float32), 'w_high': jax.random.normal(ks[2], (E,), dtype=jnp.float32), 'W_low': jax.random.uniform(ks[3], (D_IN, D_OUT), jnp.float32, -stdv, stdv), 'W_high': jax.random.uniform(ks[4], (D_IN, D_OUT), jnp.float32, -stdv, stdv), 'W_mlp': jax.random.uniform(ks[5], (D_IN, D_OUT), jnp.float32, -stdv, stdv), 'av_low': jax.random.normal(ks[6], (D_OUT, 1), dtype=jnp.float32), 'av_high': jax.random.normal(ks[7], (D_OUT, 1), dtype=jnp.float32), 'av_mlp': jax.random.normal(ks[8], (D_OUT, 1), dtype=jnp.float32), 'att_vec': jax.random.normal(ks[9], (3, 3), dtype=jnp.float32), 'src': jax.random.randint(ks[10], (E,), 0, N, dtype=jnp.int64 if jax.config.jax_enable_x64 else jnp.int32), 'dst': jax.random.randint(ks[11], (E,), 0, N, dtype=jnp.int64 if jax.config.jax_enable_x64 else jnp.int32)}
        return inp
    _L3_gnn_all = _L3_gnn_setup()
    _L3_gnn_in = {k: v for k, v in _L3_gnn_all.items() if k in ('W_low', 'W_high', 'W_mlp', 'av_low', 'av_high', 'av_mlp', 'att_vec')}
    del _L3_gnn_all
    return {'x': x, 'src': src, 'dst': dst, 'edge_attr_64': edge_attr_64, 'edge_weight': edge_weight, 'edge_weight_n2': edge_weight_n2, 'L0_gnn_W1': _L0_gnn_in['W1'], 'L0_gnn_a1_src': _L0_gnn_in['a1_src'], 'L0_gnn_a1_dst': _L0_gnn_in['a1_dst'], 'L0_gnn_b1': _L0_gnn_in['b1'], 'L0_gnn_W2': _L0_gnn_in['W2'], 'L0_gnn_a2_src': _L0_gnn_in['a2_src'], 'L0_gnn_a2_dst': _L0_gnn_in['a2_dst'], 'L0_gnn_b2': _L0_gnn_in['b2'], 'L1_gnn_Wn': _L1_gnn_in['Wn'], 'L1_gnn_bn': _L1_gnn_in['bn'], 'L1_gnn_We1': _L1_gnn_in['We1'], 'L1_gnn_be1': _L1_gnn_in['be1'], 'L1_gnn_We2': _L1_gnn_in['We2'], 'L1_gnn_be2': _L1_gnn_in['be2'], 'L1_gnn_Wc': _L1_gnn_in['Wc'], 'L1_gnn_bc': _L1_gnn_in['bc'], 'L1_gnn_Wp': _L1_gnn_in['Wp'], 'L1_gnn_bp': _L1_gnn_in['bp'], 'L2_gnn_l1_wq': _L2_gnn_in['l1_wq'], 'L2_gnn_l1_bq': _L2_gnn_in['l1_bq'], 'L2_gnn_l1_wk': _L2_gnn_in['l1_wk'], 'L2_gnn_l1_bk': _L2_gnn_in['l1_bk'], 'L2_gnn_l1_wv': _L2_gnn_in['l1_wv'], 'L2_gnn_l1_bv': _L2_gnn_in['l1_bv'], 'L2_gnn_l1_ws': _L2_gnn_in['l1_ws'], 'L2_gnn_l1_bs': _L2_gnn_in['l1_bs'], 'L2_gnn_l2_wq': _L2_gnn_in['l2_wq'], 'L2_gnn_l2_bq': _L2_gnn_in['l2_bq'], 'L2_gnn_l2_wk': _L2_gnn_in['l2_wk'], 'L2_gnn_l2_bk': _L2_gnn_in['l2_bk'], 'L2_gnn_l2_wv': _L2_gnn_in['l2_wv'], 'L2_gnn_l2_bv': _L2_gnn_in['l2_bv'], 'L2_gnn_l2_ws': _L2_gnn_in['l2_ws'], 'L2_gnn_l2_bs': _L2_gnn_in['l2_bs'], 'L3_gnn_W_low': _L3_gnn_in['W_low'], 'L3_gnn_W_high': _L3_gnn_in['W_high'], 'L3_gnn_W_mlp': _L3_gnn_in['W_mlp'], 'L3_gnn_av_low': _L3_gnn_in['av_low'], 'L3_gnn_av_high': _L3_gnn_in['av_high'], 'L3_gnn_av_mlp': _L3_gnn_in['av_mlp'], 'L3_gnn_att_vec': _L3_gnn_in['att_vec']}

def reference(x, src, dst, edge_attr_64, edge_weight, edge_weight_n2, L0_gnn_W1, L0_gnn_a1_src, L0_gnn_a1_dst, L0_gnn_b1, L0_gnn_W2, L0_gnn_a2_src, L0_gnn_a2_dst, L0_gnn_b2, L1_gnn_Wn, L1_gnn_bn, L1_gnn_We1, L1_gnn_be1, L1_gnn_We2, L1_gnn_be2, L1_gnn_Wc, L1_gnn_bc, L1_gnn_Wp, L1_gnn_bp, L2_gnn_l1_wq, L2_gnn_l1_bq, L2_gnn_l1_wk, L2_gnn_l1_bk, L2_gnn_l1_wv, L2_gnn_l1_bv, L2_gnn_l1_ws, L2_gnn_l1_bs, L2_gnn_l2_wq, L2_gnn_l2_bq, L2_gnn_l2_wk, L2_gnn_l2_bk, L2_gnn_l2_wv, L2_gnn_l2_bv, L2_gnn_l2_ws, L2_gnn_l2_bs, L3_gnn_W_low, L3_gnn_W_high, L3_gnn_W_mlp, L3_gnn_av_low, L3_gnn_av_high, L3_gnn_av_mlp, L3_gnn_att_vec):
    import jax
    import jax.numpy as jnp

    def _L0_gnn_ref(x, edge_index, W1, a1_src, a1_dst, b1, W2, a2_src, a2_dst, b2):
        import jax, jax.numpy as jnp
        import numpy as np
        N_NODES = 50000
        N_EDGES = 25000
        IN_CH, HID_CH, OUT_CH, HEADS = (64, 32, 64, 8)
        NEG_SLOPE = 0.2

        def _gat_conv(x, src, dst, W, a_s, a_d, b, heads, out_ch, concat):
            n = x.shape[0]
            h = (x @ W).reshape(n, heads, out_ch)
            al_s = jnp.einsum('nhc,hc->nh', h, a_s)
            al_d = jnp.einsum('nhc,hc->nh', h, a_d)
            e = jax.nn.leaky_relu(al_s[src] + al_d[dst], NEG_SLOPE)
            m = jax.ops.segment_max(e, dst, num_segments=n)
            m = jnp.where(jnp.isfinite(m), m, 0.0)
            ex = jnp.exp(e - m[dst])
            denom = jax.ops.segment_sum(ex, dst, num_segments=n)
            alpha = ex / (denom[dst] + 1e-16)
            msg = h[src] * alpha[:, :, None]
            out = jax.ops.segment_sum(msg, dst, num_segments=n)
            out = out.reshape(n, heads * out_ch) if concat else out.mean(axis=1)
            return out + b
        n = x.shape[0]
        loops = jnp.arange(n, dtype=edge_index.dtype)
        src = jnp.concatenate([edge_index[0], loops])
        dst = jnp.concatenate([edge_index[1], loops])
        h = _gat_conv(x, src, dst, W1, a1_src, a1_dst, b1, HEADS, HID_CH, True)
        h = jax.nn.elu(h)
        return _gat_conv(h, src, dst, W2, a2_src, a2_dst, b2, 1, OUT_CH, False)

    def _L1_gnn_ref(node_feats_in, edge_feats, src, dst, Wn, bn, We1, be1, We2, be2, Wc, bc, Wp, bp):
        import jax, jax.numpy as jnp
        import numpy as np
        LOG2 = float(np.log(2.0))

        def ssp(x):
            return jax.nn.softplus(x) - LOG2
        V = node_feats_in.shape[0]
        h = node_feats_in @ Wn.T + bn
        h_src = h[src]
        w = ssp(edge_feats @ We1.T + be1)
        w = ssp(w @ We2.T + be2)
        m = h_src * w
        agg = jax.ops.segment_sum(m, dst, num_segments=V)
        out = ssp(agg @ Wc.T + bc)
        return out @ Wp.T + bp

    def _L2_gnn_ref(x, edge_index, l1_wq, l1_bq, l1_wk, l1_bk, l1_wv, l1_bv, l1_ws, l1_bs, l2_wq, l2_bq, l2_wk, l2_bk, l2_wv, l2_bv, l2_ws, l2_bs):
        import jax, jax.numpy as jnp
        import numpy as np
        N, E, D, H, C = (50000, 25000, 64, 2, 64)

        def _transformer_conv(x, src, dst, wq, bq, wk, bk, wv, bv, ws, bs):
            n = x.shape[0]
            q = (x @ wq + bq).reshape(n, H, C)
            k = (x @ wk + bk).reshape(n, H, C)
            v = (x @ wv + bv).reshape(n, H, C)
            qi = q[dst]
            kj = k[src]
            vj = v[src]
            alpha = jnp.einsum('ehc,ehc->eh', qi, kj) / jnp.sqrt(jnp.asarray(C, x.dtype))
            amax = jax.ops.segment_max(alpha, dst, num_segments=n)
            amax = jnp.where(jnp.isfinite(amax), amax, 0.0)
            ex = jnp.exp(alpha - amax[dst])
            denom = jax.ops.segment_sum(ex, dst, num_segments=n)
            a = ex / (denom[dst] + 1e-16)
            out = jax.ops.segment_sum(a[:, :, None] * vj, dst, num_segments=n)
            out = out.mean(axis=1)
            return out + x @ ws + bs
        src, dst = (edge_index[0], edge_index[1])
        h = _transformer_conv(x, src, dst, l1_wq, l1_bq, l1_wk, l1_bk, l1_wv, l1_bv, l1_ws, l1_bs)
        h = _transformer_conv(h, src, dst, l2_wq, l2_bq, l2_wk, l2_bk, l2_wv, l2_bv, l2_ws, l2_bs)
        return h

    def _L3_gnn_ref(x, w_low, w_high, W_low, W_high, W_mlp, av_low, av_high, av_mlp, att_vec, src, dst):
        import jax, jax.numpy as jnp
        import numpy as np
        N = 3125
        E = 50000
        D_IN = 64
        D_OUT = 64

        def _spmm(w, src, dst, h, n):
            return jax.ops.segment_sum(w[:, None] * h[src], dst, num_segments=n)
        n = x.shape[0]
        h_low = jax.nn.relu(_spmm(w_low, src, dst, x @ W_low, n))
        h_high = jax.nn.relu(_spmm(w_high, src, dst, x @ W_high, n))
        h_mlp = jax.nn.relu(x @ W_mlp)
        feats = jnp.concatenate([h_low @ av_low, h_high @ av_high, h_mlp @ av_mlp], axis=1)
        logits = jax.nn.sigmoid(feats) @ att_vec / 3.0
        att = jax.nn.softmax(logits, axis=1)
        out = 3.0 * (att[:, 0:1] * h_low + att[:, 1:2] * h_high + att[:, 2:3] * h_mlp)
        return out
    edge_index = jnp.stack([src, dst])
    x = _layernorm(x + _L0_gnn_ref(x, edge_index, L0_gnn_W1, L0_gnn_a1_src, L0_gnn_a1_dst, L0_gnn_b1, L0_gnn_W2, L0_gnn_a2_src, L0_gnn_a2_dst, L0_gnn_b2), axis=-1)
    x = _layernorm(x + _L1_gnn_ref(x, edge_attr_64, src, dst, L1_gnn_Wn, L1_gnn_bn, L1_gnn_We1, L1_gnn_be1, L1_gnn_We2, L1_gnn_be2, L1_gnn_Wc, L1_gnn_bc, L1_gnn_Wp, L1_gnn_bp), axis=-1)
    x = _layernorm(x + _L2_gnn_ref(x, edge_index, L2_gnn_l1_wq, L2_gnn_l1_bq, L2_gnn_l1_wk, L2_gnn_l1_bk, L2_gnn_l1_wv, L2_gnn_l1_bv, L2_gnn_l1_ws, L2_gnn_l1_bs, L2_gnn_l2_wq, L2_gnn_l2_bq, L2_gnn_l2_wk, L2_gnn_l2_bk, L2_gnn_l2_wv, L2_gnn_l2_bv, L2_gnn_l2_ws, L2_gnn_l2_bs), axis=-1)
    x = _layernorm(x + _L3_gnn_ref(x, edge_weight, edge_weight_n2, L3_gnn_W_low, L3_gnn_W_high, L3_gnn_W_mlp, L3_gnn_av_low, L3_gnn_av_high, L3_gnn_av_mlp, L3_gnn_att_vec, src, dst), axis=-1)
    return x

_drawn_inputs = setup_inputs


def setup_inputs(seed=0):
    import zlib

    import numpy as np

    out = dict(_drawn_inputs(seed))
    spreads = {'L0_gnn_b1': (0.0, 0.1),
     'L0_gnn_b2': (0.0, 0.1),
     'L2_gnn_l1_bq': (0.0, 0.8),
     'L2_gnn_l1_bk': (0.0, 0.8),
     'L2_gnn_l1_bv': (0.0, 0.1),
     'L2_gnn_l1_bs': (0.0, 0.1),
     'L2_gnn_l2_bq': (0.0, 0.8),
     'L2_gnn_l2_bk': (0.0, 0.8),
     'L2_gnn_l2_bv': (0.0, 0.1),
     'L2_gnn_l2_bs': (0.0, 0.1)}
    factors = {'L0_gnn_a1_dst': 3.711,
     'L0_gnn_a2_src': 7.09,
     'L0_gnn_a2_dst': 8.0,
     'L1_gnn_bn': 4.725,
     'L1_gnn_be1': 8.0,
     'L1_gnn_be2': 2.777,
     'L2_gnn_l2_wq': 6.277,
     'L2_gnn_l2_wk': 6.12}
    for name, (base, spread) in spreads.items():
        noise = np.random.default_rng([zlib.crc32(name.encode()), seed]).standard_normal(out[name].shape)
        drawn = base * np.exp(spread * noise) if base else spread * noise
        out[name] = jnp.asarray(drawn.astype(out[name].dtype))
    for name, factor in factors.items():
        out[name] = (out[name] * factor).astype(out[name].dtype)
    return out
```

```python
from contextlib import ExitStack

import concourse.bass as bass
from concourse import mybir

P = 128
N, D, E = 3125, 64, 53125
KN = -(-N // P)
NPAD = KN * P
T = -(-E // P)
T += -T % 8
EPAD = T * P
S = T + KN - 1
G = 8
NG = T // G
NB = S // G
TC = 4
TP = T // TC
RING = 4
X1 = D + 1
HEADS, HID = 8, 32
BIG = 1e30
LOG2 = 0.6931471805599453
EPS = 1e-5
assert S % G == 0 and NG % RING == 0 and TP <= P

F32 = mybir.dt.float32
I32 = mybir.dt.int32
ALU = mybir.AluOpType
ACT = mybir.ActivationFunctionType
AX = mybir.AxisListType.X


class Signal:

    def __init__(self, handle):
        self.sem, self.base = handle, 0


def build(nc, a, out):
    with ExitStack() as ctx:
        def sb(name, shape, dt=F32):
            return ctx.enter_context(nc.sbuf_tensor(name, shape, dt))

        def sem(name):
            return ctx.enter_context(nc.semaphore(name))

        ps = ctx.enter_context(nc.psum_tensor("ps", [P, 8, 512], F32))

        xs = sb("xs", [P, KN, X1])
        x_all = sb("x_all", [P, T * X1])
        arena = sb("arena", [P, KN * HEADS * X1])
        score = sb("score", [P, T * HEADS])
        dsel = sb("dsel", [P, S])
        src_i = sb("src_i", [P, T], I32)
        ident = sb("ident", [P, P])
        lane = sb("lane", [P, P])
        flag_f = sb("flag_f", [TP, TC * P])
        flag_b = sb("flag_b", [TP, TC * P])
        in_first = sb("in_first", [TP, TC, P])
        in_last = sb("in_last", [TP, TC, P])
        chains = sb("chains", [33, 3 * T])
        rows = chains[0:HEADS, :].rearrange("p (n t) -> p n t", n=3)
        steps_i = chains[32:33, 0:2 * S].bitcast(I32).rearrange("p (n s) -> p n s", n=2)
        oh_s = sb("oh_s", [P, 4, P])
        msg = sb("msg", [P, 4, HEADS * X1])
        idx = sb("idx", [P, RING, G], I32)
        wbuf = sb("wbuf", [P, 456])
        small = sb("small", [P, 6 * KN])

        def view(t, at, *shape):
            n = 1
            for k in shape:
                n *= k
            v = t[:, at:at + n]
            if len(shape) == 2:
                v = v.rearrange("p (a b) -> p a b", b=shape[1])
            if len(shape) == 3:
                v = v.rearrange("p (a b c) -> p a b c", b=shape[1], c=shape[2])
            return v

        xa = view(x_all, 0, T, X1)

        loaded = Signal(sem("loaded"))
        stored = Signal(sem("stored"))
        chain = Signal(sem("vector_chain"))
        to_act = Signal(sem("vector_for_scalar"))
        from_act = Signal(sem("scalar_for_vector"))
        to_pe = Signal(sem("vector_for_tensor"))
        from_pe = Signal(sem("tensor_for_vector"))
        pool_done = Signal(sem("pool_done"))
        turned = Signal(sem("turned"))
        turned_sb = Signal(sem("turned_sb"))
        product = Signal(sem("product"))
        taken = Signal(sem("taken"))

        class Vector:

            def __init__(self, eng):
                self.eng = eng

            def __getitem__(self, ins):
                chain.base += 1
                ins.then_inc(chain.sem, 1)
                self.eng.wait_ge(chain.sem, chain.base)

        def hand(eng, signal):
            signal.base += 1
            eng.nop().then_inc(signal.sem, 1)

        def load(pairs):
            with nc.Block() as block:
                @block.sync
                def _(sp):
                    for dst, src in pairs:
                        sp.dma_start(dst, src).then_inc(loaded.sem, 16)
                        loaded.base += 16
                    sp.wait_ge(loaded.sem, loaded.base)

        def store(pairs):
            with nc.Block() as block:
                @block.sync
                def _(sp):
                    for dst, src in pairs:
                        sp.dma_start(dst, src).then_inc(stored.sem, 16)
                        stored.base += 16
                    sp.wait_ge(stored.sem, stored.base)

        def dense(sources, weights, dest):
            K = [s.shape[2] for s in sources]
            M = len(sources)
            width = dest.shape[2]
            blocks = [(i, min(4, KN - i)) for i in range(0, KN, 4)]
            xT = view(x_all, T * X1 - 2 * 3 * 512, 2, 3, 512)
            t0, s0, p0, k0 = turned.base, turned_sb.base, product.base, taken.base

            with nc.Block() as block:
                @block.tensor
                def _(pe):
                    def turn(n):
                        i, nj = blocks[n]
                        if n >= 2:
                            pe.wait_ge(turned_sb.sem, s0 + n - 1)
                        for m in range(M):
                            for j in range(nj):
                                last = nc.tensor.transpose(ps[0:K[m], 3 * (n % 2) + m, j * P:(j + 1) * P],
                                                           sources[m][:, i + j, :], ident[:, :])
                        last.then_inc(turned.sem, 1)

                    def multiply(n):
                        i, nj = blocks[n]
                        pe.wait_ge(turned_sb.sem, s0 + n + 1)
                        if n >= 1:
                            pe.wait_ge(taken.sem, k0 + n)
                        for j in range(nj):
                            for m in range(M):
                                last = nc.tensor.matmul(
                                    ps[:, 6 + j // 2, (j % 2) * 256:(j % 2) * 256 + width],
                                    xT[0:K[m], n % 2, m, j * P:(j + 1) * P], weights[m],
                                    start=(m == 0), stop=(m == M - 1))
                        last.then_inc(product.sem, 1)

                    turn(0)
                    for n in range(len(blocks)):
                        if n + 1 < len(blocks):
                            turn(n + 1)
                        multiply(n)

                @block.scalar
                def _(act):
                    for n, (i, nj) in enumerate(blocks):
                        act.wait_ge(turned.sem, t0 + n + 1)
                        if n >= 2:
                            act.wait_ge(product.sem, p0 + n - 1)
                        for m in range(M):
                            last = nc.scalar.copy(xT[0:K[m], n % 2, m, 0:nj * P],
                                                  ps[0:K[m], 3 * (n % 2) + m, 0:nj * P])
                        last.then_inc(turned_sb.sem, 1)

                @block.vector
                def _(dve):
                    for n, (i, nj) in enumerate(blocks):
                        dve.wait_ge(product.sem, p0 + n + 1)
                        for b in range(-(-nj // 2)):
                            c = min(2, nj - 2 * b)
                            got = ps[:, 6 + b, :].rearrange("p (c n) -> p c n", c=2)[:, 0:c, 0:width]
                            last = nc.vector.tensor_copy(dest[:, i + 2 * b:i + 2 * b + c, :], got)
                        last.then_inc(taken.sem, 1)
            turned.base += len(blocks)
            turned_sb.base += len(blocks)
            product.base += len(blocks)
            taken.base += len(blocks)

        def on_vector(steps, scalar=()):
            with nc.Block() as block:
                count = [0, 0]
                a0, r0 = to_act.base, from_act.base

                @block.vector
                def _(dve):
                    v = Vector(dve)

                    def ask():
                        count[0] += 1
                        dve.nop().then_inc(to_act.sem, 1)
                        dve.wait_ge(from_act.sem, r0 + count[0])

                    steps(v, ask)

                if scalar:
                    @block.scalar
                    def _(act):
                        for n, run in enumerate(scalar):
                            act.wait_ge(to_act.sem, a0 + n + 1)
                            run().then_inc(from_act.sem, 1)
                to_act.base += len(scalar)
                from_act.base += len(scalar)

        V = nc.vector

        def bc(ap, *shape):
            return ap.to_broadcast([ap.shape[0], *shape])

        def layernorm(y, scratch, dest):
            mean, var = small[:, 0:KN], small[:, KN:2 * KN]
            std, inv = small[:, 2 * KN:3 * KN], small[:, 3 * KN:4 * KN]

            def steps(v, ask):
                v[V.tensor_reduce(mean, y, AX, ALU.add)]
                v[V.tensor_scalar(mean, mean, 1.0 / D, None, ALU.mult)]
                v[V.tensor_tensor(y, y, bc(mean.unsqueeze(2), KN, D), ALU.subtract)]
                v[V.tensor_tensor(scratch, y, y, ALU.mult)]
                v[V.tensor_reduce(var, scratch, AX, ALU.add)]
                v[V.tensor_scalar(var, var, 1.0 / D, EPS, ALU.mult, ALU.add)]
                ask()
                v[V.reciprocal(inv, std)]
                v[V.tensor_tensor(dest, y, bc(inv.unsqueeze(2), KN, D), ALU.mult)]

            on_vector(steps, [lambda: nc.scalar.activation(std, var, ACT.Sqrt)])

        RW = D + HEADS
        ring_at, oh_at = 0, RING * G * RW
        ohT_at = oh_at + 2 * G * P
        prod_at = ohT_at + 2 * G * P
        tab_at = prod_at + G * 2 * X1

        def pool_gathers(block, table, width, ring, gathered, free):
            @block.gpsimd
            def _(pool):
                staged = sem_take("staged")

                def stage(slot, g):
                    cols = src_i[:, g * G:(g + 1) * G] if isinstance(g, int) else src_i[:, bass.ds(g * G, G)]
                    pool.tensor_copy(idx[:, slot, :], cols).then_inc(staged, 1)

                def group(slot, g, more=True):
                    if not isinstance(g, int) or g >= RING - 1:
                        pool.wait_ge(free, g - (RING - 2))
                    pool.wait_ge(staged, g + 1)
                    if more:
                        stage((slot + 1) % RING, g + 1)
                    for j in range(G):
                        pool.indirect_dma_start(
                            out=ring[:, slot, j, :], out_offset=None, in_=table,
                            in_offset=bass.IndirectOffsetOnAxis(ap=idx[:, slot, j:j + 1], axis=0),
                        ).then_inc(gathered[slot], 16)

                stage(0, 0)
                for slot in range(RING):
                    group(slot, slot)
                with pool.Fori(1, NG // RING - 1) as r:
                    for slot in range(RING):
                        group(slot, r * RING + slot)
                for slot in range(RING):
                    group(slot, NG - RING + slot, more=slot + 1 < RING)

        taken_sems = {}

        def sem_take(name):
            n = taken_sems.get(name, 0)
            taken_sems[name] = n + 1
            taken_now.append(nc.alloc_semaphore(name=f"{name}_{n}"))
            return taken_now[-1]

        taken_now = []

        def recycle():
            nc.clear_and_free_semaphores(taken_now)
            nc.all_engine_barrier()
            taken_now.clear()

        def gather_scores(table, width, H, tab, products):
            F = H * X1 if products else H
            ring = view(arena, ring_at, RING, G, RW)[:, :, :, 0:width]
            ring = view(arena, ring_at, RING * G * width).rearrange("p (r g w) -> p r g w", r=RING, g=G)
            oh = view(arena, oh_at, 2, G, P)
            ohT = view(arena, ohT_at, 2, G * P)
            prod = view(arena, prod_at, G, 2 * X1)
            dot = view(small, 0, G, 2)
            sc = view(score, 0, T, H)
            gathered = [sem_take("gathered") for _ in range(RING)]
            free = sem_take("ring_taken")
            oh_ready, oh_turned = sem_take("onehot_ready"), sem_take("onehot_turned")
            ohT_ready, given = sem_take("onehotT_ready"), sem_take("dst_rows_ready")
            added, multiplied, summed = sem_take("score_added"), sem_take("dst_rows_multiplied"), sem_take("dots_summed")

            with nc.Block() as block:
                pool_gathers(block, table, width, ring, gathered, free)

                @block.scalar
                def _(act):
                    def turn_out(par, g):
                        act.wait_ge(oh_turned, g + 1)
                        for b in range(2):
                            last = nc.scalar.copy(ohT[:, par, b * 512:(b + 1) * 512], ps[:, 2 * par + b, :])
                        last.then_inc(ohT_ready, 1)

                    with act.Fori(0, NG // RING) as r:
                        for slot in range(RING):
                            g = r * RING + slot
                            turn_out(slot % 2, g)
                            act.wait_ge(gathered[slot], (r + 1) * (16 * G))
                            if not products:
                                nc.scalar.copy(sc[:, bass.ds(g * G, G), :], ring[:, slot, :, D:D + H])
                            nc.scalar.copy(xa[:, bass.ds(g * G, G), 0:D], ring[:, slot, :, 0:D]).then_inc(free, 1)
                    for g in range(NG, NB):
                        turn_out(g % 2, g)

                @block.tensor
                def _(pe):
                    def turn(par, g):
                        pe.wait_ge(oh_ready, g + 1)
                        for j in range(G):
                            last = nc.tensor.transpose(ps[:, 2 * par + j // 4, (j % 4) * P:(j % 4 + 1) * P],
                                                       oh[:, par, j, :], ident[:, :])
                        last.then_inc(oh_turned, 1)

                    def rows_of_dst(par, g):
                        blocks = pe_load(pe, steps_i[0:1, 1, bass.ds(g * G, G)] if not isinstance(g, int)
                                         else steps_i[0:1, 1, g * G:(g + 1) * G], KN - 1)
                        pe.wait_ge(ohT_ready, g + 1)
                        pe.wait_ge(added, g * G + 1)
                        for j in range(G):
                            last = nc.tensor.matmul(ps[:, 4 + j // 2, (j % 2) * 256:(j % 2) * 256 + F],
                                                    ohT[:, par, j * P:(j + 1) * P],
                                                    tab[:, bass.ds(blocks[j], 1), :].rearrange("p a f -> p (a f)"),
                                                    start=True, stop=True)
                        last.then_inc(given, 1)

                    turn(0, 0)
                    with pe.Fori(0, NG // RING) as r:
                        for slot in range(RING):
                            turn((slot + 1) % 2, r * RING + (slot + 1))
                            rows_of_dst(slot % 2, r * RING + slot)
                    for g in range(NG, NB):
                        if g + 1 < NB:
                            turn((g + 1) % 2, g + 1)
                        rows_of_dst(g % 2, g)

                @block.vector
                def _(dve):
                    def onehots(par, g):
                        for j in range(G):
                            at = g * G + j
                            last = V.tensor_scalar(oh[:, par, j, :], lane[:, :],
                                                   dsel[:, bass.ds(at, 1)] if not isinstance(at, int) else dsel[:, at:at + 1],
                                                   None, ALU.is_equal)
                        last.then_inc(oh_ready, 1)

                    def add_scores(g, wait_rows):
                        tiles = dve_load(dve, steps_i[0:1, 0, bass.ds(g * G, G)] if not isinstance(g, int)
                                         else steps_i[0:1, 0, g * G:(g + 1) * G], T - 1)
                        dve.wait_ge(given, g + 1)
                        if wait_rows:
                            dve.wait_ge(free, g + 1)
                        got = [ps[:, 4 + j // 2, (j % 2) * 256:(j % 2) * 256 + F] for j in range(G)]
                        if products:
                            for j in range(G):
                                last = V.tensor_tensor(
                                    prod[:, j, :].rearrange("p (h x) -> p h x", h=H),
                                    got[j].rearrange("p (h x) -> p h x", h=H),
                                    xa[:, bass.ds(tiles[j], 1), :].to_broadcast([P, H, X1]), ALU.mult)
                            last.then_inc(multiplied, 1)
                            dve.wait_ge(multiplied, g + 1)
                            V.tensor_reduce(dot.rearrange("p g h -> p (g h)"),
                                            prod.rearrange("p g (h x) -> p (g h) x", h=H), AX, ALU.add).then_inc(summed, 1)
                            dve.wait_ge(summed, g + 1)
                            got = [dot[:, j, :] for j in range(G)]
                        for j in range(G):
                            dve.wait_ge(added, g * G + (j + 1))
                            at = sc[:, bass.ds(tiles[j], 1), :].rearrange("p a h -> p (a h)")
                            V.tensor_tensor(at, at, got[j], ALU.add).then_inc(added, 1)

                    if products:
                        V.memset(sc, 0.0)
                    V.memset(xa[:, :, D:X1], 1.0).then_inc(added, 1)
                    onehots(0, 0)
                    with dve.Fori(0, NG // RING) as r:
                        for slot in range(RING):
                            onehots((slot + 1) % 2, r * RING + (slot + 1))
                            add_scores(r * RING + slot, True)
                    for g in range(NG, NB):
                        if g + 1 < NB:
                            onehots((g + 1) % 2, g + 1)
                        add_scores(g, False)

        def dve_load(eng, ap, top):
            return nc.values_load_multi_w_load_instructions(ap, engines=(mybir.EngineType.DVE,), min_val=0, max_val=top,
                                                            skip_runtime_bounds_check_because="staircase of the edge tiles")[1]

        def pe_load(eng, ap, top):
            return nc.values_load_multi_w_load_instructions(ap, engines=(mybir.EngineType.PE,), min_val=0, max_val=top,
                                                            skip_runtime_bounds_check_because="staircase of the edge tiles")[1]

        def aggregate_tensor(pe, B, H, steps, ready, done):
            halves = 2 if H > 4 else 1
            W = H * X1 // halves
            for j in range(B):
                pe.wait_ge(ready, steps(j) + 1)
                for b in range(halves):
                    last = nc.tensor.matmul(ps[:, (j % 4) * halves + b, 0:W], oh_s[:, j % 4, :],
                                            msg[:, j % 4, b * W:(b + 1) * W], start=True, stop=True)
                last.then_inc(done, 1)

        def aggregate_vector(dve, H, acc, weight, g0, steps, ready, done, summed):
            halves = 2 if H > 4 else 1
            W = H * X1 // halves
            sl = (lambda row: steps_i[0:1, row, bass.ds(g0, 4)]) if not isinstance(g0, int) else (
                lambda row: steps_i[0:1, row, g0:g0 + 4])
            tiles = dve_load(dve, sl(0), T - 1)
            blocks = dve_load(dve, sl(1), KN - 1)
            for j in range(4):
                at = dsel[:, bass.ds(g0 + j, 1)] if not isinstance(g0, int) else dsel[:, g0 + j:g0 + j + 1]
                V.tensor_scalar(oh_s[:, j, :], lane[:, :], at, None, ALU.is_equal)
                row = xa[:, bass.ds(tiles[j], 1), :]
                if weight is None:
                    V.tensor_copy(msg[:, j, 0:X1], row.rearrange("p a x -> p (a x)")).then_inc(ready, 1)
                else:
                    V.tensor_tensor(msg[:, j, 0:H * X1].rearrange("p (h x) -> p h x", h=H),
                                    row.to_broadcast([P, H, X1]),
                                    weight[:, bass.ds(tiles[j], 1), :].rearrange("p a h -> p h a").to_broadcast([P, H, X1]),
                                    ALU.mult).then_inc(ready, 1)
            for j in range(4):
                dve.wait_ge(done, steps(j) + 1)
                dve.wait_ge(summed, steps(j) + 1)
                at = acc[:, bass.ds(blocks[j], 1), :].rearrange("p a (b w) -> p (a b) w", b=halves)
                V.tensor_tensor(at, at, ps[:, j * halves:(j + 1) * halves, 0:W], ALU.add).then_inc(summed, 1)

        def aggregate(H, weight):
            acc = view(arena, 0, KN, H * X1)
            ready, done, summed = sem_take("messages_ready"), sem_take("step_summed"), sem_take("node_summed")
            with nc.Block() as block:
                @block.tensor
                def _(pe):
                    with pe.Fori(0, S // 4) as r:
                        aggregate_tensor(pe, 4, H, lambda j: r * 4 + j, ready, done)

                @block.vector
                def _(dve):
                    V.memset(acc, 0.0).then_inc(summed, 1)
                    with dve.Fori(0, S // 4) as r:
                        aggregate_vector(dve, H, acc, weight, r * 4, lambda j: r * 4 + j, ready, done, summed)
            return acc

        def softmax_numerators(H, leaky):
            sc = view(score, 0, T, H)
            scT = view(arena, 0, H, TC * P)[0:TP]
            fwd = view(arena, HEADS * 512, H, TC * P)[0:TP]
            bwd = view(arena, 2 * HEADS * 512, H, TC * P)[0:TP]
            tail = msg[0:H, 0, 0:T]
            head = msg[0:H, 1, 0:T]
            run = msg[0:H, 2, 0:T]
            back = msg[0:H, 3, 0:T]
            carry = view(small, 0, 2, TC * H)[0:TP]
            scores_ready, turned_in = sem_take("scores_ready"), sem_take("scores_turned")
            sT_ready, scanned = sem_take("scoresT_ready"), sem_take("scanned")
            ends_out, chained = sem_take("tile_ends_turned"), sem_take("tiles_chained")
            carry_out, centred = sem_take("carries_turned"), sem_take("centred")
            exped, turned_out = sem_take("exp_done"), sem_take("exp_turned")
            is_first = view(arena, 3 * HEADS * 512, TC, P)[0:TP]
            first_max = view(arena, 2 * HEADS * 512, T, H)
            max_ready, max_out, exp_taken = sem_take("max_ready"), sem_take("max_turned"), sem_take("exp_taken")

            with nc.Block() as block:
                @block.tensor
                def _(pe):
                    pe.wait_ge(scores_ready, 1)
                    for h in range(H):
                        for c in range(TC):
                            last = nc.tensor.transpose(ps[0:TP, h, c * P:(c + 1) * P],
                                                       sc[:, c * TP:(c + 1) * TP, h], ident[:, :])
                        last.then_inc(turned_in, 1)
                    pe.wait_ge(scanned, 1)
                    for n, (of, at) in enumerate(((fwd, P - 1), (bwd, 0))):
                        for c in range(TC):
                            last = nc.tensor.transpose(ps[0:H, n, c * TP:(c + 1) * TP],
                                                       of[:, :, c * P + at], ident[0:TP, 0:TP])
                    last.then_inc(ends_out, 1)
                    pe.wait_ge(chained, 1)
                    for n, row in enumerate((run, back)):
                        for c in range(TC):
                            last = nc.tensor.transpose(ps[0:TP, n, c * H:(c + 1) * H], row[:, c * TP:(c + 1) * TP],
                                                       ident[0:H, 0:H])
                    last.then_inc(carry_out, 1)
                    for h in range(H):
                        pe.wait_ge(exped, h + 1)
                        for c in range(TC):
                            last = nc.tensor.transpose(ps[:, h, c * TP:(c + 1) * TP],
                                                       scT[:, h, c * P:(c + 1) * P], ident[0:TP, 0:TP])
                        last.then_inc(turned_out, 1)
                    if leaky:
                        for h in range(H):
                            pe.wait_ge(max_ready, h + 1)
                            pe.wait_ge(exp_taken, h + 1)
                            for c in range(TC):
                                last = nc.tensor.transpose(ps[:, h, c * TP:(c + 1) * TP],
                                                           fwd[:, h, c * P:(c + 1) * P], ident[0:TP, 0:TP])
                            last.then_inc(max_out, 1)

                @block.scalar
                def _(act):
                    for h in range(H):
                        act.wait_ge(turned_in, h + 1)
                        nc.scalar.copy(scT[:, h, :], ps[0:TP, h, :]).then_inc(sT_ready, 1)
                    for h in range(H):
                        act.wait_ge(centred, h + 1)
                        nc.scalar.activation(scT[:, h, :], scT[:, h, :], ACT.Exp).then_inc(exped, 1)

                @block.vector
                def _(dve):
                    v = Vector(dve)
                    if leaky:
                        V.scalar_tensor_tensor(out=sc, in0=sc, scalar=0.2, in1=sc, op0=ALU.mult,
                                               op1=ALU.max).then_inc(scores_ready, 1)
                    else:
                        dve.nop().then_inc(scores_ready, 1)
                    for h in range(H):
                        dve.wait_ge(sT_ready, h + 1)
                        V.tensor_tensor_scan(fwd[:, h, :], flag_f[:, :], scT[:, h, :], -BIG, ALU.add, ALU.max)
                        last = V.tensor_tensor_scan(bwd[:, h, ::-1], flag_b[:, ::-1], scT[:, h, ::-1], -BIG, ALU.add, ALU.max)
                    v[last]
                    dve.nop().then_inc(scanned, 1)
                    dve.wait_ge(ends_out, 1)
                    v[V.tensor_copy(tail, ps[0:H, 0, 0:T])]
                    v[V.tensor_copy(head, ps[0:H, 1, 0:T])]
                    v[V.tensor_tensor(fwd, fwd, bwd, ALU.max)]
                    v[V.tensor_tensor_scan(tail, rows[0:H, 0, :], tail, -BIG, ALU.add, ALU.max)]
                    v[V.tensor_tensor_scan(head[:, ::-1], rows[0:H, 2, ::-1], head[:, ::-1], -BIG, ALU.add, ALU.max)]
                    v[V.memset(run[:, 0:1], -BIG)]
                    v[V.memset(back[:, T - 1:T], -BIG)]
                    v[V.tensor_tensor(run[:, 1:T], tail[:, 0:T - 1], rows[0:H, 1, 1:T], ALU.add)]
                    v[V.tensor_tensor(back[:, 0:T - 1], head[:, 1:T], rows[0:H, 1, 1:T], ALU.add)]
                    dve.nop().then_inc(chained, 1)
                    dve.wait_ge(carry_out, 1)
                    v[V.tensor_copy(carry, ps[0:TP, 0:2, 0:TC * H])]
                    for n, mask in enumerate((in_first, in_last)):
                        for h in range(H):
                            for c in range(TC):
                                m = fwd[:, h, c * P:(c + 1) * P]
                                last = V.scalar_tensor_tensor(out=m, in0=mask[:, c, :],
                                                              scalar=carry[:, n, c * H + h:c * H + h + 1],
                                                              in1=m, op0=ALU.add, op1=ALU.max)
                        v[last]
                    for h in range(H):
                        last = V.tensor_tensor(scT[:, h, :], scT[:, h, :], fwd[:, h, :], ALU.subtract)
                        last.then_inc(centred, 1)
                    if leaky:
                        v[V.tensor_scalar(is_first, flag_f[:, :].rearrange("p (c e) -> p c e", c=TC), 0.0, None, ALU.is_lt)]
                        v[V.tensor_scalar(is_first[:, :, 0], carry[:, 0, :].rearrange("p (c h) -> p c h", h=H)[:, :, 0],
                                          -0.5 * BIG, None, ALU.is_lt)]
                        for h in range(H):
                            V.tensor_tensor(fwd[:, h, :], fwd[:, h, :], is_first.rearrange("p c e -> p (c e)"),
                                            ALU.mult).then_inc(max_ready, 1)
                    for h in range(H):
                        dve.wait_ge(turned_out, h + 1)
                        V.tensor_copy(sc[:, :, h], ps[:, h, 0:T]).then_inc(exp_taken, 1)
                    if leaky:
                        for h in range(H):
                            dve.wait_ge(max_out, h + 1)
                            V.tensor_copy(first_max[:, :, h], ps[:, h, 0:T])
            return sc, first_max

        def node_maximum(H, first_max, dest):
            ready, done, summed = sem_take("onehot_ready"), sem_take("step_summed"), sem_take("node_summed")
            with nc.Block() as block:
                @block.tensor
                def _(pe):
                    with pe.Fori(0, S // 4) as r:
                        tiles = pe_load(pe, steps_i[0:1, 0, bass.ds(r * 4, 4)], T - 1)
                        for j in range(4):
                            pe.wait_ge(ready, r * 4 + (j + 1))
                            nc.tensor.matmul(ps[:, j, 0:H], oh_s[:, j, :],
                                             first_max[:, bass.ds(tiles[j], 1), :].rearrange("p a h -> p (a h)"),
                                             start=True, stop=True).then_inc(done, 1)

                @block.vector
                def _(dve):
                    V.memset(dest, 0.0).then_inc(summed, 1)
                    with dve.Fori(0, S // 4) as r:
                        blocks = dve_load(dve, steps_i[0:1, 1, bass.ds(r * 4, 4)], KN - 1)
                        for j in range(4):
                            V.tensor_scalar(oh_s[:, j, :], lane[:, :], dsel[:, bass.ds(r * 4 + j, 1)], None,
                                            ALU.is_equal).then_inc(ready, 1)
                        for j in range(4):
                            dve.wait_ge(done, r * 4 + (j + 1))
                            dve.wait_ge(summed, r * 4 + (j + 1))
                            at = dest[:, bass.ds(blocks[j], 1), :].rearrange("p a h -> p (a h)")
                            V.tensor_tensor(at, at, ps[:, j, 0:H], ALU.add).then_inc(summed, 1)

        def add_self_loop(H, acc, peak, own, row, work):
            a4 = acc.rearrange("p k (h x) -> p k h x", h=H)
            none = view(work, KN * H * X1, KN, H)

            def steps(v, ask):
                v[V.scalar_tensor_tensor(out=own, in0=own, scalar=0.2, in1=own, op0=ALU.mult, op1=ALU.max)]
                v[V.tensor_scalar(none, a4[:, :, :, D], 0.0, -BIG, ALU.is_equal, ALU.mult)]
                v[V.tensor_tensor(peak, peak, none, ALU.add)]
                v[V.tensor_tensor(none, peak, own, ALU.max)]
                v[V.tensor_tensor(peak, peak, none, ALU.subtract)]
                v[V.tensor_tensor(own, own, none, ALU.subtract)]
                ask()
                ask()
                part = view(work, 0, KN * H, X1)
                for k in range(KN):
                    last = V.tensor_tensor(part[:, k * H:(k + 1) * H, :], row[:, k:k + 1, :].to_broadcast([P, H, X1]),
                                           own[:, k, :].unsqueeze(2).to_broadcast([P, H, X1]), ALU.mult)
                v[last]
                flat = acc.rearrange("p k (h x) -> p (k h) x", h=H)
                v[V.tensor_tensor(flat, flat, peak.rearrange("p k h -> p (k h)").unsqueeze(2).to_broadcast([P, KN * H, X1]), ALU.mult)]
                v[V.tensor_tensor(flat, flat, part, ALU.add)]
            on_vector(steps, [lambda: nc.scalar.activation(peak, peak, ACT.Exp), lambda: nc.scalar.activation(own, own, ACT.Exp)])

        def bwd_row(x):
            return x

        dst_i = msg[:, 0, 0:T].bitcast(I32)
        load([(xs[:, :, 0:D], a["x"].rearrange("(k p) d -> p k d", p=P)),
              (src_i[:, :], a["src"]), (dst_i, a["dst"])])

        s_idx = view(arena, 0, S)
        t_idx = view(arena, 448, TC)
        k_edge = view(arena, 460, KN)
        with nc.Block() as block:
            @block.gpsimd
            def _(pool):
                pool.memset(ident[:, :], 0.0).then_inc(pool_done.sem, 1)
                pool.wait_ge(pool_done.sem, pool_done.base + 1)
                pool.affine_select(out=ident[:, :], in_=ident[:, :], compare_op=ALU.not_equal, fill=1.0, base=0,
                                   pattern=[[-1, P]], channel_multiplier=1)
                pool.iota(lane[:, :], [[1, P]], base=0, channel_multiplier=0, allow_small_or_imprecise_dtypes=True)
                pool.iota(s_idx, [[1, S]], base=0, channel_multiplier=0, allow_small_or_imprecise_dtypes=True)
                pool.iota(t_idx, [[TP, TC]], base=0, channel_multiplier=1, allow_small_or_imprecise_dtypes=True)
                pool.iota(k_edge, [[P, KN]], base=0, channel_multiplier=0, allow_small_or_imprecise_dtypes=True)

            @block.vector
            def _(dve):
                V.memset(xs[:, :, D:X1], 1.0)
        pool_done.base += 1

        dst_f = view(arena, 512, T)
        dstT = view(arena, 1024, TC, P)[0:TP]
        wide = view(arena, 1536, TC, S)[0:TP]
        ones = view(arena, 3400, P)
        tile_of = view(arena, 3600, S)
        block_of = view(arena, 4100, S)
        ge = view(arena, 4600, TC, KN)[0:TP]
        end = view(arena, 4720, TC)[0:TP]
        first_row, last_row = view(arena, 4800, T)[0:HEADS], view(arena, 5300, T)[0:HEADS]
        cont = view(arena, 5800, T + 1)[0:HEADS]
        ends = view(arena, 6300, 2, HEADS)
        with nc.Block() as block:
            @block.vector
            def _(dve):
                v = Vector(dve)
                v[V.tensor_copy(dst_f, dst_i)]
                v[V.memset(ones, 1.0)]
                v[V.tensor_copy(ends[:, 0, :], ident[:, 0:1].to_broadcast([P, HEADS]))]
                v[V.tensor_copy(ends[:, 1, :], ident[:, P - 1:P].to_broadcast([P, HEADS]))]
                dve.nop().then_inc(to_pe.sem, 1)
                dve.wait_ge(from_pe.sem, from_pe.base + 1)
                v[V.tensor_copy(dstT.rearrange("p c e -> p (c e)"), ps[0:TP, 0, :])]
                v[V.tensor_tensor(ge, dstT[:, :, P - 1:P].to_broadcast([TP, TC, KN]),
                                  k_edge[0:TP].unsqueeze(1).to_broadcast([TP, TC, KN]), ALU.is_ge)]
                v[V.tensor_reduce(end, ge, AX, ALU.add)]
                v[V.scalar_tensor_tensor(out=end, in0=end, scalar=-1.0, in1=t_idx[0:TP], op0=ALU.add, op1=ALU.add)]
                for c in range(TC):
                    v[V.tensor_scalar(wide[:, c, :], s_idx[0:TP], end[:, c:c + 1], None, ALU.is_gt)]
                dve.nop().then_inc(to_pe.sem, 1)
                dve.wait_ge(from_pe.sem, from_pe.base + 2)
                v[V.tensor_copy(tile_of, ps[:, 1, 0:S])]
                v[V.tensor_tensor(block_of, s_idx, tile_of, ALU.subtract)]
                v[V.tensor_copy(steps_i[0:1, 0, :], tile_of[32:33, :])]
                v[V.tensor_copy(steps_i[0:1, 1, :], block_of[32:33, :])]
                for c in range(TC):
                    v[V.tensor_scalar(wide[:, c, :], tile_of[0:TP], t_idx[0:TP, c:c + 1], None, ALU.is_equal)]
                dve.nop().then_inc(to_pe.sem, 1)
                dve.wait_ge(from_pe.sem, from_pe.base + 3)
                v[V.scalar_tensor_tensor(out=dsel[:, :], in0=block_of, scalar=-float(P), in1=ps[:, 2, 0:S],
                                         op0=ALU.mult, op1=ALU.add)]
                ff = flag_f[:, :].rearrange("p (c e) -> p c e", c=TC)
                fb = flag_b[:, :].rearrange("p (c e) -> p c e", c=TC)
                v[V.memset(ff, 0.0)]
                v[V.memset(fb, 0.0)]
                v[V.tensor_tensor(ff[:, :, 1:P], dstT[:, :, 1:P], dstT[:, :, 0:P - 1], ALU.is_equal)]
                v[V.tensor_copy(fb[:, :, 0:P - 1], ff[:, :, 1:P])]
                v[V.tensor_tensor(in_first[:, :, :], dstT, dstT[:, :, 0:1].to_broadcast([TP, TC, P]), ALU.is_equal)]
                v[V.tensor_tensor(in_last[:, :, :], dstT, dstT[:, :, P - 1:P].to_broadcast([TP, TC, P]), ALU.is_equal)]
                for m in (ff, fb, in_first[:, :, :], in_last[:, :, :]):
                    v[V.tensor_scalar(m, m, -1.0, BIG, ALU.add, ALU.mult)]
                v[V.tensor_copy(first_row, ps[0:HEADS, 3, 0:T])]
                v[V.tensor_copy(last_row, ps[0:HEADS, 4, 0:T])]
                v[V.memset(cont, 0.0)]
                v[V.tensor_tensor(cont[:, 1:T], first_row[:, 1:T], last_row[:, 0:T - 1], ALU.is_equal)]
                v[V.tensor_tensor(first_row, first_row, last_row, ALU.is_equal)]
                v[V.tensor_tensor(rows[:, 0, :], first_row, cont[:, 0:T], ALU.mult)]
                v[V.tensor_copy(rows[:, 1, :], cont[:, 0:T])]
                v[V.tensor_tensor(rows[:, 2, :], first_row, cont[:, 1:T + 1], ALU.mult)]
                v[V.tensor_scalar(rows[:, :, :], rows[:, :, :], -1.0, BIG, ALU.add, ALU.mult)]

            @block.tensor
            def _(pe):
                pe.wait_ge(to_pe.sem, to_pe.base + 1)
                for c in range(TC):
                    nc.tensor.transpose(ps[0:TP, 0, c * P:(c + 1) * P], dst_f[:, c * TP:(c + 1) * TP], ident[:, :])
                for n in range(2):
                    last = nc.tensor.matmul(ps[0:HEADS, 3 + n, 0:T], ends[:, n, :], dst_f, start=True, stop=True)
                last.then_inc(from_pe.sem, 1)
                pe.wait_ge(to_pe.sem, to_pe.base + 2)
                for c in range(TC):
                    last = nc.tensor.matmul(ps[:, 1, 0:S], ones[0:TP, :], wide[:, c, :], start=(c == 0), stop=(c == TC - 1))
                last.then_inc(from_pe.sem, 1)
                pe.wait_ge(to_pe.sem, to_pe.base + 3)
                for c in range(TC):
                    last = nc.tensor.matmul(ps[:, 2, 0:S], dstT[:, c, :], wide[:, c, :], start=(c == 0), stop=(c == TC - 1))
                last.then_inc(from_pe.sem, 1)
        to_pe.base += 3
        from_pe.base += 3

        def table(name, width):
            return nc.dram_tensor(name, (NPAD, width), F32).ap()

        def rows_of(t):
            return t.rearrange("(k p) d -> p k d", p=P)

        xw = xs[:, :, 0:D]
        tab_H = view(arena, tab_at, KN, 2 * X1)
        node = [view(x_all, n * KN * D, KN, D) for n in range(8)]
        wide_x = view(x_all, 8 * KN * D, KN, 4 * D)

        def normalise(H, acc, dest, add_small):
            den = view(small, 0, KN, 1) if H == 1 else None
            v4 = acc.rearrange("p k (h x) -> p (k h) x", h=H)
            den = view(msg.rearrange("p a b -> p (a b)"), 0, KN * H)

            def steps(v, ask):
                v[V.tensor_scalar(den, v4[:, :, D], 1e-16, None, ALU.add)]
                v[V.reciprocal(den, den)]
                w = dest.shape[2] // H
                v[V.tensor_tensor(dest.rearrange("p k (h x) -> p (k h) x", h=H), v4[:, :, 0:w],
                                  den.unsqueeze(2).to_broadcast([P, KN * H, w]), ALU.mult)]
            on_vector(steps)

        W1 = view(x_all, 1024, 256)[0:D]
        V1 = view(x_all, 1280, 16)[0:D]
        peak, own = view(wbuf, 0, KN, HEADS), view(wbuf, KN * HEADS, KN, HEADS)
        att1 = view(x_all, 0, 2, 256)[0:D]
        t1 = view(x_all, 512, 2, 256)[0:D]
        load([(W1, a["L0_gnn_W1"]),
              (att1[:, 0, :], a["L0_gnn_a1_src"].partition_broadcast(D)),
              (att1[:, 1, :], a["L0_gnn_a1_dst"].partition_broadcast(D))])

        def steps(v, ask):
            v[V.tensor_tensor(t1, att1, W1.unsqueeze(1).to_broadcast([D, 2, 256]), ALU.mult)]
            v[V.tensor_reduce(V1, t1.rearrange("p a (h c) -> p (a h) c", c=HID), AX, ALU.add)]
        on_vector(steps)
        al = view(x_all, 8000, KN, 16)
        dense([xw], [V1], al)
        row0 = view(x_all, 2000, KN, RW)
        tab_al = view(arena, tab_at, KN, HEADS)

        def steps(v, ask):
            v[V.tensor_copy(row0[:, :, 0:D], xw)]
            v[V.tensor_copy(row0[:, :, D:RW], al[:, :, 0:HEADS])]
            v[V.tensor_copy(tab_al, al[:, :, HEADS:16])]
            v[V.tensor_tensor(own, al[:, :, 0:HEADS], al[:, :, HEADS:16], ALU.add)]
        on_vector(steps)
        table0 = table("table0", RW)
        store([(rows_of(table0), row0)])
        gather_scores(table0, RW, HEADS, tab_al, False)
        weight, first_max = softmax_numerators(HEADS, True)
        node_maximum(HEADS, first_max, peak)
        acc = aggregate(HEADS, weight)
        add_self_loop(HEADS, acc, peak, own, xs, x_all)
        agg = view(x_all, 0, KN, HEADS * D)
        normalise(HEADS, acc, agg, True)
        h1 = view(arena, 0, KN, 256)
        W1p = view(arena, 6400, 4, 2 * HID)
        W2a = view(arena, 6700, 2, D + 2)
        b1 = view(arena, 7000, 256)
        att2 = view(arena, 7300, 2, D)
        t2 = view(arena, 7500, 2, 2 * D)
        b2 = view(arena, 7800, D)

        def steps(v, ask):
            v[V.memset(W1p, 0.0)]
        on_vector(steps)
        W1v = a["L0_gnn_W1"].rearrange("f (q j c) -> f q j c", j=2, c=HID)
        load([(W1p[0:D, :, 0:HID], W1v[:, :, 0, :]), (W1p[D:P, :, HID:2 * HID], W1v[:, :, 1, :]),
              (W2a[:, :, 0:D], a["L0_gnn_W2"].rearrange("(m p) c -> p m c", p=P)),
              (b1, a["L0_gnn_b1"].partition_broadcast(P)), (b2, a["L0_gnn_b2"].partition_broadcast(P)),
              (att2[:, 0, :], a["L0_gnn_a2_src"].partition_broadcast(P)),
              (att2[:, 1, :], a["L0_gnn_a2_dst"].partition_broadcast(P))])

        def steps(v, ask):
            for n in range(2):
                v[V.tensor_tensor(t2[:, n, :].rearrange("p (m c) -> p m c", m=2), W2a[:, :, 0:D],
                                  att2[:, n:n + 1, :].to_broadcast([P, 2, D]), ALU.mult)]
                v[V.tensor_reduce(W2a[:, :, D + n], t2[:, n, :].rearrange("p (m c) -> p m c", m=2), AX, ALU.add)]
        on_vector(steps)
        for q in range(4):
            dense([agg[:, :, q * P:(q + 1) * P]], [W1p[:, q, :]], h1[:, :, q * D:(q + 1) * D])
        neg = view(x_all, 0, KN, 256)

        def steps(v, ask):
            v[V.tensor_tensor(h1, h1, b1.unsqueeze(1).to_broadcast([P, KN, 256]), ALU.add)]
            v[V.tensor_scalar(neg, h1, 0.0, None, ALU.min)]
            ask()
            v[V.tensor_scalar(h1, h1, 0.0, -1.0, ALU.max, ALU.add)]
            v[V.tensor_tensor(h1, h1, neg, ALU.add)]
        on_vector(steps, [lambda: nc.scalar.activation(neg, neg, ACT.Exp)])
        h2 = view(x_all, 0, KN, D + 2)
        dense([h1[:, :, 0:P], h1[:, :, P:256]], [W2a[:, 0, :], W2a[:, 1, :]], h2)
        row1 = view(x_all, 2000, KN, X1)
        b2_keep = wbuf[:, 0:D]
        peak, own = view(wbuf, D, KN, 1), view(wbuf, D + KN, KN, 1)
        tab1 = view(arena, tab_at, KN, 1)

        def steps(v, ask):
            v[V.tensor_copy(row1, h2[:, :, 0:X1])]
            v[V.tensor_copy(b2_keep, b2)]
            v[V.tensor_copy(tab1, h2[:, :, X1:X1 + 1])]
            v[V.tensor_tensor(own, h2[:, :, D:X1], h2[:, :, X1:X1 + 1], ALU.add)]
        on_vector(steps)
        table1 = table("table1", X1)
        store([(rows_of(table1), row1)])
        recycle()
        gather_scores(table1, X1, 1, tab1, False)
        weight, first_max = softmax_numerators(1, True)
        node_maximum(1, first_max, peak)
        acc = aggregate(1, weight)
        row1 = view(x_all, 4000, KN, X1)
        load([(row1, rows_of(table1))])

        def steps(v, ask):
            v[V.memset(row1[:, :, D:X1], 1.0)]
        on_vector(steps)
        add_self_loop(1, acc, peak, own, row1, x_all)
        y = node[0]
        normalise(1, acc, y, True)

        def steps(v, ask):
            v[V.tensor_tensor(y, y, b2_keep.unsqueeze(1).to_broadcast([P, KN, D]), ALU.add)]
            v[V.tensor_tensor(y, y, xw, ALU.add)]
        on_vector(steps)
        layernorm(y, node[1], xw)

        Wn, Wc, Wp = (wbuf[0:X1, n * D:(n + 1) * D] for n in range(3))
        be2 = wbuf[:, 3 * D:4 * D]
        We2 = wbuf[:, 4 * D:5 * D]
        We1 = wbuf[:, 5 * D:7 * D]
        be1 = wbuf[:, 7 * D:7 * D + 1]

        def steps(v, ask):
            v[V.memset(We1, 0.0)]
        on_vector(steps)
        load([(Wn, a["L1_Wn"]), (Wc, a["L1_Wc"]), (Wp, a["L1_Wp"]), (be2, a["L1_gnn_be2"].partition_broadcast(P))]
             + [pair for h in range(2) for pair in (
                 (We2[h * D:(h + 1) * D, :], a["L1_We2"]), (We1[h * D:(h + 1) * D, h * D:(h + 1) * D], a["L1_We1"]),
                 (be1[h * D:(h + 1) * D, :], a["L1_gnn_be1"].rearrange("(d o) -> d o", o=1)))])
        hn = node[0]
        dense([xs[:, :, :]], [Wn], hn)
        table2 = table("table2", D)
        store([(rows_of(table2), hn)])

        recycle()
        acc = view(arena, 0, KN, X1)
        ring = view(arena, 2048, RING * G * D).rearrange("p (r g w) -> p r g w", r=RING, g=G)
        ea = view(arena, 4096, 2, 512)
        u1 = view(arena, 5120, 512)
        z2, m2, e2, m1, e1 = (view(arena, 5632 + 512 * n, 512) for n in range(5))
        be1m = small[:, 0:2]
        gathered = [sem_take("gathered") for _ in range(RING)]
        free, ea_in, hid = sem_take("ring_taken"), [sem_take("edge_features") for _ in range(2)], sem_take("hidden_product")
        act1, u_ready, filt = sem_take("hidden_parts"), sem_take("hidden_ready"), sem_take("filter_product")
        z_ready, act2, f_sum = sem_take("filter_biased"), sem_take("filter_parts"), sem_take("filter_ready")
        ready, done, summed = sem_take("messages_ready"), sem_take("step_summed"), sem_take("node_summed")
        exp1, exp2 = sem_take("hidden_exp"), sem_take("filter_exp")
        ea_dram = a["ea"]
        with nc.Block() as block:
            pool_gathers(block, table2, D, ring, gathered, free)

            @block.sync
            def _(sp):
                sp.dma_start(ea[:, 0, :], ea_dram[:, 0, :]).then_inc(ea_in[0], 16)
                sp.dma_start(ea[:, 1, :], ea_dram[:, 1, :]).then_inc(ea_in[1], 16)
                with sp.Fori(1, NG // 2) as r:
                    for par in range(2):
                        sp.wait_ge(hid, (r - 1) * 2 + (par + 1))
                        sp.dma_start(ea[:, par, :], ea_dram[:, bass.ds(r * 2 + par, 1), :].rearrange("p a e -> p (a e)")).then_inc(ea_in[par], 16)

            @block.tensor
            def _(pe):
                with pe.Fori(0, NG // 2) as r:
                    for par in range(2):
                        g = r * 2 + par
                        pe.wait_ge(ea_in[par], (r + 1) * 16)
                        nc.tensor.matmul(ps[:, 4, :], We1, ea[:, par, :], start=True, stop=True).then_inc(hid, 1)
                        pe.wait_ge(u_ready, g + 1)
                        for j in range(G):
                            h = j // 4
                            last = nc.tensor.matmul(ps[:, 5 + h, (j % 4) * D:(j % 4 + 1) * D], u1[h * D:(h + 1) * D, (j % 4) * P:(j % 4 + 1) * P],
                                                    We2[h * D:(h + 1) * D, :], start=True, stop=True)
                        last.then_inc(filt, 1)
                        for b in range(2):
                            aggregate_tensor(pe, 4, 1, lambda j, b=b: g * G + (4 * b + j), ready, done)
                with pe.Fori(NG, NB) as g:
                    for b in range(2):
                        aggregate_tensor(pe, 4, 1, lambda j, b=b: g * G + (4 * b + j), ready, done)

            @block.scalar
            def _(act):
                with act.Fori(0, NG) as g:
                    act.wait_ge(hid, g + 1)
                    nc.scalar.activation(m1, ps[:, 4, :], ACT.Relu, bias=be1)
                    nc.scalar.activation(e1, ps[:, 4, :], ACT.Abs, bias=be1).then_inc(exp1, 1)
                    act.wait_ge(exp1, g * 3 + 1)
                    nc.scalar.activation(e1, e1, ACT.Exp, scale=-1.0).then_inc(exp1, 1)
                    act.wait_ge(exp1, g * 3 + 2)
                    nc.scalar.activation(e1, e1, ACT.Ln, bias=1.0).then_inc(exp1, 1)
                    act.wait_ge(z_ready, g + 1)
                    nc.scalar.activation(m2, z2, ACT.Relu)
                    nc.scalar.activation(e2, z2, ACT.Abs).then_inc(exp2, 1)
                    act.wait_ge(exp2, g * 3 + 1)
                    nc.scalar.activation(e2, e2, ACT.Exp, scale=-1.0).then_inc(exp2, 1)
                    act.wait_ge(exp2, g * 3 + 2)
                    nc.scalar.activation(e2, e2, ACT.Ln, bias=1.0).then_inc(exp2, 1)

            @block.vector
            def _(dve):
                Vector(dve)[V.memset(xa[:, :, D:X1], 1.0)]
                V.memset(acc, 0.0).then_inc(summed, 1)
                with dve.Fori(0, NG // RING) as r:
                    for slot in range(RING):
                        g = r * RING + slot
                        dve.wait_ge(exp1, g * 3 + 3)
                        V.scalar_tensor_tensor(out=u1, in0=m1, scalar=-LOG2, in1=e1, op0=ALU.add, op1=ALU.add).then_inc(u_ready, 1)
                        dve.wait_ge(filt, g + 1)
                        V.tensor_tensor(z2.rearrange("p (b g d) -> p b g d", b=2, d=D),
                                        ps[:, 5:7, 0:4 * D].rearrange("p b (g d) -> p b g d", d=D),
                                        be2.unsqueeze(1).unsqueeze(1).to_broadcast([P, 2, G // 2, D]), ALU.add).then_inc(z_ready, 1)
                        dve.wait_ge(exp2, g * 3 + 3)
                        V.scalar_tensor_tensor(out=m2, in0=m2, scalar=-LOG2, in1=e2, op0=ALU.add, op1=ALU.add).then_inc(f_sum, 1)
                        dve.wait_ge(f_sum, g * 2 + 1)
                        dve.wait_ge(gathered[slot], (r + 1) * (16 * G))
                        V.tensor_tensor(xa[:, bass.ds(g * G, G), 0:D], ring[:, slot, :, :],
                                        m2.rearrange("p (g d) -> p g d", g=G), ALU.mult).then_inc(f_sum, 1)
                        dve.wait_ge(f_sum, g * 2 + 2)
                        dve.nop().then_inc(free, 1)
                        for b in range(2):
                            aggregate_vector(dve, 1, acc, None, g * G + 4 * b, lambda j, b=b: g * G + (4 * b + j), ready, done, summed)
                with dve.Fori(NG, NB) as g:
                    for b in range(2):
                        aggregate_vector(dve, 1, acc, None, g * G + 4 * b, lambda j, b=b: g * G + (4 * b + j), ready, done, summed)

        def steps(v, ask):
            v[V.memset(acc[:, :, D:X1], 1.0)]
        on_vector(steps)
        z = view(x_all, 0, KN, X1)
        u = view(x_all, KN * X1, KN, X1)
        w = view(x_all, 2 * KN * X1, KN, D)
        dense([acc], [Wc], z[:, :, 0:D])
        zz, uu = z[:, :, 0:D], u[:, :, 0:D]

        def steps(v, ask):
            ask()
            ask()
            ask()
            ask()
            v[V.memset(u[:, :, D:X1], 1.0)]
            v[V.scalar_tensor_tensor(out=uu, in0=w, scalar=-LOG2, in1=zz, op0=ALU.add, op1=ALU.add)]
        on_vector(steps, [lambda: nc.scalar.activation(w, zz, ACT.Relu), lambda: nc.scalar.activation(zz, zz, ACT.Abs),
                          lambda: nc.scalar.activation(zz, zz, ACT.Exp, scale=-1.0),
                          lambda: nc.scalar.activation(zz, zz, ACT.Ln, bias=1.0)])
        y = node[3]
        dense([u], [Wp], y)

        def steps(v, ask):
            v[V.tensor_tensor(y, y, xw, ALU.add)]
        on_vector(steps)
        layernorm(y, node[4], xw)

        table3, table4 = table("table3", D), table("table4", D)
        state = view(arena, 11375, KN, X1)
        recycle()
        for n, (tab_dram, cur) in enumerate(((table3, xs[:, :, :]), (table4, state))):
            l = f"L2_l{n + 1}_"
            qT, kT = (view(x_all, m * 2 * X1, 2, X1)[0:D] for m in range(2))
            kq = wbuf[0:X1, 0:2 * X1]
            wv = wbuf[0:X1, 2 * X1:2 * X1 + 2 * D]
            ws = wbuf[0:X1, 2 * X1 + 2 * D:2 * X1 + 3 * D]
            load([(qT, a[l + "q"]), (kT, a[l + "k"]), (wv, a[l + "v"]), (ws, a[l + "s"])])
            with nc.Block() as block:
                @block.tensor
                def _(pe):
                    for h in range(2):
                        last = nc.tensor.matmul(ps[0:X1, 0, h * X1:(h + 1) * X1], qT[:, h, :], kT[:, h, :], start=True, stop=True)
                    last.then_inc(from_pe.sem, 1)

                @block.vector
                def _(dve):
                    dve.wait_ge(from_pe.sem, from_pe.base + 1)
                    V.tensor_scalar(kq, ps[0:X1, 0, 0:2 * X1], 0.125, None, ALU.mult)
                    V.tensor_scalar(wv, wv, 0.5, None, ALU.mult)
            from_pe.base += 1
            tab = view(arena, tab_at, KN, 2 * X1)
            dense([cur], [kq], tab)
            if n == 1:
                pass
            store([(rows_of(tab_dram), cur[:, :, 0:D])])
            gather_scores(tab_dram, D, 2, tab, True)
            weight, _ = softmax_numerators(2, False)
            acc = aggregate(2, weight)
            recycle()
            agg = view(x_all, 0, KN, 2 * X1)
            normalise(2, acc, agg, True)
            y = node[4]
            dense([agg[:, :, 0:X1], agg[:, :, X1:2 * X1], cur], [wv[:, 0:D], wv[:, D:2 * D], ws], y)
            if n == 0:
                def steps(v, ask):
                    v[V.memset(state, 1.0)]
                    v[V.tensor_copy(state[:, :, 0:D], y)]
                on_vector(steps)

        def steps(v, ask):
            v[V.tensor_tensor(y, y, xw, ALU.add)]
        on_vector(steps)
        layernorm(y, node[5], xw)

        Wl, Wh, Wm = (wbuf[0:D, n * D:(n + 1) * D] for n in range(3))
        av = wbuf[:, 3 * D:6 * D].rearrange("p (n d) -> p n d", n=3)
        att = wbuf[:, 6 * D:6 * D + 9]
        ew = view(score, 0, T, 2)
        load([(Wl, a["L3_gnn_W_low"]), (Wh, a["L3_gnn_W_high"]), (Wm, a["L3_gnn_W_mlp"]), (ew, a["ew"]),
              (att, a["L3_gnn_att_vec"].partition_broadcast(P))]
             + [(av[:, n, :], a[f"L3_gnn_av_{m}"].partition_broadcast(P)) for n, m in enumerate(("low", "high", "mlp"))])
        table5 = table("table5", D)
        store([(rows_of(table5), xw)])
        acc = view(arena, 0, KN, 2 * X1)
        ring = view(arena, 3328, RING * G * D).rearrange("p (r g w) -> p r g w", r=RING, g=G)
        gathered = [sem_take("gathered") for _ in range(RING)]
        free = sem_take("ring_taken")
        ready, done, summed = sem_take("messages_ready"), sem_take("step_summed"), sem_take("node_summed")
        with nc.Block() as block:
            pool_gathers(block, table5, D, ring, gathered, free)

            @block.scalar
            def _(act):
                with act.Fori(0, NG // RING) as r:
                    for slot in range(RING):
                        act.wait_ge(gathered[slot], (r + 1) * (16 * G))
                        nc.scalar.copy(xa[:, bass.ds((r * RING + slot) * G, G), 0:D], ring[:, slot, :, :]).then_inc(free, 1)

            @block.tensor
            def _(pe):
                with pe.Fori(0, S // 4) as r:
                    aggregate_tensor(pe, 4, 2, lambda j: r * 4 + j, ready, done)

            @block.vector
            def _(dve):
                Vector(dve)[V.memset(xa[:, :, D:X1], 1.0)]
                V.memset(acc, 0.0).then_inc(summed, 1)
                with dve.Fori(0, NG) as g:
                    dve.wait_ge(free, g + 1)
                    for b in range(2):
                        aggregate_vector(dve, 2, acc, ew, g * G + 4 * b, lambda j, b=b: g * G + (4 * b + j), ready, done, summed)
                with dve.Fori(NG, NB) as g:
                    for b in range(2):
                        aggregate_vector(dve, 2, acc, ew, g * G + 4 * b, lambda j, b=b: g * G + (4 * b + j), ready, done, summed)

        hs = [node[n] for n in range(3)]
        for m, (of, wm) in enumerate(((acc[:, :, 0:D], Wl), (acc[:, :, X1:X1 + D], Wh), (xw, Wm))):
            dense([of], [wm], hs[m])
        feats = small[:, 0:3 * KN].rearrange("p (n k) -> p n k", n=3)
        logits = small[:, 3 * KN:6 * KN].rearrange("p (n k) -> p n k", n=3)
        extra = view(msg.rearrange("p a b -> p (a b)"), 0, 2, KN)
        y = node[3]

        def steps(v, ask):
            for m in range(3):
                v[V.tensor_scalar(hs[m], hs[m], 0.0, None, ALU.max)]
                v[V.tensor_tensor(node[4], hs[m], av[:, m:m + 1, :].to_broadcast([P, KN, D]), ALU.mult)]
                v[V.tensor_reduce(feats[:, m, :], node[4], AX, ALU.add)]
            ask()
            for j in range(3):
                v[V.tensor_scalar(logits[:, j, :], feats[:, 0, :], att[:, j:j + 1], None, ALU.mult)]
                for i in range(1, 3):
                    v[V.scalar_tensor_tensor(out=logits[:, j, :], in0=feats[:, i, :], scalar=att[:, 3 * i + j:3 * i + j + 1],
                                             in1=logits[:, j, :], op0=ALU.mult, op1=ALU.add)]
            v[V.tensor_scalar(logits, logits, 1.0 / 3.0, None, ALU.mult)]
            top, tot = extra[:, 0, :], extra[:, 1, :]
            v[V.tensor_tensor(top, logits[:, 0, :], logits[:, 1, :], ALU.max)]
            v[V.tensor_tensor(top, top, logits[:, 2, :], ALU.max)]
            v[V.tensor_tensor(logits, logits, top.unsqueeze(1).to_broadcast([P, 3, KN]), ALU.subtract)]
            ask()
            v[V.tensor_tensor(tot, logits[:, 0, :], logits[:, 1, :], ALU.add)]
            v[V.tensor_tensor(tot, tot, logits[:, 2, :], ALU.add)]
            v[V.reciprocal(tot, tot)]
            v[V.tensor_scalar(tot, tot, 3.0, None, ALU.mult)]
            v[V.tensor_tensor(logits, logits, tot.unsqueeze(1).to_broadcast([P, 3, KN]), ALU.mult)]
            v[V.tensor_copy(y, xw)]
            for m in range(3):
                v[V.tensor_tensor(hs[m], hs[m], logits[:, m, :].unsqueeze(2).to_broadcast([P, KN, D]), ALU.mult)]
                v[V.tensor_tensor(y, y, hs[m], ALU.add)]
        on_vector(steps, [lambda: nc.scalar.activation(feats, feats, ACT.Sigmoid),
                          lambda: nc.scalar.activation(logits, logits, ACT.Exp)])
        layernorm(y, node[4], xw)
        full = N // P
        store([(out[0:full * P, :].rearrange("(k p) d -> p k d", p=P), xs[:, 0:full, 0:D]),
               (out[full * P:N, :], xs[0:N - full * P, full, 0:D])])


def kernel(**inputs):
    import numpy as np
    import concourse.bacc as bacc
    from concourse.bass_utils import run_bass_kernel_spmd

    def padded(x, n, fill=0):
        return np.concatenate([x, np.full((n - len(x),) + x.shape[1:], fill, x.dtype)])

    def tiles(x, fill=0):
        return np.ascontiguousarray(padded(x, EPAD, fill).reshape(T, P).T)

    def biased(w, b):
        return np.ascontiguousarray(np.concatenate([w, b[None]]))

    i = {k: np.asarray(v) for k, v in inputs.items()}
    arrays = {"x": padded(i["x"], NPAD), "src": tiles(i["src"]), "dst": tiles(i["dst"], NPAD - 1)}
    arrays["ea"] = np.ascontiguousarray(
        padded(i["edge_attr_64"], EPAD).reshape(NG, 2, EPAD // NG // 2, D).transpose(1, 3, 0, 2).reshape(P, NG, EPAD // NG // 2))
    arrays["ew"] = np.ascontiguousarray(np.stack([tiles(i["edge_weight"]), tiles(i["edge_weight_n2"])], -1))
    for k in ("W1", "W2"):
        arrays[f"L0_gnn_{k}"] = i[f"L0_gnn_{k}"]
    for k in ("a1_src", "a1_dst", "a2_src", "a2_dst", "b1", "b2"):
        arrays[f"L0_gnn_{k}"] = i[f"L0_gnn_{k}"].reshape(-1)
    for k, b in (("Wn", "bn"), ("Wc", "bc"), ("Wp", "bp")):
        arrays[f"L1_{k}"] = biased(i[f"L1_gnn_{k}"].T, i[f"L1_gnn_{b}"])
    for k in ("We1", "We2"):
        arrays[f"L1_{k}"] = np.ascontiguousarray(i[f"L1_gnn_{k}"].T)
    for k in ("be1", "be2"):
        arrays[f"L1_gnn_{k}"] = i[f"L1_gnn_{k}"]
    for l in ("l1", "l2"):
        w = {k: biased(i[f"L2_gnn_{l}_w{k}"], i[f"L2_gnn_{l}_b{k}"]) for k in "qkvs"}
        for k in "qk":
            arrays[f"L2_{l}_{k}"] = np.ascontiguousarray(w[k].reshape(X1, 2, D).transpose(2, 1, 0))
        for k in "vs":
            arrays[f"L2_{l}_{k}"] = w[k]
    for k in ("W_low", "W_high", "W_mlp"):
        arrays[f"L3_gnn_{k}"] = i[f"L3_gnn_{k}"]
    for k in ("av_low", "av_high", "av_mlp", "att_vec"):
        arrays[f"L3_gnn_{k}"] = i[f"L3_gnn_{k}"].reshape(-1)

    nc = bacc.Bacc("TRN2", target_bir_lowering=False, num_devices=1)
    arrays = {f"{k}_in": v for k, v in arrays.items()}
    a = {k[:-3]: nc.dram_tensor(k, v.shape, mybir.dt.from_np(v.dtype), kind="ExternalInput").ap()
         for k, v in arrays.items()}
    out = nc.dram_tensor("out", (N, D), F32, kind="ExternalOutput").ap()
    build(nc, a, out)
    r = run_bass_kernel_spmd(nc, [arrays], core_ids=[0])
    return r.results[0]["out"]
```

```python
from contextlib import ExitStack

import concourse.bass as bass
from concourse import mybir

P = 128
N, D, E = 3125, 64, 53125
KN = -(-N // P)
NPAD = KN * P
T = -(-E // P)
T += -T % 8
EPAD = T * P
G = 8
RING = 4
STEPS = T + KN - 1
S = STEPS + -STEPS % (G * RING)
NG = S // G
C = 4
TP, SP = T // C, S // C
X1 = D + 1
HEADS, HID = 8, 32
BIG = 1e30
LOG2 = 0.6931471805599453
EPS = 1e-5
assert T % C == 0 and S % C == 0 and SP <= P and S <= 512

F32 = mybir.dt.float32
I32 = mybir.dt.int32
ALU = mybir.AluOpType
ACT = mybir.ActivationFunctionType
AX = mybir.AxisListType.X


class Signal:

    def __init__(self, handle):
        self.sem, self.base = handle, 0


def build(nc, a, out):
    with ExitStack() as ctx:
        def sb(name, shape, dt=F32):
            return ctx.enter_context(nc.sbuf_tensor(name, shape, dt))

        def sem(name):
            return ctx.enter_context(nc.semaphore(name))

        ps = ctx.enter_context(nc.psum_tensor("ps", [P, 8, 512], F32))

        xs = sb("xs", [P, KN, X1])
        x_all = sb("x_all", [P, S * X1])
        arena = sb("arena", [P, KN * HEADS * X1])
        score = sb("score", [P, S * HEADS])
        dsel = sb("dsel", [P, S])
        src_i = sb("src_i", [P, S], I32)
        step_i = sb("step_i", [2, S], I32)[0:1, :]
        ident = sb("ident", [P, P])
        lane = sb("lane", [P, P])
        oh_s = sb("oh_s", [P, G * P])
        msg = sb("msg", [P, 4 * HEADS * X1])
        idx = sb("idx", [P, RING, G], I32)
        wbuf = sb("wbuf", [P, 456])
        small = sb("small", [P, 6 * KN])

        def view(t, at, *shape):
            n = 1
            for k in shape:
                n *= k
            v = t[:, at:at + n]
            if len(shape) == 2:
                v = v.rearrange("p (a b) -> p a b", b=shape[1])
            if len(shape) == 3:
                v = v.rearrange("p (a b c) -> p a b c", b=shape[1], c=shape[2])
            return v

        xa = view(x_all, 0, S, X1)

        loaded = Signal(sem("loaded"))
        stored = Signal(sem("stored"))
        chain = Signal(sem("vector_chain"))
        to_act = Signal(sem("vector_for_scalar"))
        from_act = Signal(sem("scalar_for_vector"))
        to_pe = Signal(sem("vector_for_tensor"))
        from_pe = Signal(sem("tensor_for_vector"))
        pool_done = Signal(sem("pool_done"))
        turned = Signal(sem("turned"))
        turned_sb = Signal(sem("turned_sb"))
        product = Signal(sem("product"))
        taken = Signal(sem("taken"))

        class Vector:

            def __init__(self, eng):
                self.eng = eng

            def __getitem__(self, ins):
                chain.base += 1
                ins.then_inc(chain.sem, 1)
                self.eng.wait_ge(chain.sem, chain.base)

        def hand(eng, signal):
            signal.base += 1
            eng.nop().then_inc(signal.sem, 1)

        def load(pairs):
            with nc.Block() as block:
                @block.sync
                def _(sp):
                    for dst, src in pairs:
                        sp.dma_start(dst, src).then_inc(loaded.sem, 16)
                        loaded.base += 16
                    sp.wait_ge(loaded.sem, loaded.base)

        def store(pairs):
            with nc.Block() as block:
                @block.sync
                def _(sp):
                    for dst, src in pairs:
                        sp.dma_start(dst, src).then_inc(stored.sem, 16)
                        stored.base += 16
                    sp.wait_ge(stored.sem, stored.base)

        def dense(sources, weights, dest):
            K = [s.shape[2] for s in sources]
            M = len(sources)
            width = dest.shape[2]
            blocks = [(i, min(4, KN - i)) for i in range(0, KN, 4)]
            xT = view(x_all, S * X1 - 2 * 3 * 512, 2, 3, 512)
            t0, s0, p0, k0 = turned.base, turned_sb.base, product.base, taken.base

            with nc.Block() as block:
                @block.tensor
                def _(pe):
                    def turn(n):
                        i, nj = blocks[n]
                        if n >= 2:
                            pe.wait_ge(turned_sb.sem, s0 + n - 1)
                        for m in range(M):
                            for j in range(nj):
                                last = nc.tensor.transpose(ps[0:K[m], 3 * (n % 2) + m, j * P:(j + 1) * P],
                                                           sources[m][:, i + j, :], ident[:, :])
                        last.then_inc(turned.sem, 1)

                    def multiply(n):
                        i, nj = blocks[n]
                        pe.wait_ge(turned_sb.sem, s0 + n + 1)
                        if n >= 1:
                            pe.wait_ge(taken.sem, k0 + n)
                        for j in range(nj):
                            for m in range(M):
                                last = nc.tensor.matmul(
                                    ps[:, 6 + j // 2, (j % 2) * 256:(j % 2) * 256 + width],
                                    xT[0:K[m], n % 2, m, j * P:(j + 1) * P], weights[m],
                                    start=(m == 0), stop=(m == M - 1))
                        last.then_inc(product.sem, 1)

                    turn(0)
                    for n in range(len(blocks)):
                        if n + 1 < len(blocks):
                            turn(n + 1)
                        multiply(n)

                @block.scalar
                def _(act):
                    for n, (i, nj) in enumerate(blocks):
                        act.wait_ge(turned.sem, t0 + n + 1)
                        if n >= 2:
                            act.wait_ge(product.sem, p0 + n - 1)
                        for m in range(M):
                            last = nc.scalar.copy(xT[0:K[m], n % 2, m, 0:nj * P],
                                                  ps[0:K[m], 3 * (n % 2) + m, 0:nj * P])
                        last.then_inc(turned_sb.sem, 1)

                @block.vector
                def _(dve):
                    for n, (i, nj) in enumerate(blocks):
                        dve.wait_ge(product.sem, p0 + n + 1)
                        for b in range(-(-nj // 2)):
                            c = min(2, nj - 2 * b)
                            got = ps[:, 6 + b, :].rearrange("p (c n) -> p c n", c=2)[:, 0:c, 0:width]
                            last = nc.vector.tensor_copy(dest[:, i + 2 * b:i + 2 * b + c, :], got)
                        last.then_inc(taken.sem, 1)
            turned.base += len(blocks)
            turned_sb.base += len(blocks)
            product.base += len(blocks)
            taken.base += len(blocks)

        def on_vector(steps, scalar=()):
            with nc.Block() as block:
                count = [0, 0]
                a0, r0 = to_act.base, from_act.base

                @block.vector
                def _(dve):
                    v = Vector(dve)

                    def ask():
                        count[0] += 1
                        dve.nop().then_inc(to_act.sem, 1)
                        dve.wait_ge(from_act.sem, r0 + count[0])

                    steps(v, ask)

                if scalar:
                    @block.scalar
                    def _(act):
                        for n, run in enumerate(scalar):
                            act.wait_ge(to_act.sem, a0 + n + 1)
                            run().then_inc(from_act.sem, 1)
                to_act.base += len(scalar)
                from_act.base += len(scalar)

        V = nc.vector

        def bc(ap, *shape):
            return ap.to_broadcast([ap.shape[0], *shape])

        def layernorm(y, scratch, dest):
            mean, var = small[:, 0:KN], small[:, KN:2 * KN]
            std, inv = small[:, 2 * KN:3 * KN], small[:, 3 * KN:4 * KN]

            def steps(v, ask):
                v[V.tensor_reduce(mean, y, AX, ALU.add)]
                v[V.tensor_scalar(mean, mean, 1.0 / D, None, ALU.mult)]
                v[V.tensor_tensor(y, y, bc(mean.unsqueeze(2), KN, D), ALU.subtract)]
                v[V.tensor_tensor(scratch, y, y, ALU.mult)]
                v[V.tensor_reduce(var, scratch, AX, ALU.add)]
                v[V.tensor_scalar(var, var, 1.0 / D, EPS, ALU.mult, ALU.add)]
                ask()
                v[V.reciprocal(inv, std)]
                v[V.tensor_tensor(dest, y, bc(inv.unsqueeze(2), KN, D), ALU.mult)]

            on_vector(steps, [lambda: nc.scalar.activation(std, var, ACT.Sqrt)])

        RW = D + HEADS
        ring_at, oh_at = 0, RING * G * RW
        ohT_at = oh_at + 2 * G * P
        prod_at = ohT_at + 2 * G * P
        tab_at = prod_at + G * 2 * X1

        def pool_gathers(block, table, width, ring, gathered, free):
            @block.gpsimd
            def _(pool):
                staged = sem_take("staged")

                def stage(slot, g):
                    cols = src_i[:, g * G:(g + 1) * G] if isinstance(g, int) else src_i[:, bass.ds(g * G, G)]
                    pool.tensor_copy(idx[:, slot, :], cols).then_inc(staged, 1)

                def group(slot, g, more=True):
                    if not isinstance(g, int) or g >= RING - 1:
                        pool.wait_ge(free, g - (RING - 2))
                    pool.wait_ge(staged, g + 1)
                    if more:
                        stage((slot + 1) % RING, g + 1)
                    for j in range(G):
                        pool.indirect_dma_start(
                            out=ring[:, slot, j, :], out_offset=None, in_=table,
                            in_offset=bass.IndirectOffsetOnAxis(ap=idx[:, slot, j:j + 1], axis=0),
                        ).then_inc(gathered[slot], 16)

                stage(0, 0)
                for slot in range(RING):
                    group(slot, slot)
                with pool.Fori(1, NG // RING - 1) as r:
                    for slot in range(RING):
                        group(slot, r * RING + slot)
                for slot in range(RING):
                    group(slot, NG - RING + slot, more=slot + 1 < RING)

        taken_sems = {}

        def sem_take(name):
            n = taken_sems.get(name, 0)
            taken_sems[name] = n + 1
            taken_now.append(nc.alloc_semaphore(name=f"{name}_{n}"))
            return taken_now[-1]

        taken_now = []

        def recycle():
            nc.clear_and_free_semaphores(taken_now)
            nc.all_engine_barrier()
            taken_now.clear()

        def gather_scores(table, width, H, tab, products):
            F = H * X1 if products else H
            ring = view(arena, ring_at, RING * G * width).rearrange("p (r g w) -> p r g w", r=RING, g=G)
            oh = view(arena, oh_at, 2, G, P)
            ohT = view(arena, ohT_at, 2, G * P)
            prod = view(arena, prod_at, G, 2 * X1)
            sc = view(score, 0, S, H)
            gathered = [sem_take("gathered") for _ in range(RING)]
            free = sem_take("ring_taken")
            oh_ready, oh_turned = sem_take("onehot_ready"), sem_take("onehot_turned")
            ohT_ready, given = sem_take("onehotT_ready"), sem_take("dst_rows_ready")
            added, multiplied = sem_take("score_added"), sem_take("dst_rows_multiplied")

            with nc.Block() as block:
                pool_gathers(block, table, width, ring, gathered, free)

                @block.scalar
                def _(act):
                    with act.Fori(0, NG // RING) as r:
                        for slot in range(RING):
                            g = r * RING + slot
                            act.wait_ge(oh_turned, g + 1)
                            for b in range(2):
                                last = nc.scalar.copy(ohT[:, slot % 2, b * 512:(b + 1) * 512], ps[:, 2 * (slot % 2) + b, :])
                            last.then_inc(ohT_ready, 1)
                            act.wait_ge(gathered[slot], (r + 1) * (16 * G))
                            if not products:
                                nc.scalar.copy(sc[:, bass.ds(g * G, G), :], ring[:, slot, :, D:D + H])
                            nc.scalar.copy(xa[:, bass.ds(g * G, G), 0:D], ring[:, slot, :, 0:D]).then_inc(free, 1)

                @block.tensor
                def _(pe):
                    def turn(par, g):
                        pe.wait_ge(oh_ready, g + 1)
                        for j in range(G):
                            last = nc.tensor.transpose(ps[:, 2 * par + j // 4, (j % 4) * P:(j % 4 + 1) * P],
                                                       oh[:, par, j, :], ident[:, :])
                        last.then_inc(oh_turned, 1)

                    def rows_of_dst(par, g):
                        blocks = load_blocks(mybir.EngineType.PE, g * G, G)
                        pe.wait_ge(ohT_ready, g + 1)
                        pe.wait_ge(added, g + 1)
                        for j in range(G):
                            last = nc.tensor.matmul(ps[:, 4 + j // 2, (j % 2) * 256:(j % 2) * 256 + F],
                                                    ohT[:, par, j * P:(j + 1) * P],
                                                    tab[:, bass.ds(blocks[j], 1), :].rearrange("p a f -> p (a f)"),
                                                    start=True, stop=True)
                        last.then_inc(given, 1)

                    turn(0, 0)
                    with pe.Fori(0, NG // RING - 1) as r:
                        for slot in range(RING):
                            turn((slot + 1) % 2, r * RING + (slot + 1))
                            rows_of_dst(slot % 2, r * RING + slot)
                    for g in range(NG - RING, NG):
                        if g + 1 < NG:
                            turn((g + 1) % 2, g + 1)
                        rows_of_dst(g % 2, g)

                @block.vector
                def _(dve):
                    def onehots(par, g):
                        V.tensor_tensor(oh[:, par, :, :], lane[:, :].unsqueeze(1).to_broadcast([P, G, P]),
                                        some(dsel, g * G, G).unsqueeze(2).to_broadcast([P, G, P]),
                                        ALU.is_equal).then_inc(oh_ready, 1)

                    def add_scores(g):
                        dve.wait_ge(given, g + 1)
                        dve.wait_ge(free, g + 1)
                        if products:
                            for j in range(2):
                                last = V.tensor_tensor(
                                    prod.rearrange("p (b j) (h x) -> p b j h x", j=2, h=H)[:, :, j],
                                    ps[:, 4:8, j * 256:j * 256 + F].rearrange("p b (h x) -> p b h x", h=H),
                                    some(xa, g * G, G).rearrange("p (b j) x -> p b j x", j=2)[:, :, j].unsqueeze(2)
                                    .to_broadcast([P, G // 2, H, X1]), ALU.mult)
                            last.then_inc(multiplied, 1)
                            dve.wait_ge(multiplied, g + 1)
                            V.tensor_reduce(some(sc, g * G, G).rearrange("p g h -> p (g h)"),
                                            prod.rearrange("p g (h x) -> p (g h) x", h=H), AX, ALU.add).then_inc(added, 1)
                        else:
                            at = some(sc, g * G, G).rearrange("p (b j) h -> p b j h", j=2)
                            V.tensor_tensor(at, at, ps[:, 4:8, :].rearrange("p b (j f) -> p b j f", j=2)[:, :, :, 0:H],
                                            ALU.add).then_inc(added, 1)

                    V.memset(xa[:, :, D:X1], 1.0).then_inc(added, 1)
                    onehots(0, 0)
                    with dve.Fori(0, NG // RING - 1) as r:
                        for slot in range(RING):
                            onehots((slot + 1) % 2, r * RING + (slot + 1))
                            add_scores(r * RING + slot)
                    for g in range(NG - RING, NG):
                        if g + 1 < NG:
                            onehots((g + 1) % 2, g + 1)
                        add_scores(g)

        def some(t, at, n):
            return t[:, at:at + n] if isinstance(at, int) else t[:, bass.ds(at, n)]

        def load_blocks(engine, at, n):
            return nc.values_load_multi_w_load_instructions(
                some(step_i, at, n), engines=(engine,), min_val=0, max_val=KN - 1,
                skip_runtime_bounds_check_because="the staircase clamps it to the last block")[1]

        class Aggregation:

            def __init__(self, H, W, parts, oh, messages, acc):
                self.H, self.W, self.parts, self.acc = H, W, parts, acc
                self.B = 2 if H > 4 else G
                self.NB = S // self.B
                self.oh, self.messages = oh, messages
                self.ready, self.done = sem_take("messages_ready"), sem_take("batch_multiplied")
                self.summed = sem_take("step_summed")

            def place(self, par, j):
                if self.H > 4:
                    return ps[:, 4 * par + 2 * j:4 * par + 2 * j + 2, 0:self.H * self.W // 2]
                if self.H == 1:
                    return ps[:, 2 * par + j // 4, (j % 4) * 128:(j % 4) * 128 + self.W]
                return ps[:, 4 * par + j // 2, (j % 2) * 256:(j % 2) * 256 + self.H * self.W]

            def build(self, par, b, weight):
                B, H = self.B, self.H
                V.tensor_tensor(self.oh[:, par * B:(par + 1) * B, :], lane[:, :].unsqueeze(1).to_broadcast([P, B, P]),
                                some(dsel, b * B, B).unsqueeze(2).to_broadcast([P, B, P]), ALU.is_equal)
                V.tensor_tensor(self.messages[:, par * B:(par + 1) * B, :].rearrange("p b (h x) -> p b h x", h=H),
                                some(xa, b * B, B).unsqueeze(2).to_broadcast([P, B, H, X1]),
                                some(weight, b * B, B).unsqueeze(3).to_broadcast([P, B, H, X1]),
                                ALU.mult).then_inc(self.ready, 1)

            def multiply(self, pe, par, b, row=None):
                pe.wait_ge(self.ready, b + 1)
                for j in range(self.B):
                    to = self.place(par, j)
                    at = self.messages[:, par * self.B + j, :] if row is None else row(j)
                    if self.H > 4:
                        half = self.H * self.W // 2
                        for n in range(2):
                            last = nc.tensor.matmul(to[:, n, :], self.oh[:, par * self.B + j, :],
                                                    at[:, n * half:(n + 1) * half], start=True, stop=True)
                    else:
                        last = nc.tensor.matmul(to, self.oh[:, par * self.B + j, :], at, start=True, stop=True)
                last.then_inc(self.done, 1)

            def add(self, dve, par, b, blocks):
                dve.wait_ge(self.done, b + 1)
                for j in range(self.B):
                    dve.wait_ge(self.summed, b * self.B + (j + 1))
                    at = self.acc[j % self.parts][:, bass.ds(blocks[j], 1), :]
                    if self.H > 4:
                        at = at.rearrange("p a (n w) -> p (a n) w", n=2)
                    else:
                        at = at.rearrange("p a w -> p (a w)")
                    V.tensor_tensor(at, at, self.place(par, j), ALU.add).then_inc(self.summed, 1)

            def clear(self):
                for n in range(self.parts - 1):
                    V.memset(self.acc[n], 0.0)
                V.memset(self.acc[self.parts - 1], 0.0).then_inc(self.summed, self.parts)

            def total(self, dve):
                if self.parts == 2:
                    dve.wait_ge(self.summed, S + 2)
                    V.tensor_tensor(self.acc[0], self.acc[0], self.acc[1], ALU.add)

        def aggregate(H, weight, gather=None):
            W = H * X1
            parts = 1 if H > 4 else 2
            acc = [view(arena, n * KN * W, KN, W) for n in range(parts)]
            if H > 4:
                oh, messages = view(oh_s, 0, 4, P), view(msg, 0, 4, W)
            else:
                at = parts * KN * W
                oh, messages = view(arena, at, 2 * G, P), view(arena, at + 2 * G * P, 2 * G, W)
                if gather is not None:
                    messages = view(msg, 0, 2 * G, W)
            agg = Aggregation(H, X1, parts, oh, messages, acc)
            U = G // agg.B if H > 4 else 2
            NR = agg.NB // U
            with nc.Block() as block:
                if gather is not None:
                    ring = view(arena, arena.shape[1] - RING * G * D, RING * G * D).rearrange("p (r g w) -> p r g w", r=RING, g=G)
                    gathered, free = [sem_take("gathered") for _ in range(RING)], sem_take("ring_taken")
                    pool_gathers(block, gather, D, ring, gathered, free)

                    @block.scalar
                    def _(act):
                        with act.Fori(0, NG // RING) as r:
                            for slot in range(RING):
                                act.wait_ge(gathered[slot], (r + 1) * (16 * G))
                                nc.scalar.copy(xa[:, bass.ds((r * RING + slot) * G, G), 0:D], ring[:, slot, :, :]).then_inc(free, 1)

                @block.tensor
                def _(pe):
                    with pe.Fori(0, NR) as r:
                        for u in range(U):
                            agg.multiply(pe, u % 2, r * U + u)

                @block.vector
                def _(dve):
                    if gather is not None:
                        Vector(dve)[V.memset(xa[:, :, D:X1], 1.0)]
                    agg.clear()

                    def build(par, b):
                        if gather is not None:
                            dve.wait_ge(free, b + 1)
                        agg.build(par, b, weight)

                    def body(r, last):
                        steps = load_blocks(mybir.EngineType.DVE, r * U * agg.B, G)
                        for u in range(U):
                            if u + 1 < U or not last:
                                build((u + 1) % 2, r * U + (u + 1))
                            if u * agg.B % G == 0 and u:
                                steps = load_blocks(mybir.EngineType.DVE, (r * U + u) * agg.B, G)
                            at = u * agg.B % G
                            agg.add(dve, u % 2, r * U + u, steps[at:at + agg.B])

                    build(0, 0)
                    with dve.Fori(0, NR - 1) as r:
                        body(r, False)
                    body(NR - 1, True)
                    agg.total(dve)
            return acc[0]

        def softmax_numerators(H, leaky):
            sc = view(score, 0, S, H)
            scT = view(arena, 0, H, C * P)[0:SP]
            fwd = view(arena, HEADS * 512, H, C * P)[0:SP]
            bwd = view(arena, 2 * HEADS * 512, H, C * P)[0:SP]
            flag_f, flag_b = view(msg, 0, C * P)[0:SP], view(msg, C * P, C * P)[0:SP]
            in_first, in_last = view(msg, 2 * C * P, C, P)[0:SP], view(msg, 3 * C * P, C, P)[0:SP]
            rows = view(score, 0, 3, S)[0:H]
            tail, head, run, back = (view(score, (3 + n) * S, S)[0:H] for n in range(4))
            valid = view(oh_s, 0, S)
            past = view(oh_s, S, S)
            rows_in = sem_take("rows_in")
            carry = view(small, 0, 2, C * H)[0:SP]
            scores_ready, turned_in = sem_take("scores_ready"), sem_take("scores_turned")
            sT_ready, scanned = sem_take("scoresT_ready"), sem_take("scanned")
            ends_out, chained = sem_take("tile_ends_turned"), sem_take("tiles_chained")
            carry_out, centred = sem_take("carries_turned"), sem_take("centred")
            exped, turned_out = sem_take("exp_done"), sem_take("exp_turned")
            is_first = view(arena, 3 * HEADS * 512, C, P)[0:SP]
            first_max = view(arena, 2 * HEADS * 512, S, H)
            max_ready, max_out, exp_taken = sem_take("max_ready"), sem_take("max_turned"), sem_take("exp_taken")

            with nc.Block() as block:
                @block.sync
                def _(sp):
                    for n in range(4):
                        sp.dma_start(msg[0:SP, n * C * P:(n + 1) * C * P], flags_dram[n]).then_inc(rows_in, 16)
                    sp.wait_ge(turned_in, H)
                    sp.dma_start(score[0:H, 0:3 * S], rows_dram[0:H, :]).then_inc(rows_in, 16)

                @block.tensor
                def _(pe):
                    pe.wait_ge(scores_ready, 1)
                    for h in range(H):
                        for c in range(C):
                            last = nc.tensor.transpose(ps[0:SP, h, c * P:(c + 1) * P],
                                                       sc[:, c * SP:(c + 1) * SP, h], ident[:, :])
                        last.then_inc(turned_in, 1)
                    pe.wait_ge(scanned, 1)
                    for n, (of, at) in enumerate(((fwd, P - 1), (bwd, 0))):
                        for c in range(C):
                            last = nc.tensor.transpose(ps[0:H, n, c * SP:(c + 1) * SP],
                                                       of[:, :, c * P + at], ident[0:SP, 0:SP])
                    last.then_inc(ends_out, 1)
                    pe.wait_ge(chained, 1)
                    for n, row in enumerate((run, back)):
                        for c in range(C):
                            last = nc.tensor.transpose(ps[0:SP, n, c * H:(c + 1) * H], row[:, c * SP:(c + 1) * SP],
                                                       ident[0:H, 0:H])
                    last.then_inc(carry_out, 1)
                    for h in range(H):
                        pe.wait_ge(exped, h + 1)
                        for c in range(C):
                            last = nc.tensor.transpose(ps[:, h, c * SP:(c + 1) * SP],
                                                       scT[:, h, c * P:(c + 1) * P], ident[0:SP, 0:SP])
                        last.then_inc(turned_out, 1)
                    if leaky:
                        for h in range(H):
                            pe.wait_ge(max_ready, h + 1)
                            pe.wait_ge(exp_taken, h + 1)
                            for c in range(C):
                                last = nc.tensor.transpose(ps[:, h, c * SP:(c + 1) * SP],
                                                           fwd[:, h, c * P:(c + 1) * P], ident[0:SP, 0:SP])
                            last.then_inc(max_out, 1)

                @block.scalar
                def _(act):
                    for h in range(H):
                        act.wait_ge(turned_in, h + 1)
                        nc.scalar.copy(scT[:, h, :], ps[0:SP, h, :]).then_inc(sT_ready, 1)
                    for h in range(H):
                        act.wait_ge(centred, h + 1)
                        nc.scalar.activation(scT[:, h, :], scT[:, h, :], ACT.Exp).then_inc(exped, 1)

                @block.vector
                def _(dve):
                    v = Vector(dve)
                    if leaky:
                        v[V.scalar_tensor_tensor(out=sc, in0=sc, scalar=0.2, in1=sc, op0=ALU.mult, op1=ALU.max)]
                    v[V.tensor_scalar(valid, dsel[:, :], 0.0, None, ALU.is_ge)]
                    v[V.tensor_scalar(past, dsel[:, :], float(P), None, ALU.is_ge)]
                    v[V.tensor_tensor(valid, valid, past, ALU.subtract)]
                    v[V.tensor_scalar(valid, valid, -1.0, BIG, ALU.add, ALU.mult)]
                    V.tensor_tensor(sc, sc, valid.unsqueeze(2).to_broadcast([P, S, H]), ALU.add).then_inc(scores_ready, 1)
                    dve.wait_ge(rows_in, 16 * 5)
                    for h in range(H):
                        dve.wait_ge(sT_ready, h + 1)
                        V.tensor_tensor_scan(fwd[:, h, :], flag_f, scT[:, h, :], -BIG, ALU.add, ALU.max)
                        last = V.tensor_tensor_scan(bwd[:, h, ::-1], flag_b[:, ::-1], scT[:, h, ::-1], -BIG, ALU.add, ALU.max)
                    v[last]
                    dve.nop().then_inc(scanned, 1)
                    dve.wait_ge(ends_out, 1)
                    v[V.tensor_copy(tail, ps[0:H, 0, 0:S])]
                    v[V.tensor_copy(head, ps[0:H, 1, 0:S])]
                    v[V.tensor_tensor(fwd, fwd, bwd, ALU.max)]
                    v[V.tensor_tensor_scan(tail, rows[:, 0, :], tail, -BIG, ALU.add, ALU.max)]
                    v[V.tensor_tensor_scan(head[:, ::-1], rows[:, 2, ::-1], head[:, ::-1], -BIG, ALU.add, ALU.max)]
                    v[V.memset(run[:, 0:1], -BIG)]
                    v[V.memset(back[:, S - 1:S], -BIG)]
                    v[V.tensor_tensor(run[:, 1:S], tail[:, 0:S - 1], rows[:, 1, 1:S], ALU.add)]
                    v[V.tensor_tensor(back[:, 0:S - 1], head[:, 1:S], rows[:, 1, 1:S], ALU.add)]
                    dve.nop().then_inc(chained, 1)
                    dve.wait_ge(carry_out, 1)
                    v[V.tensor_copy(carry, ps[0:SP, 0:2, 0:C * H])]
                    for n, mask in enumerate((in_first, in_last)):
                        for h in range(H):
                            for c in range(C):
                                m = fwd[:, h, c * P:(c + 1) * P]
                                last = V.scalar_tensor_tensor(out=m, in0=mask[:, c, :],
                                                              scalar=carry[:, n, c * H + h:c * H + h + 1],
                                                              in1=m, op0=ALU.add, op1=ALU.max)
                        v[last]
                    for h in range(H):
                        last = V.tensor_tensor(scT[:, h, :], scT[:, h, :], fwd[:, h, :], ALU.subtract)
                        last.then_inc(centred, 1)
                    if leaky:
                        v[V.tensor_scalar(is_first, flag_f.rearrange("p (c e) -> p c e", c=C), 0.0, None, ALU.is_lt)]
                        v[V.tensor_scalar(is_first[:, :, 0], carry[:, 0, :].rearrange("p (c h) -> p c h", h=H)[:, :, 0],
                                          -0.5 * BIG, None, ALU.is_lt)]
                        for h in range(H):
                            V.tensor_tensor(fwd[:, h, :], fwd[:, h, :], is_first.rearrange("p c e -> p (c e)"),
                                            ALU.mult).then_inc(max_ready, 1)
                    for h in range(H):
                        dve.wait_ge(turned_out, h + 1)
                        V.tensor_copy(sc[:, :, h], ps[:, h, 0:S]).then_inc(exp_taken, 1)
                    if leaky:
                        for h in range(H):
                            dve.wait_ge(max_out, h + 1)
                            V.tensor_copy(first_max[:, :, h], ps[:, h, 0:S])
            return sc, first_max

        def node_maximum(H, first_max, dest):
            oh, rows = view(arena, 0, 2 * G, P), first_max
            other = view(arena, 2 * G * P, KN, H)
            agg = Aggregation(1, H, 2, oh, None, [dest, other])
            with nc.Block() as block:
                def onehots(par, b):
                    V.tensor_tensor(oh[:, par * G:(par + 1) * G, :], lane[:, :].unsqueeze(1).to_broadcast([P, G, P]),
                                    some(dsel, b * G, G).unsqueeze(2).to_broadcast([P, G, P]),
                                    ALU.is_equal).then_inc(agg.ready, 1)

                @block.tensor
                def _(pe):
                    with pe.Fori(0, NG // 2) as r:
                        for u in range(2):
                            agg.multiply(pe, u, r * 2 + u, row=lambda j: some(rows, (r * 2 + u) * G + j, 1).rearrange("p a h -> p (a h)"))

                @block.vector
                def _(dve):
                    def body(r, last):
                        for u in range(2):
                            blocks = load_blocks(mybir.EngineType.DVE, (r * 2 + u) * G, G)
                            if u == 0 or not last:
                                onehots(1 - u, r * 2 + (u + 1))
                            agg.add(dve, u, r * 2 + u, blocks)

                    agg.clear()
                    onehots(0, 0)
                    with dve.Fori(0, NG // 2 - 1) as r:
                        body(r, False)
                    body(NG // 2 - 1, True)
                    agg.total(dve)

        def add_self_loop(H, acc, peak, own, row, work):
            a4 = acc.rearrange("p k (h x) -> p k h x", h=H)
            none = view(work, KN * H * X1, KN, H)

            def steps(v, ask):
                v[V.scalar_tensor_tensor(out=own, in0=own, scalar=0.2, in1=own, op0=ALU.mult, op1=ALU.max)]
                v[V.tensor_scalar(none, a4[:, :, :, D], 0.0, -BIG, ALU.is_equal, ALU.mult)]
                v[V.tensor_tensor(peak, peak, none, ALU.add)]
                v[V.tensor_tensor(none, peak, own, ALU.max)]
                v[V.tensor_tensor(peak, peak, none, ALU.subtract)]
                v[V.tensor_tensor(own, own, none, ALU.subtract)]
                ask()
                ask()
                part = view(work, 0, KN * H, X1)
                for k in range(KN):
                    last = V.tensor_tensor(part[:, k * H:(k + 1) * H, :], row[:, k:k + 1, :].to_broadcast([P, H, X1]),
                                           own[:, k, :].unsqueeze(2).to_broadcast([P, H, X1]), ALU.mult)
                v[last]
                flat = acc.rearrange("p k (h x) -> p (k h) x", h=H)
                v[V.tensor_tensor(flat, flat, peak.rearrange("p k h -> p (k h)").unsqueeze(2).to_broadcast([P, KN * H, X1]), ALU.mult)]
                v[V.tensor_tensor(flat, flat, part, ALU.add)]
            on_vector(steps, [lambda: nc.scalar.activation(peak, peak, ACT.Exp), lambda: nc.scalar.activation(own, own, ACT.Exp)])

        def bwd_row(x):
            return x

        raw_i = view(msg, 0, 2, T).bitcast(I32)
        load([(xs[:, :, 0:D], a["x"].rearrange("(k p) d -> p k d", p=P)),
              (raw_i[:, 0, :], a["dst"]), (raw_i[:, 1, :], a["src"])])

        s_idx = view(arena, 0, S)
        t_idx = view(arena, 448, C)
        k_edge = view(arena, 460, KN)
        with nc.Block() as block:
            @block.gpsimd
            def _(pool):
                pool.memset(ident[:, :], 0.0).then_inc(pool_done.sem, 1)
                pool.wait_ge(pool_done.sem, pool_done.base + 1)
                pool.affine_select(out=ident[:, :], in_=ident[:, :], compare_op=ALU.not_equal, fill=1.0, base=0,
                                   pattern=[[-1, P]], channel_multiplier=1)
                pool.iota(lane[:, :], [[1, P]], base=0, channel_multiplier=0, allow_small_or_imprecise_dtypes=True)
                pool.iota(s_idx, [[1, S]], base=0, channel_multiplier=0, allow_small_or_imprecise_dtypes=True)
                pool.iota(t_idx, [[TP, C]], base=0, channel_multiplier=1, allow_small_or_imprecise_dtypes=True)
                pool.iota(k_edge, [[P, KN]], base=0, channel_multiplier=0, allow_small_or_imprecise_dtypes=True)

            @block.vector
            def _(dve):
                V.memset(xs[:, :, D:X1], 1.0)
        pool_done.base += 1

        flags_dram = nc.dram_tensor("flags", (4, SP, C * P), F32).ap()
        rows_dram = nc.dram_tensor("rows", (HEADS, 3 * S), F32).ap()
        sel_dram = nc.dram_tensor("tile_of_steps", (P, S), F32).ap()
        raw_f = view(arena, 512, 2, T)
        rawT = view(x_all, 0, 2 * C, P)[0:TP]
        wide = view(x_all, 1100, C, S)[0:TP]
        ones = view(x_all, 3000, P)
        tile_of = view(x_all, 3200, S)
        block_of = view(x_all, 3700, S)
        ge = view(x_all, 4200, C, KN)[0:TP]
        end = view(x_all, 4400, C)[0:TP]
        key, valid = view(x_all, 4500, S), view(x_all, 5000, S)
        keyT = view(x_all, 5500, C, P)[0:SP]
        flags = view(x_all, 6100, 4, C * P)[0:SP]
        first_row, last_row = view(x_all, 8200, S)[0:HEADS], view(x_all, 8700, S)[0:HEADS]
        cont = view(x_all, 9200, S + 1)[0:HEADS]
        rows = view(x_all, 9700, 3, S)[0:HEADS]
        ends = view(x_all, 11100, 2, HEADS)
        with nc.Block() as block:
            @block.vector
            def _(dve):
                v = Vector(dve)
                v[V.tensor_copy(raw_f, raw_i)]
                v[V.memset(ones, 1.0)]
                v[V.tensor_copy(ends[:, 0, :], ident[:, 0:1].to_broadcast([P, HEADS]))]
                v[V.tensor_copy(ends[:, 1, :], ident[:, P - 1:P].to_broadcast([P, HEADS]))]
                dve.nop().then_inc(to_pe.sem, 1)
                dve.wait_ge(from_pe.sem, from_pe.base + 1)
                v[V.tensor_copy(rawT.rearrange("p (b c) e -> p b (c e)", b=2), ps[0:TP, 0:2, :])]
                dstT = rawT[:, 0:C, :]
                v[V.tensor_tensor(ge, dstT[:, :, P - 1:P].to_broadcast([TP, C, KN]),
                                  k_edge[0:TP].unsqueeze(1).to_broadcast([TP, C, KN]), ALU.is_ge)]
                v[V.tensor_reduce(end, ge, AX, ALU.add)]
                v[V.scalar_tensor_tensor(out=end, in0=end, scalar=-1.0, in1=t_idx[0:TP], op0=ALU.add, op1=ALU.add)]
                for c in range(C):
                    v[V.tensor_scalar(wide[:, c, :], s_idx[0:TP], end[:, c:c + 1], None, ALU.is_gt)]
                dve.nop().then_inc(to_pe.sem, 1)
                dve.wait_ge(from_pe.sem, from_pe.base + 2)
                v[V.tensor_copy(tile_of, ps[:, 2, 0:S])]
                v[V.tensor_tensor(block_of, s_idx, tile_of, ALU.subtract)]
                v[V.tensor_scalar(block_of, block_of, float(KN - 1), 0.0, ALU.min, ALU.max)]
                v[V.tensor_copy(step_i, block_of[0:1, :])]
                for c in range(C):
                    v[V.tensor_scalar(wide[:, c, :], tile_of[0:TP], t_idx[0:TP, c:c + 1], None, ALU.is_equal)]
                dve.nop().then_inc(to_pe.sem, 1)
                dve.wait_ge(from_pe.sem, from_pe.base + 3)
                v[V.tensor_copy(src_i[:, :], ps[:, 4, 0:S])]
                v[V.scalar_tensor_tensor(out=dsel[:, :], in0=block_of, scalar=-float(P), in1=ps[:, 3, 0:S],
                                         op0=ALU.mult, op1=ALU.add)]
                v[V.tensor_scalar(valid, dsel[:, :], 0.0, None, ALU.is_ge)]
                v[V.tensor_scalar(key, dsel[:, :], float(P), None, ALU.is_ge)]
                v[V.tensor_tensor(valid, valid, key, ALU.subtract)]
                v[V.scalar_tensor_tensor(out=key, in0=ps[:, 3, 0:S], scalar=1.0, in1=valid, op0=ALU.add, op1=ALU.mult)]
                dve.nop().then_inc(to_pe.sem, 1)
                dve.wait_ge(from_pe.sem, from_pe.base + 4)
                v[V.tensor_copy(keyT.rearrange("p c e -> p (c e)"), ps[0:SP, 5, :])]
                ff, fb, inf, inl = (flags[:, n, :].rearrange("p (c e) -> p c e", c=C) for n in range(4))
                v[V.memset(flags[:, 0:2, :], 0.0)]
                v[V.tensor_tensor(ff[:, :, 1:P], keyT[:, :, 1:P], keyT[:, :, 0:P - 1], ALU.is_equal)]
                v[V.tensor_copy(fb[:, :, 0:P - 1], ff[:, :, 1:P])]
                v[V.tensor_tensor(inf, keyT, keyT[:, :, 0:1].to_broadcast([SP, C, P]), ALU.is_equal)]
                v[V.tensor_tensor(inl, keyT, keyT[:, :, P - 1:P].to_broadcast([SP, C, P]), ALU.is_equal)]
                v[V.tensor_scalar(flags, flags, -1.0, BIG, ALU.add, ALU.mult)]
                v[V.tensor_copy(first_row, ps[0:HEADS, 6, 0:S])]
                v[V.tensor_copy(last_row, ps[0:HEADS, 7, 0:S])]
                v[V.memset(cont, 0.0)]
                v[V.tensor_tensor(cont[:, 1:S], first_row[:, 1:S], last_row[:, 0:S - 1], ALU.is_equal)]
                v[V.tensor_tensor(first_row, first_row, last_row, ALU.is_equal)]
                v[V.tensor_tensor(rows[:, 0, :], first_row, cont[:, 0:S], ALU.mult)]
                v[V.tensor_copy(rows[:, 1, :], cont[:, 0:S])]
                v[V.tensor_tensor(rows[:, 2, :], first_row, cont[:, 1:S + 1], ALU.mult)]
                v[V.tensor_scalar(rows, rows, -1.0, BIG, ALU.add, ALU.mult)]

            @block.tensor
            def _(pe):
                pe.wait_ge(to_pe.sem, to_pe.base + 1)
                for b in range(2):
                    for c in range(C):
                        last = nc.tensor.transpose(ps[0:TP, b, c * P:(c + 1) * P], raw_f[:, b, c * TP:(c + 1) * TP], ident[:, :])
                last.then_inc(from_pe.sem, 1)
                pe.wait_ge(to_pe.sem, to_pe.base + 2)
                for c in range(C):
                    last = nc.tensor.matmul(ps[:, 2, 0:S], ones[0:TP, :], wide[:, c, :], start=(c == 0), stop=(c == C - 1))
                last.then_inc(from_pe.sem, 1)
                pe.wait_ge(to_pe.sem, to_pe.base + 3)
                for b in range(2):
                    for c in range(C):
                        last = nc.tensor.matmul(ps[:, 3 + b, 0:S], rawT[:, b * C + c, :], wide[:, c, :],
                                                start=(c == 0), stop=(c == C - 1))
                last.then_inc(from_pe.sem, 1)
                pe.wait_ge(to_pe.sem, to_pe.base + 4)
                for c in range(C):
                    nc.tensor.transpose(ps[0:SP, 5, c * P:(c + 1) * P], key[:, c * SP:(c + 1) * SP], ident[:, :])
                for n in range(2):
                    last = nc.tensor.matmul(ps[0:HEADS, 6 + n, 0:S], ends[:, n, :], key, start=True, stop=True)
                last.then_inc(from_pe.sem, 1)
        to_pe.base += 4
        from_pe.base += 4
        tiles_dram = nc.dram_tensor("tiles", (1, S), I32).ap()
        tiles_i = view(x_all, 12000, S).bitcast(I32)

        def steps(v, ask):
            v[V.tensor_scalar(tile_of, tile_of, float(T - 1), None, ALU.min)]
            v[V.tensor_copy(tiles_i, tile_of)]
        store([(flags_dram[n], flags[:, n, :]) for n in range(4)]
              + [(rows_dram, rows.rearrange("p n s -> p (n s)")), (sel_dram, tile_of)])
        on_vector(steps)
        store([(tiles_dram, tiles_i[0:1, :])])

        ew_dram = nc.dram_tensor("ew_by_step", (P, S, 2), F32).ap()
        ew_raw, ewT = view(x_all, 13000, 2, T), view(x_all, 14000, 2 * C, P)[0:TP]
        ew_step = view(x_all, 15100, S, 2)
        load([(ew_raw, a["ew"])])
        with nc.Block() as block:
            @block.tensor
            def _(pe):
                for b in range(2):
                    for c in range(C):
                        last = nc.tensor.transpose(ps[0:TP, b, c * P:(c + 1) * P], ew_raw[:, b, c * TP:(c + 1) * TP], ident[:, :])
                last.then_inc(from_pe.sem, 1)
                pe.wait_ge(to_pe.sem, to_pe.base + 1)
                for b in range(2):
                    for c in range(C):
                        last = nc.tensor.matmul(ps[:, 2 + b, 0:S], ewT[:, b * C + c, :], wide[:, c, :],
                                                start=(c == 0), stop=(c == C - 1))
                last.then_inc(from_pe.sem, 1)

            @block.vector
            def _(dve):
                dve.wait_ge(from_pe.sem, from_pe.base + 1)
                V.tensor_copy(ewT.rearrange("p (b c) e -> p b (c e)", b=2), ps[0:TP, 0:2, :]).then_inc(to_pe.sem, 1)
                dve.wait_ge(from_pe.sem, from_pe.base + 2)
                V.tensor_copy(ew_step.rearrange("p s h -> p h s"), ps[:, 2:4, 0:S])
        to_pe.base += 1
        from_pe.base += 2
        store([(ew_dram, ew_step)])

        def table(name, width):
            return nc.dram_tensor(name, (NPAD, width), F32).ap()

        def rows_of(t):
            return t.rearrange("(k p) d -> p k d", p=P)

        xw = xs[:, :, 0:D]
        tab_H = view(arena, tab_at, KN, 2 * X1)
        node = [view(x_all, n * KN * D, KN, D) for n in range(8)]
        wide_x = view(x_all, 8 * KN * D, KN, 4 * D)

        def normalise(H, acc, dest, add_small):
            den = view(small, 0, KN, 1) if H == 1 else None
            v4 = acc.rearrange("p k (h x) -> p (k h) x", h=H)
            den = view(msg, 0, KN * H)

            def steps(v, ask):
                v[V.tensor_scalar(den, v4[:, :, D], 1e-16, None, ALU.add)]
                v[V.reciprocal(den, den)]
                w = dest.shape[2] // H
                v[V.tensor_tensor(dest.rearrange("p k (h x) -> p (k h) x", h=H), v4[:, :, 0:w],
                                  den.unsqueeze(2).to_broadcast([P, KN * H, w]), ALU.mult)]
            on_vector(steps)

        W1 = view(x_all, 1024, 256)[0:D]
        V1 = view(x_all, 1280, 16)[0:D]
        peak, own = view(wbuf, 0, KN, HEADS), view(wbuf, KN * HEADS, KN, HEADS)
        att1 = view(x_all, 0, 2, 256)[0:D]
        t1 = view(x_all, 512, 2, 256)[0:D]
        load([(W1, a["L0_gnn_W1"]),
              (att1[:, 0, :], a["L0_gnn_a1_src"].partition_broadcast(D)),
              (att1[:, 1, :], a["L0_gnn_a1_dst"].partition_broadcast(D))])

        def steps(v, ask):
            v[V.tensor_tensor(t1, att1, W1.unsqueeze(1).to_broadcast([D, 2, 256]), ALU.mult)]
            v[V.tensor_reduce(V1, t1.rearrange("p a (h c) -> p (a h) c", c=HID), AX, ALU.add)]
        on_vector(steps)
        al = view(x_all, 8000, KN, 16)
        dense([xw], [V1], al)
        row0 = view(x_all, 2000, KN, RW)
        tab_al = view(arena, tab_at, KN, HEADS)

        def steps(v, ask):
            v[V.tensor_copy(row0[:, :, 0:D], xw)]
            v[V.tensor_copy(row0[:, :, D:RW], al[:, :, 0:HEADS])]
            v[V.tensor_copy(tab_al, al[:, :, HEADS:16])]
            v[V.tensor_tensor(own, al[:, :, 0:HEADS], al[:, :, HEADS:16], ALU.add)]
        on_vector(steps)
        table0 = table("table0", RW)
        store([(rows_of(table0), row0)])
        gather_scores(table0, RW, HEADS, tab_al, False)
        weight, first_max = softmax_numerators(HEADS, True)
        node_maximum(HEADS, first_max, peak)
        acc = aggregate(HEADS, weight)
        add_self_loop(HEADS, acc, peak, own, xs, x_all)
        agg = view(x_all, 0, KN, HEADS * D)
        normalise(HEADS, acc, agg, True)
        h1 = view(arena, 0, KN, 256)
        W1p = view(arena, 6400, 4, 2 * HID)
        W2a = view(arena, 6700, 2, D + 2)
        b1 = view(arena, 7000, 256)
        att2 = view(arena, 7300, 2, D)
        t2 = view(arena, 7500, 2, 2 * D)
        b2 = view(arena, 7800, D)

        def steps(v, ask):
            v[V.memset(W1p, 0.0)]
        on_vector(steps)
        W1v = a["L0_gnn_W1"].rearrange("f (q j c) -> f q j c", j=2, c=HID)
        load([(W1p[0:D, :, 0:HID], W1v[:, :, 0, :]), (W1p[D:P, :, HID:2 * HID], W1v[:, :, 1, :]),
              (W2a[:, :, 0:D], a["L0_gnn_W2"].rearrange("(m p) c -> p m c", p=P)),
              (b1, a["L0_gnn_b1"].partition_broadcast(P)), (b2, a["L0_gnn_b2"].partition_broadcast(P)),
              (att2[:, 0, :], a["L0_gnn_a2_src"].partition_broadcast(P)),
              (att2[:, 1, :], a["L0_gnn_a2_dst"].partition_broadcast(P))])

        def steps(v, ask):
            for n in range(2):
                v[V.tensor_tensor(t2[:, n, :].rearrange("p (m c) -> p m c", m=2), W2a[:, :, 0:D],
                                  att2[:, n:n + 1, :].to_broadcast([P, 2, D]), ALU.mult)]
                v[V.tensor_reduce(W2a[:, :, D + n], t2[:, n, :].rearrange("p (m c) -> p m c", m=2), AX, ALU.add)]
        on_vector(steps)
        for q in range(4):
            dense([agg[:, :, q * P:(q + 1) * P]], [W1p[:, q, :]], h1[:, :, q * D:(q + 1) * D])
        neg = view(x_all, 0, KN, 256)

        def steps(v, ask):
            v[V.tensor_tensor(h1, h1, b1.unsqueeze(1).to_broadcast([P, KN, 256]), ALU.add)]
            v[V.tensor_scalar(neg, h1, 0.0, None, ALU.min)]
            ask()
            v[V.tensor_scalar(h1, h1, 0.0, -1.0, ALU.max, ALU.add)]
            v[V.tensor_tensor(h1, h1, neg, ALU.add)]
        on_vector(steps, [lambda: nc.scalar.activation(neg, neg, ACT.Exp)])
        h2 = view(x_all, 0, KN, D + 2)
        dense([h1[:, :, 0:P], h1[:, :, P:256]], [W2a[:, 0, :], W2a[:, 1, :]], h2)
        row1 = view(x_all, 2000, KN, X1)
        b2_keep = wbuf[:, 0:D]
        peak, own = view(wbuf, D, KN, 1), view(wbuf, D + KN, KN, 1)
        tab1 = view(arena, tab_at, KN, 1)

        def steps(v, ask):
            v[V.tensor_copy(row1, h2[:, :, 0:X1])]
            v[V.tensor_copy(b2_keep, b2)]
            v[V.tensor_copy(tab1, h2[:, :, X1:X1 + 1])]
            v[V.tensor_tensor(own, h2[:, :, D:X1], h2[:, :, X1:X1 + 1], ALU.add)]
        on_vector(steps)
        table1 = table("table1", X1)
        store([(rows_of(table1), row1)])
        recycle()
        gather_scores(table1, X1, 1, tab1, False)
        weight, first_max = softmax_numerators(1, True)
        node_maximum(1, first_max, peak)
        acc = aggregate(1, weight)
        row1 = view(x_all, 4000, KN, X1)
        load([(row1, rows_of(table1))])

        def steps(v, ask):
            v[V.memset(row1[:, :, D:X1], 1.0)]
        on_vector(steps)
        add_self_loop(1, acc, peak, own, row1, x_all)
        y = node[0]
        normalise(1, acc, y, True)

        def steps(v, ask):
            v[V.tensor_tensor(y, y, b2_keep.unsqueeze(1).to_broadcast([P, KN, D]), ALU.add)]
            v[V.tensor_tensor(y, y, xw, ALU.add)]
        on_vector(steps)
        layernorm(y, node[1], xw)

        Wn, Wc, Wp = (wbuf[0:X1, n * D:(n + 1) * D] for n in range(3))
        be2 = wbuf[:, 3 * D:4 * D]
        We2 = wbuf[:, 4 * D:5 * D]
        We1 = wbuf[:, 5 * D:7 * D]
        be1 = wbuf[:, 7 * D:7 * D + 1]

        def steps(v, ask):
            v[V.memset(We1, 0.0)]
        on_vector(steps)
        load([(Wn, a["L1_Wn"]), (Wc, a["L1_Wc"]), (Wp, a["L1_Wp"]), (be2, a["L1_gnn_be2"].partition_broadcast(P))]
             + [pair for h in range(2) for pair in (
                 (We2[h * D:(h + 1) * D, :], a["L1_We2"]), (We1[h * D:(h + 1) * D, h * D:(h + 1) * D], a["L1_We1"]),
                 (be1[h * D:(h + 1) * D, :], a["L1_gnn_be1"].rearrange("(d o) -> d o", o=1)))])
        hn = node[0]
        dense([xs[:, :, :]], [Wn], hn)
        table2 = table("table2", D)
        store([(rows_of(table2), hn)])

        recycle()
        agg = Aggregation(1, X1, 2, view(arena, 3328, 2 * G, P), None, [view(arena, n * KN * X1, KN, X1) for n in range(2)])
        acc = agg.acc[0]
        ring = view(arena, 5376, RING * G * D).rearrange("p (r g w) -> p r g w", r=RING, g=G)
        ea = view(arena, 7424, 2, 512)
        u1 = view(arena, 8448, 512)
        z2, m2, e2, m1, e1 = (view(arena, 8960 + 512 * n, 512) for n in range(5))
        tile_i = view(score, 0, S).bitcast(I32)[0:1]
        gathered = [sem_take("gathered") for _ in range(RING)]
        free, ea_in, hid = sem_take("ring_taken"), [sem_take("edge_features") for _ in range(2)], sem_take("hidden_product")
        u_ready, filt = sem_take("hidden_ready"), sem_take("filter_product")
        z_ready, f_sum = sem_take("filter_biased"), sem_take("filter_ready")
        exp1, exp2 = sem_take("hidden_parts"), sem_take("filter_parts")
        load([(tile_i, tiles_dram)])
        with nc.Block() as block:
            pool_gathers(block, table2, D, ring, gathered, free)

            @block.sync
            def _(sp):
                def fetch(par, g):
                    tiles = nc.values_load_multi_w_load_instructions(
                        some(tile_i, g * G, G), engines=(mybir.EngineType.SP,), min_val=0, max_val=T - 1,
                        skip_runtime_bounds_check_because="clamped to the last tile")[1]
                    for j in range(G):
                        h = j // 4
                        sp.dma_start(ea[h * D:(h + 1) * D, par, (j % 4) * P:(j % 4 + 1) * P],
                                     a["ea"][bass.ds(tiles[j], 1), :, :].rearrange("a d e -> (a d) e")).then_inc(ea_in[par], 16)

                fetch(0, 0)
                fetch(1, 1)
                with sp.Fori(1, NG // 2) as r:
                    for par in range(2):
                        sp.wait_ge(hid, (r - 1) * 2 + (par + 1))
                        fetch(par, r * 2 + par)

            def inside(g, lo=0, hi=NG):
                return not isinstance(g, int) or lo <= g < hi

            def run_groups(eng, body):
                for g in range(RING):
                    body(g, 0, g)
                with eng.Fori(1, NG // RING - 1) as r:
                    for slot in range(RING):
                        body(r * RING + slot, r, slot)
                for g in range(NG - RING, NG + 2):
                    body(g, g // RING, g % RING)

            @block.tensor
            def _(pe):
                def body(g, r, slot):
                    if inside(g + 1):
                        pe.wait_ge(ea_in[(slot + 1) % 2], r * (32 * G) + ((slot + 1) // 2 + 1) * (16 * G))
                        nc.tensor.matmul(ps[:, 4 + (slot + 1) % 2, :], We1, ea[:, (slot + 1) % 2, :],
                                         start=True, stop=True).then_inc(hid, 1)
                    if inside(g):
                        pe.wait_ge(u_ready, g + 1)
                        for j in range(G):
                            h = j // 4
                            last = nc.tensor.matmul(ps[:, 6 + h, (j % 4) * D:(j % 4 + 1) * D],
                                                    u1[h * D:(h + 1) * D, (j % 4) * P:(j % 4 + 1) * P],
                                                    We2[h * D:(h + 1) * D, :], start=True, stop=True)
                        last.then_inc(filt, 1)
                    if inside(g - 1):
                        pe.wait_ge(f_sum, (g - 1) * 2 + 2)
                        agg.multiply(pe, (slot + 1) % 2, g - 1,
                                     row=lambda j: some(xa, (g - 1) * G + j, 1).rearrange("p a x -> p (a x)"))

                pe.wait_ge(ea_in[0], 16 * G)
                nc.tensor.matmul(ps[:, 4, :], We1, ea[:, 0, :], start=True, stop=True).then_inc(hid, 1)
                run_groups(pe, body)

            @block.scalar
            def _(act):
                def softplus_parts(z, relu, log, bias, signal, g):
                    nc.scalar.activation(relu, z, ACT.Relu, bias=bias)
                    nc.scalar.activation(log, z, ACT.Abs, bias=bias).then_inc(signal, 1)
                    act.wait_ge(signal, g * 3 + 1)
                    nc.scalar.activation(log, log, ACT.Exp, scale=-1.0).then_inc(signal, 1)
                    act.wait_ge(signal, g * 3 + 2)
                    nc.scalar.activation(log, log, ACT.Ln, bias=1.0).then_inc(signal, 1)

                def hidden(g, slot):
                    act.wait_ge(hid, g + 1)
                    if not isinstance(g, int) or g:
                        act.wait_ge(u_ready, g)
                    softplus_parts(ps[:, 4 + slot % 2, :], m1, e1, be1, exp1, g)

                def body(g, r, slot):
                    if inside(g + 1):
                        hidden(g + 1, slot + 1)
                    if inside(g):
                        act.wait_ge(z_ready, g + 1)
                        softplus_parts(z2, m2, e2, 0.0, exp2, g)

                hidden(0, 0)
                run_groups(act, body)

            @block.vector
            def _(dve):
                def hidden_sum(g):
                    dve.wait_ge(exp1, g * 3 + 3)
                    V.scalar_tensor_tensor(out=u1, in0=m1, scalar=-LOG2, in1=e1, op0=ALU.add, op1=ALU.add).then_inc(u_ready, 1)

                def body(g, r, slot):
                    if inside(g - 1):
                        dve.wait_ge(exp2, (g - 1) * 3 + 3)
                        V.scalar_tensor_tensor(out=m2, in0=m2, scalar=-LOG2, in1=e2, op0=ALU.add, op1=ALU.add).then_inc(f_sum, 1)
                        dve.wait_ge(f_sum, (g - 1) * 2 + 1)
                        dve.wait_ge(gathered[(slot - 1) % RING], (r + 1 if slot else r) * (16 * G))
                        V.tensor_tensor(some(xa, (g - 1) * G, G)[:, :, 0:D], ring[:, (slot - 1) % RING, :, :],
                                        m2.rearrange("p (g d) -> p g d", g=G), ALU.mult).then_inc(f_sum, 1)
                    if inside(g):
                        dve.wait_ge(filt, g + 1)
                        V.tensor_tensor(z2.rearrange("p (b g d) -> p b g d", b=2, d=D),
                                        ps[:, 6:8, 0:4 * D].rearrange("p b (g d) -> p b g d", d=D),
                                        be2.unsqueeze(1).unsqueeze(1).to_broadcast([P, 2, G // 2, D]), ALU.add).then_inc(z_ready, 1)
                    if inside(g - 1):
                        dve.wait_ge(f_sum, (g - 1) * 2 + 2)
                        dve.nop().then_inc(free, 1)
                    if inside(g + 1):
                        hidden_sum(g + 1)
                    if inside(g - 2):
                        agg.add(dve, slot % 2, g - 2, load_blocks(mybir.EngineType.DVE, (g - 2) * G, G))
                    if inside(g):
                        V.tensor_tensor(agg.oh[:, (slot % 2) * G:(slot % 2 + 1) * G, :], lane[:, :].unsqueeze(1).to_broadcast([P, G, P]),
                                        some(dsel, g * G, G).unsqueeze(2).to_broadcast([P, G, P]),
                                        ALU.is_equal).then_inc(agg.ready, 1)

                Vector(dve)[V.memset(xa[:, :, D:X1], 1.0)]
                agg.clear()
                hidden_sum(0)
                run_groups(dve, body)
                agg.total(dve)

        def steps(v, ask):
            v[V.memset(acc[:, :, D:X1], 1.0)]
        on_vector(steps)
        z = view(x_all, 0, KN, X1)
        u = view(x_all, KN * X1, KN, X1)
        w = view(x_all, 2 * KN * X1, KN, D)
        dense([acc], [Wc], z[:, :, 0:D])
        zz, uu = z[:, :, 0:D], u[:, :, 0:D]

        def steps(v, ask):
            ask()
            ask()
            ask()
            ask()
            v[V.memset(u[:, :, D:X1], 1.0)]
            v[V.scalar_tensor_tensor(out=uu, in0=w, scalar=-LOG2, in1=zz, op0=ALU.add, op1=ALU.add)]
        on_vector(steps, [lambda: nc.scalar.activation(w, zz, ACT.Relu), lambda: nc.scalar.activation(zz, zz, ACT.Abs),
                          lambda: nc.scalar.activation(zz, zz, ACT.Exp, scale=-1.0),
                          lambda: nc.scalar.activation(zz, zz, ACT.Ln, bias=1.0)])
        y = node[3]
        dense([u], [Wp], y)

        def steps(v, ask):
            v[V.tensor_tensor(y, y, xw, ALU.add)]
        on_vector(steps)
        layernorm(y, node[4], xw)

        table3, table4 = table("table3", D), table("table4", D)
        state = view(arena, 11375, KN, X1)
        recycle()
        for n, (tab_dram, cur) in enumerate(((table3, xs[:, :, :]), (table4, state))):
            l = f"L2_l{n + 1}_"
            qT, kT = (view(x_all, m * 2 * X1, 2, X1)[0:D] for m in range(2))
            kq = wbuf[0:X1, 0:2 * X1]
            wv = wbuf[0:X1, 2 * X1:2 * X1 + 2 * D]
            ws = wbuf[0:X1, 2 * X1 + 2 * D:2 * X1 + 3 * D]
            load([(qT, a[l + "q"]), (kT, a[l + "k"]), (wv, a[l + "v"]), (ws, a[l + "s"])])
            with nc.Block() as block:
                @block.tensor
                def _(pe):
                    for h in range(2):
                        last = nc.tensor.matmul(ps[0:X1, 0, h * X1:(h + 1) * X1], qT[:, h, :], kT[:, h, :], start=True, stop=True)
                    last.then_inc(from_pe.sem, 1)

                @block.vector
                def _(dve):
                    dve.wait_ge(from_pe.sem, from_pe.base + 1)
                    V.tensor_scalar(kq, ps[0:X1, 0, 0:2 * X1], 0.125, None, ALU.mult)
                    V.tensor_scalar(wv, wv, 0.5, None, ALU.mult)
            from_pe.base += 1
            tab = view(arena, tab_at, KN, 2 * X1)
            dense([cur], [kq], tab)
            if n == 1:
                pass
            store([(rows_of(tab_dram), cur[:, :, 0:D])])
            gather_scores(tab_dram, D, 2, tab, True)
            weight, _ = softmax_numerators(2, False)
            acc = aggregate(2, weight)
            recycle()
            agg = view(x_all, 0, KN, 2 * X1)
            normalise(2, acc, agg, True)
            y = node[4]
            dense([agg[:, :, 0:X1], agg[:, :, X1:2 * X1], cur], [wv[:, 0:D], wv[:, D:2 * D], ws], y)
            if n == 0:
                def steps(v, ask):
                    v[V.memset(state, 1.0)]
                    v[V.tensor_copy(state[:, :, 0:D], y)]
                on_vector(steps)

        def steps(v, ask):
            v[V.tensor_tensor(y, y, xw, ALU.add)]
        on_vector(steps)
        layernorm(y, node[5], xw)

        Wl, Wh, Wm = (wbuf[0:D, n * D:(n + 1) * D] for n in range(3))
        av = wbuf[:, 3 * D:6 * D].rearrange("p (n d) -> p n d", n=3)
        att = wbuf[:, 6 * D:6 * D + 9]
        ew = view(score, 0, S, 2)
        load([(Wl, a["L3_gnn_W_low"]), (Wh, a["L3_gnn_W_high"]), (Wm, a["L3_gnn_W_mlp"]), (ew, ew_dram),
              (att, a["L3_gnn_att_vec"].partition_broadcast(P))]
             + [(av[:, n, :], a[f"L3_gnn_av_{m}"].partition_broadcast(P)) for n, m in enumerate(("low", "high", "mlp"))])
        table5 = table("table5", D)
        store([(rows_of(table5), xw)])
        acc = aggregate(2, ew, gather=table5)
        hs = [node[n] for n in range(3)]
        for m, (of, wm) in enumerate(((acc[:, :, 0:D], Wl), (acc[:, :, X1:X1 + D], Wh), (xw, Wm))):
            dense([of], [wm], hs[m])
        feats = small[:, 0:3 * KN].rearrange("p (n k) -> p n k", n=3)
        logits = small[:, 3 * KN:6 * KN].rearrange("p (n k) -> p n k", n=3)
        extra = view(msg, 0, 2, KN)
        y = node[3]

        def steps(v, ask):
            for m in range(3):
                v[V.tensor_scalar(hs[m], hs[m], 0.0, None, ALU.max)]
                v[V.tensor_tensor(node[4], hs[m], av[:, m:m + 1, :].to_broadcast([P, KN, D]), ALU.mult)]
                v[V.tensor_reduce(feats[:, m, :], node[4], AX, ALU.add)]
            ask()
            for j in range(3):
                v[V.tensor_scalar(logits[:, j, :], feats[:, 0, :], att[:, j:j + 1], None, ALU.mult)]
                for i in range(1, 3):
                    v[V.scalar_tensor_tensor(out=logits[:, j, :], in0=feats[:, i, :], scalar=att[:, 3 * i + j:3 * i + j + 1],
                                             in1=logits[:, j, :], op0=ALU.mult, op1=ALU.add)]
            v[V.tensor_scalar(logits, logits, 1.0 / 3.0, None, ALU.mult)]
            top, tot = extra[:, 0, :], extra[:, 1, :]
            v[V.tensor_tensor(top, logits[:, 0, :], logits[:, 1, :], ALU.max)]
            v[V.tensor_tensor(top, top, logits[:, 2, :], ALU.max)]
            v[V.tensor_tensor(logits, logits, top.unsqueeze(1).to_broadcast([P, 3, KN]), ALU.subtract)]
            ask()
            v[V.tensor_tensor(tot, logits[:, 0, :], logits[:, 1, :], ALU.add)]
            v[V.tensor_tensor(tot, tot, logits[:, 2, :], ALU.add)]
            v[V.reciprocal(tot, tot)]
            v[V.tensor_scalar(tot, tot, 3.0, None, ALU.mult)]
            v[V.tensor_tensor(logits, logits, tot.unsqueeze(1).to_broadcast([P, 3, KN]), ALU.mult)]
            v[V.tensor_copy(y, xw)]
            for m in range(3):
                v[V.tensor_tensor(hs[m], hs[m], logits[:, m, :].unsqueeze(2).to_broadcast([P, KN, D]), ALU.mult)]
                v[V.tensor_tensor(y, y, hs[m], ALU.add)]
        on_vector(steps, [lambda: nc.scalar.activation(feats, feats, ACT.Sigmoid),
                          lambda: nc.scalar.activation(logits, logits, ACT.Exp)])
        layernorm(y, node[4], xw)
        full = N // P
        store([(out[0:full * P, :].rearrange("(k p) d -> p k d", p=P), xs[:, 0:full, 0:D]),
               (out[full * P:N, :], xs[0:N - full * P, full, 0:D])])


def kernel(**inputs):
    import numpy as np
    import concourse.bacc as bacc
    from concourse.bass_utils import run_bass_kernel_spmd

    def padded(x, n, fill=0):
        return np.concatenate([x, np.full((n - len(x),) + x.shape[1:], fill, x.dtype)])

    def tiles(x, fill=0):
        return np.ascontiguousarray(padded(x, EPAD, fill).reshape(T, P).T)

    def biased(w, b):
        return np.ascontiguousarray(np.concatenate([w, b[None]]))

    i = {k: np.asarray(v) for k, v in inputs.items()}
    arrays = {"x": padded(i["x"], NPAD), "src": tiles(i["src"]), "dst": tiles(i["dst"], NPAD - 1)}
    arrays["ea"] = np.ascontiguousarray(padded(i["edge_attr_64"], EPAD).reshape(T, P, D).transpose(0, 2, 1))
    arrays["ew"] = np.ascontiguousarray(np.stack([tiles(i["edge_weight"]), tiles(i["edge_weight_n2"])], 1))
    for k in ("W1", "W2"):
        arrays[f"L0_gnn_{k}"] = i[f"L0_gnn_{k}"]
    for k in ("a1_src", "a1_dst", "a2_src", "a2_dst", "b1", "b2"):
        arrays[f"L0_gnn_{k}"] = i[f"L0_gnn_{k}"].reshape(-1)
    for k, b in (("Wn", "bn"), ("Wc", "bc"), ("Wp", "bp")):
        arrays[f"L1_{k}"] = biased(i[f"L1_gnn_{k}"].T, i[f"L1_gnn_{b}"])
    for k in ("We1", "We2"):
        arrays[f"L1_{k}"] = np.ascontiguousarray(i[f"L1_gnn_{k}"].T)
    for k in ("be1", "be2"):
        arrays[f"L1_gnn_{k}"] = i[f"L1_gnn_{k}"]
    for l in ("l1", "l2"):
        w = {k: biased(i[f"L2_gnn_{l}_w{k}"], i[f"L2_gnn_{l}_b{k}"]) for k in "qkvs"}
        for k in "qk":
            arrays[f"L2_{l}_{k}"] = np.ascontiguousarray(w[k].reshape(X1, 2, D).transpose(2, 1, 0))
        for k in "vs":
            arrays[f"L2_{l}_{k}"] = w[k]
    for k in ("W_low", "W_high", "W_mlp"):
        arrays[f"L3_gnn_{k}"] = i[f"L3_gnn_{k}"]
    for k in ("av_low", "av_high", "av_mlp", "att_vec"):
        arrays[f"L3_gnn_{k}"] = i[f"L3_gnn_{k}"].reshape(-1)

    nc = bacc.Bacc("TRN2", target_bir_lowering=False, num_devices=1)
    arrays = {f"{k}_in": v for k, v in arrays.items()}
    a = {k[:-3]: nc.dram_tensor(k, v.shape, mybir.dt.from_np(v.dtype), kind="ExternalInput").ap()
         for k, v in arrays.items()}
    out = nc.dram_tensor("out", (N, D), F32, kind="ExternalOutput").ap()
    build(nc, a, out)
    r = run_bass_kernel_spmd(nc, [arrays], core_ids=[0])
    return r.results[0]["out"]
```

```python
from contextlib import ExitStack

import concourse.bass as bass
from concourse import mybir

P = 128
N, D, E = 3125, 64, 53125
KN = -(-N // P)
NPAD = KN * P
T = -(-E // P)
T += -T % 8
EPAD = T * P
G = 8
RING = 4
STEPS = T + KN - 1
S = STEPS + -STEPS % (G * RING)
NG = S // G
C = 4
TP, SP = T // C, S // C
X1 = D + 1
U = X1 + 1
PER_BANK = 512 // U
HEADS, HID = 8, 32
BIG = 1e30
LOG2 = 0.6931471805599453
EPS = 1e-5
assert T % C == 0 and S % C == 0 and SP <= P and S <= 512

F32 = mybir.dt.float32
I32 = mybir.dt.int32
ALU = mybir.AluOpType
ACT = mybir.ActivationFunctionType
AX = mybir.AxisListType.X


class Signal:

    def __init__(self, handle):
        self.sem, self.base = handle, 0


def build(nc, a, out):
    with ExitStack() as ctx:
        def sb(name, shape, dt=F32):
            return ctx.enter_context(nc.sbuf_tensor(name, shape, dt))

        def sem(name):
            return ctx.enter_context(nc.semaphore(name))

        ps = ctx.enter_context(nc.psum_tensor("ps", [P, 8, 512], F32))

        xs = sb("xs", [P, KN, X1])
        x_all = sb("x_all", [P, S * X1])
        arena = sb("arena", [P, 12800])
        score = sb("score", [P, S * HEADS])
        dsel = sb("dsel", [P, S])
        src_i = sb("src_i", [P, S], I32)
        step_i = sb("step_i", [2, S], I32)[0:1, :]
        place_i = sb("place_i", [2, S], I32)[0:1, :]
        unsorted = sb("unsorted", [P, 1], I32)
        has_edges = sb("has_edges", [P, KN, 1])
        zeros = sb("zeros", [2, P])[0:1, :]
        ident = sb("ident", [P, P])
        lane = sb("lane", [P, P])
        oh_s = sb("oh_s", [P, G * P])
        msg = sb("msg", [P, 4 * 512])
        idx = sb("idx", [P, RING, G], I32)
        wbuf = sb("wbuf", [P, 456])
        small = sb("small", [P, 6 * KN])

        def view(t, at, *shape):
            n = 1
            for k in shape:
                n *= k
            v = t[:, at:at + n]
            if len(shape) == 2:
                v = v.rearrange("p (a b) -> p a b", b=shape[1])
            if len(shape) == 3:
                v = v.rearrange("p (a b c) -> p a b c", b=shape[1], c=shape[2])
            return v

        xa = view(x_all, 0, S, X1)

        loaded = Signal(sem("loaded"))
        stored = Signal(sem("stored"))
        chain = Signal(sem("vector_chain"))
        to_act = Signal(sem("vector_for_scalar"))
        from_act = Signal(sem("scalar_for_vector"))
        to_pe = Signal(sem("vector_for_tensor"))
        from_pe = Signal(sem("tensor_for_vector"))
        pool_done = Signal(sem("pool_done"))
        turned = Signal(sem("turned"))
        turned_sb = Signal(sem("turned_sb"))
        product = Signal(sem("product"))
        taken = Signal(sem("taken"))

        class Vector:

            def __init__(self, eng):
                self.eng = eng

            def __getitem__(self, ins):
                chain.base += 1
                ins.then_inc(chain.sem, 1)
                self.eng.wait_ge(chain.sem, chain.base)

        def load(pairs):
            with nc.Block() as block:
                @block.sync
                def _(sp):
                    for dst, src in pairs:
                        sp.dma_start(dst, src).then_inc(loaded.sem, 16)
                        loaded.base += 16
                    sp.wait_ge(loaded.sem, loaded.base)

        def store(pairs):
            with nc.Block() as block:
                @block.sync
                def _(sp):
                    for dst, src in pairs:
                        sp.dma_start(dst, src).then_inc(stored.sem, 16)
                        stored.base += 16
                    sp.wait_ge(stored.sem, stored.base)

        def dense(sources, weights, dest):
            tensor, scalar, vector = dense_programs(sources, weights, dest)
            with nc.Block() as block:
                @block.tensor
                def _(pe):
                    tensor(pe)

                @block.scalar
                def _(act):
                    scalar(act)

                @block.vector
                def _(dve):
                    vector(dve)

        def dense_programs(sources, weights, dest):
            K = [s.shape[2] for s in sources]
            M = len(sources)
            width = dest.shape[2]
            blocks = [(i, min(4, KN - i)) for i in range(0, KN, 4)]
            xT = view(x_all, S * X1 - 2 * 3 * 512, 2, 3, 512)
            t0, s0, p0, k0 = turned.base, turned_sb.base, product.base, taken.base

            def tensor(pe):
                def turn(n):
                    i, nj = blocks[n]
                    if n >= 2:
                        pe.wait_ge(turned_sb.sem, s0 + n - 1)
                    for m in range(M):
                        for j in range(nj):
                            last = nc.tensor.transpose(ps[0:K[m], 3 * (n % 2) + m, j * P:(j + 1) * P],
                                                       sources[m][:, i + j, :], ident[:, :])
                    last.then_inc(turned.sem, 1)

                def multiply(n):
                    i, nj = blocks[n]
                    pe.wait_ge(turned_sb.sem, s0 + n + 1)
                    if n >= 1:
                        pe.wait_ge(taken.sem, k0 + n)
                    for j in range(nj):
                        for m in range(M):
                            last = nc.tensor.matmul(
                                ps[:, 6 + j // 2, (j % 2) * 256:(j % 2) * 256 + width],
                                xT[0:K[m], n % 2, m, j * P:(j + 1) * P], weights[m],
                                start=(m == 0), stop=(m == M - 1))
                    last.then_inc(product.sem, 1)

                turn(0)
                for n in range(len(blocks)):
                    if n + 1 < len(blocks):
                        turn(n + 1)
                    multiply(n)

            def scalar(act):
                for n, (i, nj) in enumerate(blocks):
                    act.wait_ge(turned.sem, t0 + n + 1)
                    if n >= 2:
                        act.wait_ge(product.sem, p0 + n - 1)
                    for m in range(M):
                        last = nc.scalar.copy(xT[0:K[m], n % 2, m, 0:nj * P],
                                              ps[0:K[m], 3 * (n % 2) + m, 0:nj * P])
                    last.then_inc(turned_sb.sem, 1)

            def vector(dve):
                for n, (i, nj) in enumerate(blocks):
                    dve.wait_ge(product.sem, p0 + n + 1)
                    for b in range(-(-nj // 2)):
                        c = min(2, nj - 2 * b)
                        got = ps[:, 6 + b, :].rearrange("p (c n) -> p c n", c=2)[:, 0:c, 0:width]
                        last = nc.vector.tensor_copy(dest[:, i + 2 * b:i + 2 * b + c, :], got)
                    last.then_inc(taken.sem, 1)
            turned.base += len(blocks)
            turned_sb.base += len(blocks)
            product.base += len(blocks)
            taken.base += len(blocks)
            return tensor, scalar, vector

        def on_vector(steps, scalar=()):
            with nc.Block() as block:
                count = [0, 0]
                a0, r0 = to_act.base, from_act.base

                @block.vector
                def _(dve):
                    v = Vector(dve)

                    def ask():
                        count[0] += 1
                        dve.nop().then_inc(to_act.sem, 1)
                        dve.wait_ge(from_act.sem, r0 + count[0])

                    steps(v, ask)

                if scalar:
                    @block.scalar
                    def _(act):
                        for n, run in enumerate(scalar):
                            act.wait_ge(to_act.sem, a0 + n + 1)
                            run().then_inc(from_act.sem, 1)
                to_act.base += len(scalar)
                from_act.base += len(scalar)

        V = nc.vector

        def bc(ap, *shape):
            return ap.to_broadcast([ap.shape[0], *shape])

        def layernorm(y, scratch, dest):
            mean, var = small[:, 0:KN], small[:, KN:2 * KN]
            std, inv = small[:, 2 * KN:3 * KN], small[:, 3 * KN:4 * KN]

            def steps(v, ask):
                v[V.tensor_reduce(mean, y, AX, ALU.add)]
                v[V.tensor_scalar(mean, mean, 1.0 / D, None, ALU.mult)]
                v[V.tensor_tensor(y, y, bc(mean.unsqueeze(2), KN, D), ALU.subtract)]
                v[V.tensor_tensor(scratch, y, y, ALU.mult)]
                v[V.tensor_reduce(var, scratch, AX, ALU.add)]
                v[V.tensor_scalar(var, var, 1.0 / D, EPS, ALU.mult, ALU.add)]
                ask()
                v[V.reciprocal(inv, std)]
                v[V.tensor_tensor(dest, y, bc(inv.unsqueeze(2), KN, D), ALU.mult)]

            on_vector(steps, [lambda: nc.scalar.activation(std, var, ACT.Sqrt)])

        RW = D + HEADS
        ring_at, oh_at = 0, RING * G * RW
        ohT_at = oh_at + 2 * G * P
        prod_at = ohT_at + 2 * G * P
        tab_at = prod_at + G * 2 * X1
        OWN_AT = 2 * HEADS * 512

        def pool_gathers(block, table, width, ring, gathered, free):
            @block.gpsimd
            def _(pool):
                staged = sem_take("staged")

                def stage(slot, g):
                    cols = src_i[:, g * G:(g + 1) * G] if isinstance(g, int) else src_i[:, bass.ds(g * G, G)]
                    pool.tensor_copy(idx[:, slot, :], cols).then_inc(staged, 1)

                def group(slot, g, more=True):
                    if not isinstance(g, int) or g >= RING - 1:
                        pool.wait_ge(free, g - (RING - 2))
                    pool.wait_ge(staged, g + 1)
                    if more:
                        stage((slot + 1) % RING, g + 1)
                    for j in range(G):
                        pool.indirect_dma_start(
                            out=ring[:, slot, j, :], out_offset=None, in_=table,
                            in_offset=bass.IndirectOffsetOnAxis(ap=idx[:, slot, j:j + 1], axis=0),
                        ).then_inc(gathered[slot], 16)

                stage(0, 0)
                for slot in range(RING):
                    group(slot, slot)
                with pool.Fori(1, NG // RING - 1) as r:
                    for slot in range(RING):
                        group(slot, r * RING + slot)
                for slot in range(RING):
                    group(slot, NG - RING + slot, more=slot + 1 < RING)

        taken_sems = {}

        def sem_take(name):
            n = taken_sems.get(name, 0)
            taken_sems[name] = n + 1
            taken_now.append(nc.alloc_semaphore(name=f"{name}_{n}"))
            return taken_now[-1]

        taken_now = []

        def recycle():
            nc.clear_and_free_semaphores(taken_now)
            nc.all_engine_barrier()
            taken_now.clear()

        def gather_scores(table, width, H, tab, products, own=None, turned_rows=None, first=None):
            F = H * X1 if products else 2 * H
            ring = view(arena, ring_at, RING * G * width).rearrange("p (r g w) -> p r g w", r=RING, g=G)
            oh = view(arena, oh_at, 2, G, P)
            ohT = view(arena, ohT_at, 2, G * P)
            prod = view(arena, prod_at, G, 2 * X1)
            sc = view(score, 0, S, H)
            gathered = [sem_take("gathered") for _ in range(RING)]
            free = sem_take("ring_taken")
            oh_ready, oh_turned = sem_take("onehot_ready"), sem_take("onehot_turned")
            ohT_ready, given = sem_take("onehotT_ready"), sem_take("dst_rows_ready")
            added, multiplied = sem_take("score_added"), sem_take("dst_rows_multiplied")
            rows_turned = sem_take("rows_turned")

            def row_place(j):
                return ps[:, 4 + j // 2, (j % 2) * 256:(j % 2) * 256 + F] if products else ps[:, 4, j * 16:j * 16 + F]

            with nc.Block() as block:
                pool_gathers(block, table, width, ring, gathered, free)

                @block.scalar
                def _(act):
                    if first is not None:
                        first[1](act)
                    with act.Fori(0, NG // RING) as r:
                        for slot in range(RING):
                            g = r * RING + slot
                            act.wait_ge(oh_turned, g + 1)
                            for b in range(2):
                                last = nc.scalar.copy(ohT[:, slot % 2, b * 512:(b + 1) * 512], ps[:, 2 * (slot % 2) + b, :])
                            last.then_inc(ohT_ready, 1)
                            act.wait_ge(gathered[slot], (r + 1) * (16 * G))
                            if not products:
                                nc.scalar.copy(sc[:, bass.ds(g * G, G), :], ring[:, slot, :, D:D + H])
                            if turned_rows is None:
                                nc.scalar.copy(xa[:, bass.ds(g * G, G), 0:D], ring[:, slot, :, 0:D]).then_inc(free, 1)
                            else:
                                act.wait_ge(rows_turned, g + 1)
                                for h in range(2):
                                    last = nc.scalar.copy(turned_rows[h * D:(h + 1) * D, bass.ds(g * (G // 2), G // 2), :]
                                                          .rearrange("p a e -> p (a e)"), ps[0:D, 6 + h, :])
                                last.then_inc(free, 1)

                @block.tensor
                def _(pe):
                    def await_rows(g, r, slot):
                        pe.wait_ge(gathered[slot], (r + 1) * (16 * G))
                        if not isinstance(g, int) or g:
                            pe.wait_ge(free, g)

                    def turn_rows(slot):
                        for j in range(G):
                            last = nc.tensor.transpose(ps[0:D, 6 + j // 4, (j % 4) * P:(j % 4 + 1) * P],
                                                       ring[:, slot, j, 0:D], ident[:, :])
                        last.then_inc(rows_turned, 1)

                    def turn(par, g):
                        pe.wait_ge(oh_ready, g + 1)
                        for j in range(G):
                            last = nc.tensor.transpose(ps[:, 2 * par + j // 4, (j % 4) * P:(j % 4 + 1) * P],
                                                       oh[:, par, j, :], ident[:, :])
                        last.then_inc(oh_turned, 1)

                    def rows_of_dst(par, g):
                        blocks = load_steps(step_i, mybir.EngineType.PE, g * G, G)
                        pe.wait_ge(ohT_ready, g + 1)
                        if not products:
                            pe.wait_ge(added, g + 1)
                        elif not isinstance(g, int) or g:
                            pe.wait_ge(multiplied, g)
                        for j in range(G):
                            last = nc.tensor.matmul(row_place(j), ohT[:, par, j * P:(j + 1) * P],
                                                    tab[:, bass.ds(blocks[j], 1), :].rearrange("p a f -> p (a f)"),
                                                    start=True, stop=True)
                        last.then_inc(given, 1)

                    def body(g, r, slot):
                        if turned_rows is not None:
                            await_rows(g, r, slot)
                        if not isinstance(g, int) or g + 1 < NG:
                            turn((slot + 1) % 2, g + 1)
                        if turned_rows is not None:
                            turn_rows(slot)
                        rows_of_dst(slot % 2, g)

                    if first is not None:
                        first[0](pe)
                        pe.wait_ge(taken.sem, taken.base)
                    turn(0, 0)
                    for g in range(RING):
                        body(g, 0, g)
                    with pe.Fori(1, NG // RING - 1) as r:
                        for slot in range(RING):
                            body(r * RING + slot, r, slot)
                    for g in range(NG - RING, NG):
                        body(g, g // RING, g % RING)

                @block.vector
                def _(dve):
                    def onehots(par, g):
                        V.tensor_tensor(oh[:, par, :, :], lane[:, :].unsqueeze(1).to_broadcast([P, G, P]),
                                        some(dsel, g * G, G).unsqueeze(2).to_broadcast([P, G, P]),
                                        ALU.is_equal).then_inc(oh_ready, 1)

                    def add_scores(g):
                        dve.wait_ge(given, g + 1)
                        dve.wait_ge(free, g + 1)
                        if products:
                            dve.wait_ge(added, g + 1)
                            for j in range(2):
                                last = V.tensor_tensor(
                                    prod.rearrange("p (b j) (h x) -> p b j h x", j=2, h=H)[:, :, j],
                                    ps[:, 4:8, j * 256:j * 256 + F].rearrange("p b (h x) -> p b h x", h=H),
                                    some(xa, g * G, G).rearrange("p (b j) x -> p b j x", j=2)[:, :, j].unsqueeze(2)
                                    .to_broadcast([P, G // 2, H, X1]), ALU.mult)
                            last.then_inc(multiplied, 1)
                            dve.wait_ge(multiplied, g + 1)
                            V.tensor_reduce(some(sc, g * G, G).rearrange("p g h -> p (g h)"),
                                            prod.rearrange("p g (h x) -> p (g h) x", h=H), AX, ALU.add).then_inc(added, 1)
                        else:
                            at, got = some(sc, g * G, G), ps[:, 4, 0:16 * G].rearrange("p (j f) -> p j f", j=G)
                            V.tensor_tensor(at, at, got[:, :, 0:H], ALU.add)
                            V.tensor_copy(some(own, g * G, G), got[:, :, H:2 * H]).then_inc(added, 1)

                    if first is not None:
                        first[2](dve)
                    if turned_rows is None:
                        V.memset(xa[:, :, D:X1], 1.0)
                    dve.nop().then_inc(added, 1)
                    onehots(0, 0)
                    with dve.Fori(0, NG // RING - 1) as r:
                        for slot in range(RING):
                            onehots((slot + 1) % 2, r * RING + (slot + 1))
                            add_scores(r * RING + slot)
                    for g in range(NG - RING, NG):
                        if g + 1 < NG:
                            onehots((g + 1) % 2, g + 1)
                        add_scores(g)

        def some(t, at, n):
            return t[:, at:at + n] if isinstance(at, int) else t[:, bass.ds(at, n)]

        def load_steps(of, engine, at, n):
            return nc.values_load_multi_w_load_instructions(
                some(of, at, n), engines=(engine,), min_val=0, max_val=KN - 1 if of is step_i else 4 * 512 - U,
                skip_runtime_bounds_check_because="the staircase clamps it to the last block")[1]

        def frame_sums(start, narrow=False):
            for n in range(4 if narrow else -(-KN // 4)):
                last = nc.tensor.matmul(ps[:, n, :], zeros, xs[0:1, 0:8, 0:D], start=start, stop=not start)
            return last

        def take_sums(dest, narrow=False):
            width = dest.shape[2]
            per, stride = (PER_BANK, U) if narrow else (4, P)
            for n in range(-(-KN // per)):
                c = min(per, KN - n * per)
                got = ps[:, n, 0:c * stride].rearrange("p (k x) -> p k x", x=stride)
                V.tensor_copy(dest[:, n * per:n * per + c, :], got[:, :, 0:width])

        def add_step(place, onehot, row):
            at = ps[:, :, :].rearrange("p b n -> p (b n)")
            return nc.tensor.matmul(at[:, bass.ds(place, row.shape[1])], onehot, row, start=False, stop=False)

        def aggregate(H, weight, gather=None, loops=None):
            W, F = (P, X1) if H == 1 else (D, D)
            acc = view(arena, 3584, KN, H * W)
            at = 3584 + KN * H * W
            oh, messages = view(arena, at, 2 * G, P), view(arena, at + 2 * G * P, 2 * G, H * W)
            ready, done = sem_take("messages_ready"), sem_take("batch_multiplied")
            onehot_ready = sem_take("onehots_ready")

            by_pool = gather is None

            def multiply(eng, par, b):
                to = messages[:, par * G:(par + 1) * G, :]
                eng.tensor_tensor(to.rearrange("p b (h x) -> p b h x", h=H)[:, :, :, 0:F],
                                  some(xa, b * G, G)[:, :, 0:F].unsqueeze(2).to_broadcast([P, G, H, F]),
                                  some(weight, b * G, G).unsqueeze(3).to_broadcast([P, G, H, F]),
                                  ALU.mult).then_inc(ready, 1)

            def await_half(eng, b):
                if not isinstance(b, int) or b >= 2:
                    eng.wait_ge(done, b - 1)

            with nc.Block() as block:
                if by_pool:
                    @block.gpsimd
                    def _(pool):
                        pool.wait_ge(onehot_ready, 1)
                        for b in range(2):
                            multiply(pool, b, b)
                        with pool.Fori(1, NG // 2) as r:
                            for par in range(2):
                                await_half(pool, r * 2 + par)
                                multiply(pool, par, r * 2 + par)

                if gather is not None:
                    ring = view(arena, 0, RING * G * D).rearrange("p (r g w) -> p r g w", r=RING, g=G)
                    gathered, free = [sem_take("gathered") for _ in range(RING)], sem_take("ring_taken")
                    pool_gathers(block, gather, D, ring, gathered, free)

                    @block.scalar
                    def _(act):
                        with act.Fori(0, NG // RING) as r:
                            for slot in range(RING):
                                act.wait_ge(gathered[slot], (r + 1) * (16 * G))
                                nc.scalar.copy(xa[:, bass.ds((r * RING + slot) * G, G), 0:D], ring[:, slot, :, :]).then_inc(free, 1)

                @block.tensor
                def _(pe):
                    frame_sums(True)
                    with pe.Fori(0, NG // 2) as r:
                        for par in range(2):
                            b = r * 2 + par
                            blocks = load_steps(step_i, mybir.EngineType.PE, b * G, G)
                            pe.wait_ge(onehot_ready, b + 1)
                            pe.wait_ge(ready, b + 1)
                            for j in range(G):
                                last = add_step(blocks[j] * P,
                                                oh[:, par * G + j, :], messages[:, par * G + j, :])
                            last.then_inc(done, 1)
                    frame_sums(False).then_inc(done, 1)

                @block.vector
                def _(dve):
                    def build(par, b):
                        await_half(dve, b)
                        if loops is not None:
                            V.tensor_copy(messages[:, par * G:(par + 1) * G, X1:X1 + 1], some(loops, b * G, G))
                        V.tensor_tensor(oh[:, par * G:(par + 1) * G, :], lane[:, :].unsqueeze(1).to_broadcast([P, G, P]),
                                        some(dsel, b * G, G).unsqueeze(2).to_broadcast([P, G, P]),
                                        ALU.is_equal).then_inc(onehot_ready, 1)
                        if gather is not None:
                            dve.wait_ge(free, b + 1)
                        if not by_pool:
                            multiply(V, par, b)

                    if H == 1:
                        Vector(dve)[V.memset(messages, 0.0)]
                    for b in range(2):
                        build(b, b)
                    with dve.Fori(1, NG // 2) as r:
                        for par in range(2):
                            build(par, r * 2 + par)
                    dve.wait_ge(done, NG + 1)
                    take_sums(acc)
            return acc

        def aggregate_heads(xT, w1, weight, loops):
            B, F = 4, HEADS * HID
            W = F + 2 * HEADS
            NB = S // B
            acc = view(arena, 3584, KN, W)
            oh = view(oh_s, 0, 2 * B, P)
            messages = view(arena, 3584 + KN * W, 2 * B, W)
            xs_now = view(msg, 0, B, P)
            staged, made = sem_take("rows_staged"), sem_take("hidden_rows_made")
            copied, ready = sem_take("hidden_rows_copied"), sem_take("messages_ready")
            onehot_ready = sem_take("onehots_ready")
            done, summed = sem_take("batch_multiplied"), sem_take("step_summed")

            with nc.Block() as block:
                @block.scalar
                def _(act):
                    def rows(par, b, pair):
                        if not isinstance(b, int) or b >= 2:
                            act.wait_ge(made, b - 1)
                        half = slice(par * D, (par + 1) * D)
                        nc.scalar.copy(xs_now[half].rearrange("p a e -> p (a e)"),
                                       some(xT, pair * B, B)[half].rearrange("p a e -> p (a e)")).then_inc(staged, 1)

                    def hidden_rows(par, b):
                        act.wait_ge(made, b + 1)
                        if not isinstance(b, int) or b >= 2:
                            act.wait_ge(done, b * B - B)
                        to = messages[:, par * B:(par + 1) * B, :]
                        nc.scalar.copy(to[:, :, F:F + HEADS], some(weight, b * B, B))
                        nc.scalar.copy(to[:, :, F + HEADS:W], some(loops, b * B, B))
                        nc.scalar.copy(to[:, :, 0:F], ps[:, 2 * par:2 * par + 2, :]
                                       .rearrange("p b (j f) -> p (b j) f", j=2)).then_inc(copied, 1)

                    def body(par, b, r):
                        if not isinstance(b, int) or b + 2 < NB:
                            rows(par, b + 2, r + 1)
                        if not isinstance(b, int) or b + 1 < NB:
                            hidden_rows(1 - par, b + 1)

                    rows(0, 0, 0)
                    rows(1, 1, 0)
                    hidden_rows(0, 0)
                    for b in range(2):
                        body(b, b, 0)
                    with act.Fori(1, NB // 2 - 1) as r:
                        for par in range(2):
                            body(par, r * 2 + par, r)
                    for b in range(NB - 2, NB):
                        body(b % 2, b, b // 2)

                @block.gpsimd
                def _(pool):
                    with pool.Fori(0, NB // 2) as r:
                        for par in range(2):
                            b = r * 2 + par
                            to = messages[:, par * B:(par + 1) * B, 0:F].rearrange("p b (h c) -> p b h c", h=HEADS)
                            pool.wait_ge(copied, b + 1)
                            pool.tensor_tensor(to, to, some(weight, b * B, B).unsqueeze(3).to_broadcast([P, B, HEADS, HID]),
                                               ALU.mult).then_inc(ready, 1)

                @block.tensor
                def _(pe):
                    def hidden(par, b):
                        pe.wait_ge(staged, b + 1)
                        if not isinstance(b, int) or b >= 2:
                            pe.wait_ge(copied, b - 1)
                        for j in range(B):
                            last = nc.tensor.matmul(ps[:, 2 * par + j // 2, (j % 2) * F:(j % 2 + 1) * F],
                                                    xs_now[par * D:(par + 1) * D, j, :],
                                                    w1[par * D:(par + 1) * D, :], start=True, stop=True)
                        last.then_inc(made, 1)

                    def body(par, b):
                        if not isinstance(b, int) or b + 2 < NB:
                            hidden(par, b + 2)
                        pe.wait_ge(ready, b + 1)
                        pe.wait_ge(onehot_ready, b + 1)
                        for j in range(B):
                            if not isinstance(b, int) or b:
                                pe.wait_ge(summed, b * B + (j + 2 - B))
                            nc.tensor.matmul(ps[:, 4 + j, 0:W], oh[:, par * B + j, :], messages[:, par * B + j, :],
                                             start=True, stop=True).then_inc(done, 1)

                    hidden(0, 0)
                    hidden(1, 1)
                    for b in range(2):
                        body(b, b)
                    with pe.Fori(1, NB // 2 - 1) as r:
                        for par in range(2):
                            body(par, r * 2 + par)
                    for b in range(NB - 2, NB):
                        body(b % 2, b)

                @block.vector
                def _(dve):
                    def build(par, b):
                        V.tensor_tensor(oh[:, par * B:(par + 1) * B, :], lane[:, :].unsqueeze(1).to_broadcast([P, B, P]),
                                        some(dsel, b * B, B).unsqueeze(2).to_broadcast([P, B, P]), ALU.is_equal).then_inc(onehot_ready, 1)

                    def add(b, blocks):
                        for j in range(B):
                            dve.wait_ge(done, b * B + (j + 1))
                            dve.wait_ge(summed, b * B + (j + 1))
                            at = acc[:, bass.ds(blocks[j], 1), :].rearrange("p a w -> p (a w)")
                            V.tensor_tensor(at, at, ps[:, 4 + j, 0:W], ALU.add).then_inc(summed, 1)

                    def body(r, last):
                        blocks = load_steps(step_i, mybir.EngineType.DVE, r * (2 * B), 2 * B)
                        for par in range(2):
                            if par == 0 or not last:
                                build(1 - par, r * 2 + (par + 1))
                            add(r * 2 + par, blocks[par * B:(par + 1) * B])

                    V.memset(acc, 0.0).then_inc(summed, 1)
                    build(0, 0)
                    with dve.Fori(0, NB // 2 - 1) as r:
                        body(r, False)
                    body(NB // 2 - 1, True)
            return acc

        def softmax(H, leaky):
            sc = view(score, 0, S, H)
            scT = view(arena, 0, H, C * P)[0:SP]
            fwd = view(arena, HEADS * 512, H, C * P)[0:SP]
            own = view(arena, OWN_AT, S, H)
            loopT = view(arena, OWN_AT, H, C * P)[0:SP]
            bwd = view(arena, OWN_AT + (HEADS * S if leaky else 0), 2, C * P)[0:SP]
            flag_f, flag_b = view(msg, 0, C * P)[0:SP], view(msg, C * P, C * P)[0:SP]
            in_first, in_last = view(msg, 2 * C * P, C, P)[0:SP], view(msg, 3 * C * P, C, P)[0:SP]
            rows = view(score, 0, 3, S)[0:H]
            tail, head, run, back = (view(score, (3 + n) * S, S)[0:H] for n in range(4))
            valid = view(oh_s, 0, S)
            past = view(oh_s, S, S)
            rows_in = sem_take("rows_in")
            carry = view(small, 0, 2, C * H)[0:SP]
            scores_ready, turned_in = sem_take("scores_ready"), sem_take("scores_turned")
            sT_ready, scanned = sem_take("scoresT_ready"), sem_take("scanned")
            ends_out, chained = sem_take("tile_ends_turned"), sem_take("tiles_chained")
            carry_out, centred = sem_take("carries_turned"), sem_take("centred")
            exped, turned_out = sem_take("exp_done"), sem_take("exp_turned")
            is_first = view(arena, OWN_AT + HEADS * 512, C, P)[0:SP]
            loops = view(arena, 0, S, H)
            summed, sums_out = sem_take("sums_ready"), sem_take("sums_turned")
            carry_taken, own_turned = sem_take("carries_taken"), sem_take("own_turned")
            loop_exped, bwd_done = sem_take("loop_exp_done"), sem_take("scans_merged")
            loop_ready, loop_out, exp_taken = sem_take("loop_ready"), sem_take("loop_turned"), sem_take("exp_taken")

            with nc.Block() as block:
                @block.sync
                def _(sp):
                    for n in range(4):
                        sp.dma_start(msg[0:SP, n * C * P:(n + 1) * C * P], flags_dram[n]).then_inc(rows_in, 16)
                    sp.wait_ge(turned_in, H)
                    sp.dma_start(score[0:H, 0:3 * S], rows_dram[0:H, :]).then_inc(rows_in, 16)

                @block.tensor
                def _(pe):
                    pe.wait_ge(scores_ready, 1)
                    for h in range(H):
                        for c in range(C):
                            last = nc.tensor.transpose(ps[0:SP, h, c * P:(c + 1) * P],
                                                       sc[:, c * SP:(c + 1) * SP, h], ident[:, :])
                        last.then_inc(turned_in, 1)
                    pe.wait_ge(scanned, 1)
                    for n, at in enumerate((P - 1, 0)):
                        for c in range(C):
                            last = nc.tensor.transpose(ps[0:H, n, c * SP:(c + 1) * SP],
                                                       fwd[:, :, c * P + at], ident[0:SP, 0:SP])
                    last.then_inc(ends_out, 1)
                    pe.wait_ge(chained, 1)
                    for n, row in enumerate((run, back)):
                        for c in range(C):
                            last = nc.tensor.transpose(ps[0:SP, n, c * H:(c + 1) * H], row[:, c * SP:(c + 1) * SP],
                                                       ident[0:H, 0:H])
                    last.then_inc(carry_out, 1)
                    if leaky:
                        pe.wait_ge(carry_taken, 1)
                        for h in range(H):
                            for c in range(C):
                                last = nc.tensor.transpose(ps[0:SP, h, c * P:(c + 1) * P],
                                                           own[:, c * SP:(c + 1) * SP, h], ident[:, :])
                        last.then_inc(own_turned, 1)
                    if not leaky:
                        pe.wait_ge(summed, 1)
                        for c in range(C):
                            last = nc.tensor.transpose(ps[0:H, 2, c * SP:(c + 1) * SP],
                                                       fwd[:, :, c * P + P - 1], ident[0:SP, 0:SP])
                        last.then_inc(sums_out, 1)
                        pe.wait_ge(summed, 2)
                        for c in range(C):
                            last = nc.tensor.transpose(ps[0:SP, 3, c * H:(c + 1) * H], run[:, c * SP:(c + 1) * SP], ident[0:H, 0:H])
                        last.then_inc(sums_out, 1)
                        pe.wait_ge(summed, 3)
                        for c in range(C):
                            last = nc.tensor.transpose(ps[0:H, 4, c * SP:(c + 1) * SP],
                                                       bwd[:, :, c * P], ident[0:SP, 0:SP])
                        last.then_inc(sums_out, 1)
                        pe.wait_ge(summed, 4)
                        for c in range(C):
                            last = nc.tensor.transpose(ps[0:SP, 5, c * H:(c + 1) * H], back[:, c * SP:(c + 1) * SP], ident[0:H, 0:H])
                        last.then_inc(sums_out, 1)
                        pe.wait_ge(summed, 5)
                    for h in range(H):
                        pe.wait_ge(exped, h + 1)
                        for c in range(C):
                            last = nc.tensor.transpose(ps[:, h, c * SP:(c + 1) * SP],
                                                       scT[:, h, c * P:(c + 1) * P], ident[0:SP, 0:SP])
                        last.then_inc(turned_out, 1)
                    if leaky:
                        for h in range(H):
                            pe.wait_ge(loop_ready, h + 1)
                            pe.wait_ge(exp_taken, h + 1)
                            for c in range(C):
                                last = nc.tensor.transpose(ps[:, h, c * SP:(c + 1) * SP],
                                                           loopT[:, h, c * P:(c + 1) * P], ident[0:SP, 0:SP])
                            last.then_inc(loop_out, 1)

                @block.scalar
                def _(act):
                    for h in range(H):
                        act.wait_ge(turned_in, h + 1)
                        nc.scalar.copy(scT[:, h, :], ps[0:SP, h, :]).then_inc(sT_ready, 1)
                    for h in range(H):
                        act.wait_ge(centred, h + 1)
                        nc.scalar.activation(scT[:, h, :], scT[:, h, :], ACT.Exp).then_inc(exped, 1)
                        if leaky:
                            nc.scalar.activation(loopT[:, h, :], loopT[:, h, :], ACT.Exp).then_inc(loop_exped, 1)

                @block.vector
                def _(dve):
                    v = Vector(dve)
                    if leaky:
                        v[V.scalar_tensor_tensor(out=sc, in0=sc, scalar=0.2, in1=sc, op0=ALU.mult, op1=ALU.max)]
                    v[V.tensor_scalar(valid, dsel[:, :], 0.0, None, ALU.is_ge)]
                    v[V.tensor_scalar(past, dsel[:, :], float(P), None, ALU.is_ge)]
                    v[V.tensor_tensor(valid, valid, past, ALU.subtract)]
                    v[V.tensor_scalar(valid, valid, -1.0, BIG, ALU.add, ALU.mult)]
                    V.tensor_tensor(sc, sc, valid.unsqueeze(2).to_broadcast([P, S, H]), ALU.add).then_inc(scores_ready, 1)
                    dve.wait_ge(rows_in, 16 * 5)
                    for h in range(H):
                        dve.wait_ge(sT_ready, h + 1)
                        V.tensor_tensor_scan(fwd[:, h, :], flag_f, scT[:, h, :], -BIG, ALU.add, ALU.max)
                        if h >= 2:
                            dve.wait_ge(bwd_done, h - 1)
                        v[V.tensor_tensor_scan(bwd[:, h % 2, ::-1], flag_b[:, ::-1], scT[:, h, ::-1], -BIG, ALU.add, ALU.max)]
                        V.tensor_tensor(fwd[:, h, :], fwd[:, h, :], bwd[:, h % 2, :], ALU.max).then_inc(bwd_done, 1)
                    dve.wait_ge(bwd_done, H)
                    dve.nop().then_inc(scanned, 1)
                    dve.wait_ge(ends_out, 1)
                    v[V.tensor_copy(tail, ps[0:H, 0, 0:S])]
                    v[V.tensor_copy(head, ps[0:H, 1, 0:S])]
                    v[V.tensor_tensor_scan(tail, rows[:, 0, :], tail, -BIG, ALU.add, ALU.max)]
                    v[V.tensor_tensor_scan(head[:, ::-1], rows[:, 2, ::-1], head[:, ::-1], -BIG, ALU.add, ALU.max)]
                    v[V.memset(run[:, 0:1], -BIG)]
                    v[V.memset(back[:, S - 1:S], -BIG)]
                    v[V.tensor_tensor(run[:, 1:S], tail[:, 0:S - 1], rows[:, 1, 1:S], ALU.add)]
                    v[V.tensor_tensor(back[:, 0:S - 1], head[:, 1:S], rows[:, 1, 1:S], ALU.add)]
                    dve.nop().then_inc(chained, 1)
                    dve.wait_ge(carry_out, 1)
                    v[V.tensor_copy(carry, ps[0:SP, 0:2, 0:C * H])]
                    dve.nop().then_inc(carry_taken, 1)
                    for n, mask in enumerate((in_first, in_last)):
                        for h in range(H):
                            for c in range(C):
                                m = fwd[:, h, c * P:(c + 1) * P]
                                last = V.scalar_tensor_tensor(out=m, in0=mask[:, c, :],
                                                              scalar=carry[:, n, c * H + h:c * H + h + 1],
                                                              in1=m, op0=ALU.add, op1=ALU.max)
                        v[last]
                    if leaky:
                        v[V.tensor_scalar(is_first, flag_f.rearrange("p (c e) -> p c e", c=C), 0.0, None, ALU.is_lt)]
                        v[V.tensor_scalar(is_first[:, :, 0], carry[:, 0, :].rearrange("p (c h) -> p c h", h=H)[:, :, 0],
                                          -0.5 * BIG, None, ALU.is_lt)]
                        dve.wait_ge(own_turned, 1)
                        for h in range(H):
                            last = V.tensor_tensor(fwd[:, h, :], fwd[:, h, :], ps[0:SP, h, :], ALU.max)
                        v[last]
                    for h in range(H):
                        if leaky:
                            V.tensor_tensor(loopT[:, h, :], ps[0:SP, h, :], fwd[:, h, :], ALU.subtract)
                        V.tensor_tensor(scT[:, h, :], scT[:, h, :], fwd[:, h, :], ALU.subtract).then_inc(centred, 1)
                    if leaky:
                        for h in range(H):
                            dve.wait_ge(loop_exped, h + 1)
                            V.tensor_tensor(loopT[:, h, :], loopT[:, h, :], is_first.rearrange("p c e -> p (c e)"),
                                            ALU.mult).then_inc(loop_ready, 1)
                    if not leaky:
                        same, into = view(arena, 8192 + 1024, C * P)[0:SP], view(arena, 8192 + 1536, C, P)[0:SP]
                        rows01 = view(score, 7 * S, S)[0:H]
                        dve.wait_ge(exped, H)
                        v[V.tensor_scalar(same, flag_f, 0.0, None, ALU.is_ge)]
                        v[V.tensor_scalar(into, in_first, 0.0, None, ALU.is_ge)]
                        for h in range(H):
                            last = V.tensor_tensor_scan(fwd[:, h, :], same, scT[:, h, :], 0.0, ALU.mult, ALU.add)
                        v[last]
                        dve.nop().then_inc(summed, 1)
                        dve.wait_ge(sums_out, 1)
                        v[V.tensor_copy(tail, ps[0:H, 2, 0:S])]
                        v[V.tensor_scalar(rows01, rows[:, 0, :], 0.0, None, ALU.is_ge)]
                        v[V.tensor_tensor_scan(tail, rows01, tail, 0.0, ALU.mult, ALU.add)]
                        v[V.tensor_scalar(rows01, rows[:, 1, :], 0.0, None, ALU.is_ge)]
                        v[V.memset(run[:, 0:1], 0.0)]
                        v[V.tensor_tensor(run[:, 1:S], tail[:, 0:S - 1], rows01[:, 1:S], ALU.mult)]
                        dve.nop().then_inc(summed, 1)
                        dve.wait_ge(sums_out, 2)
                        v[V.tensor_copy(carry[:, 0, :], ps[0:SP, 3, 0:C * H])]
                        for h in range(H):
                            for c in range(C):
                                m = fwd[:, h, c * P:(c + 1) * P]
                                last = V.scalar_tensor_tensor(out=m, in0=into[:, c, :], scalar=carry[:, 0, c * H + h:c * H + h + 1],
                                                              in1=m, op0=ALU.mult, op1=ALU.add)
                        v[last]
                        for h in range(H):
                            last = V.tensor_tensor_scan(bwd[:, h, ::-1], flag_b[:, ::-1], fwd[:, h, ::-1], -BIG, ALU.add, ALU.max)
                        v[last]
                        dve.nop().then_inc(summed, 1)
                        dve.wait_ge(sums_out, 3)
                        v[V.tensor_copy(head, ps[0:H, 4, 0:S])]
                        v[V.tensor_tensor_scan(head[:, ::-1], rows[:, 2, ::-1], head[:, ::-1], -BIG, ALU.add, ALU.max)]
                        v[V.tensor_tensor(back[:, 0:S - 1], head[:, 1:S], rows[:, 1, 1:S], ALU.add)]
                        dve.nop().then_inc(summed, 1)
                        dve.wait_ge(sums_out, 4)
                        v[V.tensor_copy(carry[:, 1, :], ps[0:SP, 5, 0:C * H])]
                        for h in range(H):
                            for c in range(C):
                                m = bwd[:, h, c * P:(c + 1) * P]
                                last = V.scalar_tensor_tensor(out=m, in0=in_last[:, c, :], scalar=carry[:, 1, c * H + h:c * H + h + 1],
                                                              in1=m, op0=ALU.add, op1=ALU.max)
                        v[last]
                        v[V.tensor_scalar(bwd, bwd, 1e-16, None, ALU.add)]
                        v[V.reciprocal(bwd, bwd)]
                        v[V.tensor_tensor(scT, scT, bwd, ALU.mult)]
                        dve.nop().then_inc(summed, 1)
                    for h in range(H):
                        dve.wait_ge(turned_out, h + 1)
                        V.tensor_copy(sc[:, :, h], ps[:, h, 0:S]).then_inc(exp_taken, 1)
                    if leaky:
                        for h in range(H):
                            dve.wait_ge(loop_out, h + 1)
                            V.tensor_copy(loops[:, :, h], ps[:, h, 0:S])
            return sc, loops

        def add_self_loop(H, sums, den, loop, row, dest, work):
            def steps(v, ask):
                none, tot = view(work, 0, KN, H), view(work, KN * H, KN, H)
                v[V.tensor_tensor(tot, den, loop, ALU.add)]
                v[V.tensor_scalar(none, tot, 0.0, None, ALU.is_equal)]
                if H == 1:
                    v[V.tensor_scalar(has_edges[:, :, :], tot, 0.0, None, ALU.is_gt)]
                v[V.tensor_tensor(none, none, loop, ALU.add)]
                v[V.tensor_tensor(tot, den, none, ALU.add)]
                v[V.tensor_scalar(tot, tot, 1e-16, None, ALU.add)]
                v[V.reciprocal(tot, tot)]
                w = row.shape[2] // H
                sums4, row4, dest4 = (x.rearrange("p k (h c) -> p k h c", h=H) for x in (sums, row, dest))
                v[V.tensor_tensor(row4, row4, none.unsqueeze(3).to_broadcast([P, KN, H, w]), ALU.mult)]
                v[V.tensor_tensor(row4, row4, sums4, ALU.add)]
                v[V.tensor_tensor(dest4, row4, tot.unsqueeze(3).to_broadcast([P, KN, H, w]), ALU.mult)]
            on_vector(steps)

        def order_edges(raw_i, next_i, raw_f, rows, ea_sorted, raw_sorted):
            NB = -(-NPAD // 512)
            oh, node_no, start, work = (view(x_all, n * NPAD, NPAD) for n in range(4))
            at = 4 * NPAD
            ones, before, same, dst_wide = (view(x_all, at + n * P, P) for n in range(4))
            at += 4 * P
            base, within, place = (view(x_all, at + n, 1) for n in range(3))
            idx_i, spare, none, spare_2 = (view(x_all, at + 3 + n, 1).bitcast(I32) for n in range(4))
            places = view(x_all, at + 4 * P + 2 * T, 4 * T).bitcast(I32)
            spare_f = view(x_all, at + 8, 1)
            row, features = view(x_all, at + P, D + 4), view(x_all, at + 2 * P, P)[0:D]
            ew_in = view(x_all, at + 3 * P, 2, T)
            viol = view(x_all, at + 4 * P + 6 * T, T)
            flagged, count_in = sem_take("disorder_found"), sem_take("disorder_summed")
            with nc.Block() as block:
                @block.gpsimd
                def _(pool):
                    pool.iota(node_no, [[1, NPAD]], base=0, channel_multiplier=0, allow_small_or_imprecise_dtypes=True)
                    pool.iota(before, [[-1, P]], base=0, channel_multiplier=1, allow_small_or_imprecise_dtypes=True)

                @block.tensor
                def _(pe):
                    pe.wait_ge(flagged, 1)
                    nc.tensor.matmul(ps[:, 0, 0:1], ones, base, start=True, stop=True).then_inc(count_in, 1)

                @block.vector
                def _(dve):
                    v = Vector(dve)
                    v[V.memset(ones, 1.0)]
                    v[V.tensor_copy(raw_f, raw_i)]
                    v[V.memset(none, 0)]
                    v[V.tensor_copy(viol, next_i)]
                    v[V.tensor_tensor(viol, viol, raw_f[:, 0, :], ALU.is_lt)]
                    v[V.tensor_reduce(base, viol, AX, ALU.add)]
                    dve.nop().then_inc(flagged, 1)
                    dve.wait_ge(count_in, 1)
                    v[V.tensor_scalar(unsorted[:, :], ps[:, 0, 0:1], 1.0, None, ALU.min)]

            def if_unsorted(eng):
                return eng.If(eng.value_load(unsorted[0:1, :], min_val=0, max_val=1) > 0)

            oh_ready, counted = sem_take("onehots_ready"), sem_take("edges_counted")
            tile_ready, tile_done = sem_take("tile_ready"), sem_take("tile_counted")
            ea_in, row_ready = sem_take("features_in"), sem_take("row_ready")
            index_ready, scattered, row_free = sem_take("index_ready"), sem_take("rows_scattered"), sem_take("row_free")
            with nc.Block() as block:
                @block.sync
                def _(sp):
                    with if_unsorted(sp):
                        sp.dma_start(ew_in, a["ew"]).then_inc(ea_in, 16)
                        with sp.Fori(0, T) as t:
                            sp.wait_ge(tile_done, t + 1)
                            sp.dma_start(features, a["ea"][bass.ds(t, 1), :, :].rearrange("a d e -> (a d) e")).then_inc(ea_in, 16)

                @block.tensor
                def _(pe):
                    def by_bank(start, stop):
                        for n in range(NB):
                            w = min(512, NPAD - n * 512)
                            last = nc.tensor.matmul(ps[:, n, 0:w], ones, oh[:, n * 512:n * 512 + w], start=start, stop=stop)
                        return last

                    with if_unsorted(pe):
                        for n in range(NB):
                            nc.tensor.matmul(ps[:, n, :], zeros, xs[0:1, 0:8, 0:D], start=True, stop=False)
                        with pe.Fori(0, T) as t:
                            pe.wait_ge(oh_ready, t + 1)
                            by_bank(False, False).then_inc(counted, 1)
                        for n in range(NB):
                            last = nc.tensor.matmul(ps[:, n, :], zeros, xs[0:1, 0:8, 0:D], start=False, stop=True)
                        last.then_inc(counted, 1)
                        with pe.Fori(0, T) as t:
                            pe.wait_ge(ea_in, t * 16 + 32)
                            pe.wait_ge(tile_ready, t + 1)
                            by_bank(True, True)
                            nc.tensor.matmul(ps[:, NB, 0:P], dst_wide, ident[:, :], start=True, stop=True)
                            nc.tensor.transpose(ps[:, NB, P:P + D], features, ident[0:D, 0:D]).then_inc(tile_done, 1)

                @block.gpsimd
                def _(pool):
                    with if_unsorted(pool):
                        with pool.Fori(0, T) as t:
                            pool.wait_ge(row_ready, t + 1)
                            pool.tensor_tensor(idx_i, some(places, t * 4, 1), none, ALU.add).then_inc(index_ready, 1)
                            pool.wait_ge(index_ready, t + 1)
                            pool.tensor_tensor(spare, some(places, t * 4 + 1, 1), none, ALU.add)
                            pool.indirect_dma_start(out=rows, out_offset=bass.IndirectOffsetOnAxis(ap=idx_i, axis=0),
                                                    in_=row, in_offset=None).then_inc(scattered, 16)
                            pool.wait_ge(scattered, t * 16 + 16)
                            pool.tensor_tensor(spare_2, some(places, t * 4 + 2, 1), none, ALU.add).then_inc(row_free, 1)

                @block.vector
                def _(dve):
                    v = Vector(dve)

                    def onehots(t):
                        return V.tensor_tensor(oh, node_no, some(raw_f[:, 0, :], t, 1).to_broadcast([P, NPAD]), ALU.is_equal)

                    link = sem_take("tile_chain")
                    LINKS = 12

                    with if_unsorted(dve):
                        dve.nop().then_inc(counted, 1)
                        dve.nop().then_inc(tile_done, 1)
                        dve.nop().then_inc(row_free, 1)
                        with dve.Fori(0, T) as t:
                            dve.wait_ge(counted, t + 1)
                            onehots(t).then_inc(oh_ready, 1)
                        dve.wait_ge(counted, T + 2)
                        V.tensor_scalar(before, before, 0.0, None, ALU.is_gt).then_inc(link, 1)
                        V.memset(oh, 1.0).then_inc(link, 1)
                        for n in range(NB):
                            w = min(512, NPAD - n * 512)
                            V.tensor_copy(work[:, n * 512:n * 512 + w], ps[:, n, 0:w]).then_inc(link, 1)
                        dve.wait_ge(link, NB + 2)
                        V.tensor_tensor_scan(start, oh, work, 0.0, ALU.mult, ALU.add).then_inc(link, 1)
                        dve.wait_ge(link, NB + 3)
                        V.tensor_tensor(start, start, work, ALU.subtract).then_inc(link, 1)
                        first = NB + 4
                        dve.wait_ge(link, first)
                        with dve.Fori(0, T) as t:
                            def then(n, ins):
                                ins.then_inc(link, 1)
                                dve.wait_ge(link, t * LINKS + (first + n))

                            then(1, V.tensor_copy(dst_wide, some(raw_f[:, 0, :], t, 1).to_broadcast([P, P])))
                            then(2, onehots(t))
                            dve.nop().then_inc(tile_ready, 1)
                            then(3, V.tensor_tensor(work, oh, start, ALU.mult))
                            then(4, V.tensor_reduce(base, work, AX, ALU.add))
                            dve.wait_ge(tile_done, t + 2)
                            then(5, V.tensor_tensor(same, ps[:, NB, 0:P], dst_wide, ALU.is_equal))
                            then(6, V.tensor_tensor(same, same, before, ALU.mult))
                            then(7, V.tensor_reduce(within, same, AX, ALU.add))
                            dve.wait_ge(row_free, t + 1)
                            then(8, V.tensor_tensor(base, base, within, ALU.add))
                            V.tensor_copy(some(places, t * 4, 3), base.to_broadcast([P, 3]))
                            V.tensor_copy(row[:, 0:D], ps[:, NB, P:P + D])
                            V.tensor_copy(row[:, D:D + 2], some(raw_f.rearrange("p b t -> p t b"), t, 1).rearrange("p t b -> p (t b)"))
                            then(9, V.tensor_copy(row[:, D + 2:D + 4], some(ew_in.rearrange("p b t -> p t b"), t, 1).rearrange("p t b -> p (t b)")))
                            dve.nop().then_inc(row_ready, 1)
                            full = NPAD // 512
                            then(10, V.tensor_tensor(start[:, 0:full * 512], start[:, 0:full * 512],
                                                     ps[:, 0:full, :].rearrange("p b n -> p (b n)"), ALU.add))
                            then(11, V.tensor_tensor(start[:, full * 512:], start[:, full * 512:],
                                                     ps[:, full, 0:NPAD - full * 512], ALU.add))
                            then(12, V.memset(spare_f, 0.0))
                        dve.wait_ge(row_free, T + 1)

            row_in, turned_out = sem_take("sorted_row_in"), sem_take("sorted_features_turned")
            features_ready, written = sem_take("sorted_features_ready"), sem_take("sorted_features_written")
            with nc.Block() as block:
                @block.sync
                def _(sp):
                    with if_unsorted(sp):
                        def turn_tile(t, rows_of_tile, tile):
                            sp.dma_start(row, rows_of_tile).then_inc(row_in, 16)
                            sp.wait_ge(features_ready, t + 1)
                            sp.dma_start(tile.rearrange("a d e -> (a d) e"), features).then_inc(written, 16)

                        turn_tile(0, rows[0:P, :], ea_sorted[0:1, :, :])
                        with sp.Fori(1, T) as t:
                            sp.wait_ge(written, t * 16)
                            turn_tile(t, rows[bass.ds(t * P, P), :], ea_sorted[bass.ds(t, 1), :, :])
                        sp.wait_ge(written, 16 * T)
                        sp.dma_start(raw_sorted, rows.rearrange("(t p) f -> p t f", p=P)[:, :, D:D + 4]).then_inc(row_in, 16)
                        sp.wait_ge(row_in, 16 * T + 16)

                @block.tensor
                def _(pe):
                    with if_unsorted(pe):
                        with pe.Fori(0, T) as t:
                            pe.wait_ge(row_in, t * 16 + 16)
                            nc.tensor.matmul(ps[:, 1, 0:P], ident[:, :], ident[:, :], start=True, stop=True)
                            nc.tensor.transpose(ps[0:D, 0, 0:P], row[:, 0:D], ident[:, :]).then_inc(turned_out, 1)

                @block.vector
                def _(dve):
                    with if_unsorted(dve):
                        with dve.Fori(0, T) as t:
                            dve.wait_ge(turned_out, t + 1)
                            V.tensor_copy(features, ps[0:D, 0, 0:P]).then_inc(features_ready, 1)
                        dve.wait_ge(row_in, 16 * T + 16)
                        V.tensor_copy(raw_f.rearrange("p b t -> p t b"), raw_sorted[:, :, 0:2])
            recycle()

        raw_i = view(msg, 0, 2, T).bitcast(I32)
        next_i = view(msg, 2 * T, T).bitcast(I32)

        def steps(v, ask):
            v[V.memset(next_i, NPAD)]
        on_vector(steps)
        load([(xs[:, :, 0:D], a["x"].rearrange("(k p) d -> p k d", p=P)),
              (raw_i[:, 0, :], a["dst"]), (raw_i[:, 1, :], a["src"]),
              (next_i[0:P - 1, :], a["dst"][1:P, :]), (next_i[P - 1:P, 0:T - 1], a["dst"][0:1, 1:T])])

        s_idx = view(arena, 0, S)
        t_idx = view(arena, 448, C)
        k_edge = view(arena, 460, KN)
        with nc.Block() as block:
            @block.gpsimd
            def _(pool):
                pool.memset(ident[:, :], 0.0).then_inc(pool_done.sem, 1)
                pool.wait_ge(pool_done.sem, pool_done.base + 1)
                pool.affine_select(out=ident[:, :], in_=ident[:, :], compare_op=ALU.not_equal, fill=1.0, base=0,
                                   pattern=[[-1, P]], channel_multiplier=1)
                pool.iota(lane[:, :], [[1, P]], base=0, channel_multiplier=0, allow_small_or_imprecise_dtypes=True)
                pool.iota(s_idx, [[1, S]], base=0, channel_multiplier=0, allow_small_or_imprecise_dtypes=True)
                pool.iota(t_idx, [[TP, C]], base=0, channel_multiplier=1, allow_small_or_imprecise_dtypes=True)
                pool.iota(k_edge, [[P, KN]], base=0, channel_multiplier=0, allow_small_or_imprecise_dtypes=True)

            @block.vector
            def _(dve):
                V.memset(zeros, 0.0)
                V.memset(xs[:, :, D:X1], 1.0)
        pool_done.base += 1

        flags_dram = nc.dram_tensor("flags", (4, SP, C * P), F32).ap()
        rows_dram = nc.dram_tensor("rows", (HEADS, 3 * S), F32).ap()
        sel_dram = nc.dram_tensor("tile_of_steps", (P, S), F32).ap()
        raw_f = view(arena, 512, 2, T)
        sorted_rows = nc.dram_tensor("sorted_rows", (EPAD, D + 4), F32).ap()
        sorted_ea = nc.dram_tensor("sorted_edge_features", (T, D, P), F32).ap()
        sorted_raw = view(x_all, 20000, T, 4)
        order_edges(raw_i, next_i, raw_f, sorted_rows, sorted_ea, sorted_raw)
        rawT = view(x_all, 0, 2 * C, P)[0:TP]
        wide = view(x_all, 1100, C, S)[0:TP]
        ones = view(x_all, 3000, P)
        tile_of = view(x_all, 3200, S)
        block_of = view(x_all, 3700, S)
        ge = view(x_all, 4200, C, KN)[0:TP]
        end = view(x_all, 4400, C)[0:TP]
        key, valid = view(x_all, 4500, S), view(x_all, 5000, S)
        keyT = view(x_all, 5500, C, P)[0:SP]
        flags = view(x_all, 6100, 4, C * P)[0:SP]
        first_row, last_row = view(x_all, 8200, S)[0:HEADS], view(x_all, 8700, S)[0:HEADS]
        cont = view(x_all, 9200, S + 1)[0:HEADS]
        rows = view(x_all, 9700, 3, S)[0:HEADS]
        ends = view(x_all, 11100, 2, HEADS)
        place, bank = view(x_all, 16500, S)[0:1], view(x_all, 17000, S)[0:1]
        with nc.Block() as block:
            @block.vector
            def _(dve):
                v = Vector(dve)
                v[V.memset(ones, 1.0)]
                v[V.tensor_copy(ends[:, 0, :], ident[:, 0:1].to_broadcast([P, HEADS]))]
                v[V.tensor_copy(ends[:, 1, :], ident[:, P - 1:P].to_broadcast([P, HEADS]))]
                dve.nop().then_inc(to_pe.sem, 1)
                dve.wait_ge(from_pe.sem, from_pe.base + 1)
                v[V.tensor_copy(rawT.rearrange("p (b c) e -> p b (c e)", b=2), ps[0:TP, 0:2, :])]
                dstT = rawT[:, 0:C, :]
                v[V.tensor_tensor(ge, dstT[:, :, P - 1:P].to_broadcast([TP, C, KN]),
                                  k_edge[0:TP].unsqueeze(1).to_broadcast([TP, C, KN]), ALU.is_ge)]
                v[V.tensor_reduce(end, ge, AX, ALU.add)]
                v[V.scalar_tensor_tensor(out=end, in0=end, scalar=-1.0, in1=t_idx[0:TP], op0=ALU.add, op1=ALU.add)]
                for c in range(C):
                    v[V.tensor_scalar(wide[:, c, :], s_idx[0:TP], end[:, c:c + 1], None, ALU.is_gt)]
                dve.nop().then_inc(to_pe.sem, 1)
                dve.wait_ge(from_pe.sem, from_pe.base + 2)
                v[V.tensor_copy(tile_of, ps[:, 2, 0:S])]
                v[V.tensor_tensor(block_of, s_idx, tile_of, ALU.subtract)]
                v[V.tensor_scalar(block_of, block_of, float(KN - 1), 0.0, ALU.min, ALU.max)]
                v[V.tensor_copy(step_i, block_of[0:1, :])]
                v[V.tensor_scalar(place, block_of[0:1, :], float(U), None, ALU.mult)]
                for n in range(1, 4):
                    v[V.tensor_scalar(bank, block_of[0:1, :], float(n * PER_BANK), float(512 - PER_BANK * U), ALU.is_ge, ALU.mult)]
                    v[V.tensor_tensor(place, place, bank, ALU.add)]
                v[V.tensor_copy(place_i, place)]
                for c in range(C):
                    v[V.tensor_scalar(wide[:, c, :], tile_of[0:TP], t_idx[0:TP, c:c + 1], None, ALU.is_equal)]
                dve.nop().then_inc(to_pe.sem, 1)
                dve.wait_ge(from_pe.sem, from_pe.base + 3)
                v[V.tensor_copy(src_i[:, :], ps[:, 4, 0:S])]
                v[V.scalar_tensor_tensor(out=dsel[:, :], in0=block_of, scalar=-float(P), in1=ps[:, 3, 0:S],
                                         op0=ALU.mult, op1=ALU.add)]
                v[V.tensor_scalar(valid, dsel[:, :], 0.0, None, ALU.is_ge)]
                v[V.tensor_scalar(key, dsel[:, :], float(P), None, ALU.is_ge)]
                v[V.tensor_tensor(valid, valid, key, ALU.subtract)]
                v[V.scalar_tensor_tensor(out=key, in0=ps[:, 3, 0:S], scalar=1.0, in1=valid, op0=ALU.add, op1=ALU.mult)]
                dve.nop().then_inc(to_pe.sem, 1)
                dve.wait_ge(from_pe.sem, from_pe.base + 4)
                v[V.tensor_copy(keyT.rearrange("p c e -> p (c e)"), ps[0:SP, 5, :])]
                ff, fb, inf, inl = (flags[:, n, :].rearrange("p (c e) -> p c e", c=C) for n in range(4))
                v[V.memset(flags[:, 0:2, :], 0.0)]
                v[V.tensor_tensor(ff[:, :, 1:P], keyT[:, :, 1:P], keyT[:, :, 0:P - 1], ALU.is_equal)]
                v[V.tensor_copy(fb[:, :, 0:P - 1], ff[:, :, 1:P])]
                v[V.tensor_tensor(inf, keyT, keyT[:, :, 0:1].to_broadcast([SP, C, P]), ALU.is_equal)]
                v[V.tensor_tensor(inl, keyT, keyT[:, :, P - 1:P].to_broadcast([SP, C, P]), ALU.is_equal)]
                v[V.tensor_scalar(flags, flags, -1.0, BIG, ALU.add, ALU.mult)]
                v[V.tensor_copy(first_row, ps[0:HEADS, 6, 0:S])]
                v[V.tensor_copy(last_row, ps[0:HEADS, 7, 0:S])]
                v[V.memset(cont, 0.0)]
                v[V.tensor_tensor(cont[:, 1:S], first_row[:, 1:S], last_row[:, 0:S - 1], ALU.is_equal)]
                v[V.tensor_tensor(first_row, first_row, last_row, ALU.is_equal)]
                v[V.tensor_tensor(rows[:, 0, :], first_row, cont[:, 0:S], ALU.mult)]
                v[V.tensor_copy(rows[:, 1, :], cont[:, 0:S])]
                v[V.tensor_tensor(rows[:, 2, :], first_row, cont[:, 1:S + 1], ALU.mult)]
                v[V.tensor_scalar(rows, rows, -1.0, BIG, ALU.add, ALU.mult)]

            @block.tensor
            def _(pe):
                pe.wait_ge(to_pe.sem, to_pe.base + 1)
                for b in range(2):
                    for c in range(C):
                        last = nc.tensor.transpose(ps[0:TP, b, c * P:(c + 1) * P], raw_f[:, b, c * TP:(c + 1) * TP], ident[:, :])
                last.then_inc(from_pe.sem, 1)
                pe.wait_ge(to_pe.sem, to_pe.base + 2)
                for c in range(C):
                    last = nc.tensor.matmul(ps[:, 2, 0:S], ones[0:TP, :], wide[:, c, :], start=(c == 0), stop=(c == C - 1))
                last.then_inc(from_pe.sem, 1)
                pe.wait_ge(to_pe.sem, to_pe.base + 3)
                for b in range(2):
                    for c in range(C):
                        last = nc.tensor.matmul(ps[:, 3 + b, 0:S], rawT[:, b * C + c, :], wide[:, c, :],
                                                start=(c == 0), stop=(c == C - 1))
                last.then_inc(from_pe.sem, 1)
                pe.wait_ge(to_pe.sem, to_pe.base + 4)
                for c in range(C):
                    nc.tensor.transpose(ps[0:SP, 5, c * P:(c + 1) * P], key[:, c * SP:(c + 1) * SP], ident[:, :])
                for n in range(2):
                    last = nc.tensor.matmul(ps[0:HEADS, 6 + n, 0:S], ends[:, n, :], key, start=True, stop=True)
                last.then_inc(from_pe.sem, 1)
        to_pe.base += 4
        from_pe.base += 4
        tiles_dram = nc.dram_tensor("tiles", (1, S), I32).ap()
        tiles_i = view(x_all, 12000, S).bitcast(I32)

        def steps(v, ask):
            v[V.tensor_scalar(tile_of, tile_of, float(T - 1), None, ALU.min)]
            v[V.tensor_copy(tiles_i, tile_of)]
        store([(flags_dram[n], flags[:, n, :]) for n in range(4)]
              + [(rows_dram, rows.rearrange("p n s -> p (n s)")), (sel_dram, tile_of)])
        on_vector(steps)
        store([(tiles_dram, tiles_i[0:1, :])])

        ew_dram = nc.dram_tensor("ew_by_step", (P, S, 2), F32).ap()
        ew_raw, ewT = view(x_all, 13000, 2, T), view(x_all, 14000, 2 * C, P)[0:TP]
        ew_step = view(x_all, 15100, S, 2)
        load([(ew_raw, a["ew"])])
        with nc.Block() as block:
            @block.vector
            def _(dve):
                with dve.If(dve.value_load(unsorted[0:1, :], min_val=0, max_val=1) > 0):
                    V.tensor_copy(ew_raw.rearrange("p h t -> p t h"), sorted_raw[:, :, 2:4])
        with nc.Block() as block:
            @block.tensor
            def _(pe):
                for b in range(2):
                    for c in range(C):
                        last = nc.tensor.transpose(ps[0:TP, b, c * P:(c + 1) * P], ew_raw[:, b, c * TP:(c + 1) * TP], ident[:, :])
                last.then_inc(from_pe.sem, 1)
                pe.wait_ge(to_pe.sem, to_pe.base + 1)
                for b in range(2):
                    for c in range(C):
                        last = nc.tensor.matmul(ps[:, 2 + b, 0:S], ewT[:, b * C + c, :], wide[:, c, :],
                                                start=(c == 0), stop=(c == C - 1))
                last.then_inc(from_pe.sem, 1)

            @block.vector
            def _(dve):
                dve.wait_ge(from_pe.sem, from_pe.base + 1)
                V.tensor_copy(ewT.rearrange("p (b c) e -> p b (c e)", b=2), ps[0:TP, 0:2, :]).then_inc(to_pe.sem, 1)
                dve.wait_ge(from_pe.sem, from_pe.base + 2)
                V.tensor_copy(ew_step.rearrange("p s h -> p h s"), ps[:, 2:4, 0:S])
        to_pe.base += 1
        from_pe.base += 2
        store([(ew_dram, ew_step)])

        def table(name, width):
            return nc.dram_tensor(name, (NPAD, width), F32).ap()

        def rows_of(t):
            return t.rearrange("(k p) d -> p k d", p=P)

        xw = xs[:, :, 0:D]
        node = [view(x_all, n * KN * D, KN, D) for n in range(8)]

        W1both = wbuf[:, 0:256]
        W1 = W1both[0:D]
        V1 = view(x_all, 1280, 16)[0:D]
        att1 = view(x_all, 0, 2, 256)[0:D]
        t1 = view(x_all, 512, 2, 256)[0:D]
        load([(W1, a["L0_gnn_W1"]), (W1both[D:P], a["L0_gnn_W1"]),
              (att1[:, 0, :], a["L0_gnn_a1_src"].partition_broadcast(D)),
              (att1[:, 1, :], a["L0_gnn_a1_dst"].partition_broadcast(D))])

        def steps(v, ask):
            v[V.tensor_tensor(t1, att1, W1.unsqueeze(1).to_broadcast([D, 2, 256]), ALU.mult)]
            v[V.tensor_reduce(V1, t1.rearrange("p a (h c) -> p (a h) c", c=HID), AX, ALU.add)]
        on_vector(steps)
        al = view(x_all, 8000, KN, 16)
        dense([xw], [V1], al)
        row0 = view(x_all, 2000, KN, RW)
        tab_al = view(arena, tab_at, KN, 2 * HEADS)
        tab_own = tab_al[:, :, HEADS:2 * HEADS]

        def steps(v, ask):
            v[V.tensor_copy(row0[:, :, 0:D], xw)]
            v[V.tensor_copy(row0[:, :, D:RW], al[:, :, 0:HEADS])]
            v[V.tensor_copy(tab_al[:, :, 0:HEADS], al[:, :, HEADS:16])]
            v[V.tensor_tensor(tab_own, al[:, :, 0:HEADS], al[:, :, HEADS:16], ALU.add)]
            v[V.scalar_tensor_tensor(out=tab_own, in0=tab_own, scalar=0.2, in1=tab_own, op0=ALU.mult, op1=ALU.max)]
        on_vector(steps)
        table0 = table("table0", RW)
        store([(rows_of(table0), row0)])
        xT = view(x_all, 0, S // 2, P)
        gather_scores(table0, RW, HEADS, tab_al, False, view(arena, OWN_AT, S, HEADS), xT)
        weight, loops = softmax(HEADS, True)
        acc = aggregate_heads(xT, W1both, weight, loops)
        F = HEADS * HID
        h_self, h1 = view(x_all, 0, KN, F), view(x_all, KN * F, KN, F)
        dense([xw], [W1], h_self)
        add_self_loop(HEADS, acc[:, :, 0:F], acc[:, :, F:F + HEADS], acc[:, :, F + HEADS:F + 2 * HEADS], h_self, h1, msg)
        W2a = view(arena, 6700, 2, D + 2)
        b1 = view(arena, 7000, 256)
        att2 = view(arena, 7300, 2, D)
        t2 = view(arena, 7500, 2, 2 * D)
        b2 = view(arena, 7800, D)
        load([(W2a[:, :, 0:D], a["L0_gnn_W2"].rearrange("(m p) c -> p m c", p=P)),
              (b1, a["L0_gnn_b1"].partition_broadcast(P)), (b2, a["L0_gnn_b2"].partition_broadcast(P)),
              (att2[:, 0, :], a["L0_gnn_a2_src"].partition_broadcast(P)),
              (att2[:, 1, :], a["L0_gnn_a2_dst"].partition_broadcast(P))])

        def steps(v, ask):
            for n in range(2):
                v[V.tensor_tensor(t2[:, n, :].rearrange("p (m c) -> p m c", m=2), W2a[:, :, 0:D],
                                  att2[:, n:n + 1, :].to_broadcast([P, 2, D]), ALU.mult)]
                v[V.tensor_reduce(W2a[:, :, D + n], t2[:, n, :].rearrange("p (m c) -> p m c", m=2), AX, ALU.add)]
        on_vector(steps)
        neg = view(x_all, 0, KN, 256)

        def steps(v, ask):
            v[V.tensor_tensor(h1, h1, b1.unsqueeze(1).to_broadcast([P, KN, 256]), ALU.add)]
            v[V.tensor_scalar(neg, h1, 0.0, None, ALU.min)]
            ask()
            v[V.tensor_scalar(h1, h1, 0.0, -1.0, ALU.max, ALU.add)]
            v[V.tensor_tensor(h1, h1, neg, ALU.add)]
        on_vector(steps, [lambda: nc.scalar.activation(neg, neg, ACT.Exp)])
        h2 = view(x_all, 0, KN, D + 2)
        dense([h1[:, :, 0:P], h1[:, :, P:256]], [W2a[:, 0, :], W2a[:, 1, :]], h2)
        row1 = view(x_all, 2000, KN, X1)
        b2_keep = wbuf[:, 0:D]
        tab1 = view(arena, tab_at, KN, 2)
        tab1_own = tab1[:, :, 1:2]

        def steps(v, ask):
            v[V.tensor_copy(row1, h2[:, :, 0:X1])]
            v[V.tensor_copy(b2_keep, b2)]
            v[V.tensor_copy(tab1[:, :, 0:1], h2[:, :, X1:X1 + 1])]
            v[V.tensor_tensor(tab1_own, h2[:, :, D:X1], h2[:, :, X1:X1 + 1], ALU.add)]
            v[V.scalar_tensor_tensor(out=tab1_own, in0=tab1_own, scalar=0.2, in1=tab1_own, op0=ALU.mult, op1=ALU.max)]
        on_vector(steps)
        table1 = table("table1", X1)
        store([(rows_of(table1), row1)])
        recycle()
        gather_scores(table1, X1, 1, tab1, False, view(arena, OWN_AT, S, 1))
        weight, loops = softmax(1, True)
        acc = aggregate(1, weight, loops=loops)
        row1 = view(x_all, 4000, KN, X1)
        load([(row1, rows_of(table1))])
        y = node[0]
        add_self_loop(1, acc[:, :, 0:D], acc[:, :, D:X1], acc[:, :, X1:X1 + 1], row1[:, :, 0:D], y, msg)

        def steps(v, ask):
            v[V.tensor_tensor(y, y, b2_keep.unsqueeze(1).to_broadcast([P, KN, D]), ALU.add)]
            v[V.tensor_tensor(y, y, xw, ALU.add)]
        on_vector(steps)
        layernorm(y, node[1], xw)

        Wn, Wc, Wp = (wbuf[0:X1, n * D:(n + 1) * D] for n in range(3))
        be2 = wbuf[:, 3 * D:4 * D]
        We2 = wbuf[:, 4 * D:5 * D]
        We1 = wbuf[:, 5 * D:7 * D]
        be1 = wbuf[:, 7 * D:7 * D + 1]

        def steps(v, ask):
            v[V.memset(We1, 0.0)]
            v[V.memset(wbuf[:, 7 * D + 1:7 * D + 2], 0.5)]
        on_vector(steps)
        load([(Wn, a["L1_Wn"]), (Wc, a["L1_Wc"]), (Wp, a["L1_Wp"]), (be2, a["L1_gnn_be2"].partition_broadcast(P))]
             + [pair for h in range(2) for pair in (
                 (We2[h * D:(h + 1) * D, :], a["L1_We2"]), (We1[h * D:(h + 1) * D, h * D:(h + 1) * D], a["L1_We1"]),
                 (be1[h * D:(h + 1) * D, :], a["L1_gnn_be1"].rearrange("(d o) -> d o", o=1)))])
        hn = node[0]
        dense([xs[:, :, :]], [Wn], hn)
        table2 = table("table2", D)
        store([(rows_of(table2), hn)])

        recycle()
        onehots = view(arena, 3328, 2 * G, P)
        acc = view(arena, 0, KN, X1)
        onehot_ready, done = sem_take("onehots_ready"), sem_take("group_multiplied")
        ring = view(arena, 5376, RING * G * D).rearrange("p (r g w) -> p r g w", r=RING, g=G)
        ea = view(arena, 7424, 2, 512)
        u1 = view(arena, 8448, 512)
        z2, m2, e2, m1, e1 = (view(arena, 8960 + 512 * n, 512) for n in range(5))
        tile_i = view(score, 0, S).bitcast(I32)[0:1]
        gathered = [sem_take("gathered") for _ in range(RING)]
        free, ea_in, hid = sem_take("ring_taken"), [sem_take("edge_features") for _ in range(2)], sem_take("hidden_product")
        u_ready, filt = sem_take("hidden_ready"), sem_take("filter_product")
        z_ready, f_sum = sem_take("filter_biased"), sem_take("filter_ready")
        relu_done = sem_take("hidden_relu_done")
        half = wbuf[:, 7 * D + 1:7 * D + 2]
        exp1, exp2 = sem_take("hidden_parts"), sem_take("filter_parts")
        load([(tile_i, tiles_dram)])
        with nc.Block() as block:
            pool_gathers(block, table2, D, ring, gathered, free)

            @block.sync
            def _(sp):
                def fetch(par, g, ea_dram):
                    tiles = nc.values_load_multi_w_load_instructions(
                        some(tile_i, g * G, G), engines=(mybir.EngineType.SP,), min_val=0, max_val=T - 1,
                        skip_runtime_bounds_check_because="clamped to the last tile")[1]
                    for j in range(G):
                        h = j // 4
                        sp.dma_start(ea[h * D:(h + 1) * D, par, (j % 4) * P:(j % 4 + 1) * P],
                                     ea_dram[bass.ds(tiles[j], 1), :, :].rearrange("a d e -> (a d) e")).then_inc(ea_in[par], 16)

                def fetch_all(ea_dram):
                    fetch(0, 0, ea_dram)
                    fetch(1, 1, ea_dram)
                    with sp.Fori(1, NG // 2) as r:
                        for par in range(2):
                            sp.wait_ge(hid, (r - 1) * 2 + (par + 1))
                            fetch(par, r * 2 + par, ea_dram)

                by_order = sp.value_load(unsorted[0:1, :], min_val=0, max_val=1)
                with sp.If(by_order > 0):
                    fetch_all(sorted_ea)
                with sp.Else():
                    fetch_all(a["ea"])

            def inside(g, lo=0, hi=NG):
                return not isinstance(g, int) or lo <= g < hi

            def run_groups(eng, body):
                for g in range(RING):
                    body(g, 0, g)
                with eng.Fori(1, NG // RING - 1) as r:
                    for slot in range(RING):
                        body(r * RING + slot, r, slot)
                for g in range(NG - RING, NG + 1):
                    body(g, g // RING, g % RING)

            @block.tensor
            def _(pe):
                def body(g, r, slot):
                    if inside(g + 1):
                        pe.wait_ge(ea_in[(slot + 1) % 2], r * (32 * G) + ((slot + 1) // 2 + 1) * (16 * G))
                        nc.tensor.matmul(ps[:, 4 + (slot + 1) % 2, :], We1, ea[:, (slot + 1) % 2, :],
                                         start=True, stop=True).then_inc(hid, 1)
                    if inside(g):
                        pe.wait_ge(u_ready, g + 1)
                        for j in range(G):
                            h = j // 4
                            last = nc.tensor.matmul(ps[:, 6 + h, (j % 4) * D:(j % 4 + 1) * D],
                                                    u1[h * D:(h + 1) * D, (j % 4) * P:(j % 4 + 1) * P],
                                                    We2[h * D:(h + 1) * D, :], start=True, stop=True)
                        last.then_inc(filt, 1)
                    if inside(g - 1):
                        pe.wait_ge(f_sum, (g - 1) * 2 + 2)
                        pe.wait_ge(onehot_ready, g)
                        places = load_steps(place_i, mybir.EngineType.PE, (g - 1) * G, G)
                        for j in range(G):
                            last = add_step(places[j], onehots[:, ((slot + 1) % 2) * G + j, :],
                                            some(xa, (g - 1) * G + j, 1).rearrange("p a x -> p (a x)"))
                        last.then_inc(done, 1)

                frame_sums(True, narrow=True)
                pe.wait_ge(ea_in[0], 16 * G)
                nc.tensor.matmul(ps[:, 4, :], We1, ea[:, 0, :], start=True, stop=True).then_inc(hid, 1)
                run_groups(pe, body)
                frame_sums(False, narrow=True).then_inc(done, 1)

            @block.scalar
            def _(act):
                def softplus_part(z, log, bias, signal, g):
                    nc.scalar.activation(log, z, ACT.Abs, bias=bias).then_inc(signal, 1)
                    act.wait_ge(signal, g * 3 + 1)
                    nc.scalar.activation(log, log, ACT.Exp, scale=-1.0).then_inc(signal, 1)
                    act.wait_ge(signal, g * 3 + 2)
                    nc.scalar.activation(log, log, ACT.Ln, bias=half, scale=0.5).then_inc(signal, 1)

                def hidden(g, slot):
                    act.wait_ge(hid, g + 1)
                    if not isinstance(g, int) or g:
                        act.wait_ge(u_ready, g)
                    softplus_part(ps[:, 4 + slot % 2, :], e1, be1, exp1, g)

                def body(g, r, slot):
                    if inside(g + 1):
                        hidden(g + 1, slot + 1)
                    if inside(g):
                        act.wait_ge(z_ready, g + 1)
                        softplus_part(z2, e2, 0.0, exp2, g)

                hidden(0, 0)
                run_groups(act, body)

            @block.vector
            def _(dve):
                def hidden_sum(g, slot):
                    dve.wait_ge(exp1, g * 3 + 1)
                    V.tensor_scalar(m1, ps[:, 4 + slot % 2, :], be1, 0.0, ALU.add, ALU.max).then_inc(relu_done, 1)
                    dve.wait_ge(relu_done, g + 1)
                    dve.wait_ge(exp1, g * 3 + 3)
                    V.tensor_tensor(u1, m1, e1, ALU.add).then_inc(u_ready, 1)

                def body(g, r, slot):
                    if inside(g - 1):
                        dve.wait_ge(exp2, (g - 1) * 3 + 3)
                        V.scalar_tensor_tensor(out=m2, in0=z2, scalar=0.0, in1=e2, op0=ALU.max, op1=ALU.add).then_inc(f_sum, 1)
                        dve.wait_ge(f_sum, (g - 1) * 2 + 1)
                        dve.wait_ge(gathered[(slot - 1) % RING], (r + 1 if slot else r) * (16 * G))
                        V.tensor_tensor(some(xa, (g - 1) * G, G)[:, :, 0:D], ring[:, (slot - 1) % RING, :, :],
                                        m2.rearrange("p (g d) -> p g d", g=G), ALU.mult).then_inc(f_sum, 1)
                    if inside(g):
                        dve.wait_ge(filt, g + 1)
                        V.tensor_tensor(z2.rearrange("p (b g d) -> p b g d", b=2, d=D),
                                        ps[:, 6:8, 0:4 * D].rearrange("p b (g d) -> p b g d", d=D),
                                        be2.unsqueeze(1).unsqueeze(1).to_broadcast([P, 2, G // 2, D]), ALU.add).then_inc(z_ready, 1)
                    if inside(g - 1):
                        dve.wait_ge(f_sum, (g - 1) * 2 + 2)
                        dve.nop().then_inc(free, 1)
                    if inside(g + 1):
                        hidden_sum(g + 1, slot + 1)
                    if inside(g):
                        if not isinstance(g, int) or g >= 2:
                            dve.wait_ge(done, g - 1)
                        V.tensor_tensor(onehots[:, (slot % 2) * G:(slot % 2 + 1) * G, :], lane[:, :].unsqueeze(1).to_broadcast([P, G, P]),
                                        some(dsel, g * G, G).unsqueeze(2).to_broadcast([P, G, P]),
                                        ALU.is_equal).then_inc(onehot_ready, 1)

                Vector(dve)[V.memset(xa[:, :, D:X1], 1.0)]
                hidden_sum(0, 0)
                run_groups(dve, body)
                dve.wait_ge(done, NG + 1)
                take_sums(acc, narrow=True)

        def steps(v, ask):
            v[V.memset(acc[:, :, D:X1], 1.0)]
        on_vector(steps)
        z = view(x_all, 0, KN, X1)
        u = view(x_all, KN * X1, KN, X1)
        w = view(x_all, 2 * KN * X1, KN, D)
        dense([acc], [Wc], z[:, :, 0:D])
        zz, uu = z[:, :, 0:D], u[:, :, 0:D]

        def steps(v, ask):
            ask()
            ask()
            ask()
            ask()
            v[V.memset(u[:, :, D:X1], 1.0)]
            v[V.scalar_tensor_tensor(out=uu, in0=w, scalar=-LOG2, in1=zz, op0=ALU.add, op1=ALU.add)]
        on_vector(steps, [lambda: nc.scalar.activation(w, zz, ACT.Relu), lambda: nc.scalar.activation(zz, zz, ACT.Abs),
                          lambda: nc.scalar.activation(zz, zz, ACT.Exp, scale=-1.0),
                          lambda: nc.scalar.activation(zz, zz, ACT.Ln, bias=1.0)])
        y = node[3]
        dense([u], [Wp], y)

        def steps(v, ask):
            v[V.tensor_tensor(y, y, xw, ALU.add)]
        on_vector(steps)
        layernorm(y, node[4], xw)

        table3, table4 = table("table3", D), table("table4", D)
        state = view(arena, 11175, KN, X1)
        recycle()
        for n, (tab_dram, cur) in enumerate(((table3, xs[:, :, :]), (table4, state))):
            l = f"L2_l{n + 1}_"
            qT, kT = (view(x_all, m * 2 * X1, 2, X1)[0:D] for m in range(2))
            kq = wbuf[0:X1, 0:2 * X1]
            wv = wbuf[0:X1, 2 * X1:2 * X1 + 2 * D]
            ws = wbuf[0:X1, 2 * X1 + 2 * D:2 * X1 + 3 * D]
            load([(qT, a[l + "q"]), (kT, a[l + "k"]), (wv, a[l + "v"]), (ws, a[l + "s"])])
            with nc.Block() as block:
                @block.tensor
                def _(pe):
                    for h in range(2):
                        last = nc.tensor.matmul(ps[0:X1, 0, h * X1:(h + 1) * X1], qT[:, h, :], kT[:, h, :], start=True, stop=True)
                    last.then_inc(from_pe.sem, 1)

                @block.vector
                def _(dve):
                    dve.wait_ge(from_pe.sem, from_pe.base + 1)
                    V.tensor_scalar(kq, ps[0:X1, 0, 0:2 * X1], 0.125, None, ALU.mult)
                    V.tensor_scalar(wv, wv, 0.5, None, ALU.mult)
            from_pe.base += 1
            tab = view(arena, tab_at, KN, 2 * X1)
            store([(rows_of(tab_dram), cur[:, :, 0:D])])
            gather_scores(tab_dram, D, 2, tab, True, first=dense_programs([cur], [kq], tab))
            weight, _ = softmax(2, False)
            acc = aggregate(2, weight)
            recycle()
            agg = view(x_all, 0, KN, 2 * X1)

            def steps(v, ask):
                v[V.tensor_copy(agg.rearrange("p k (h x) -> p k h x", h=2)[:, :, :, 0:D], acc.rearrange("p k (h x) -> p k h x", h=2))]
                for h in range(2):
                    v[V.tensor_copy(agg[:, :, h * X1 + D:(h + 1) * X1], has_edges[:, :, :])]
            on_vector(steps)
            y = node[4]
            dense([agg[:, :, 0:X1], agg[:, :, X1:2 * X1], cur], [wv[:, 0:D], wv[:, D:2 * D], ws], y)
            if n == 0:
                def steps(v, ask):
                    v[V.memset(state, 1.0)]
                    v[V.tensor_copy(state[:, :, 0:D], y)]
                on_vector(steps)

        def steps(v, ask):
            v[V.tensor_tensor(y, y, xw, ALU.add)]
        on_vector(steps)
        layernorm(y, node[5], xw)

        Wlh, Wm = wbuf[:, 0:3 * D], wbuf[0:D, 3 * D:6 * D]
        av = view(score, 2 * S, 3, D)
        att = wbuf[:, 6 * D:6 * D + 9]
        ew = view(score, 0, S, 2)

        def steps(v, ask):
            v[V.memset(wbuf[:, 0:6 * D], 0.0)]
        on_vector(steps)
        load([(Wlh[0:D, 0:D], a["L3_gnn_W_low"]), (Wlh[D:P, D:2 * D], a["L3_gnn_W_high"]),
              (Wm[:, 2 * D:3 * D], a["L3_gnn_W_mlp"]), (ew, ew_dram),
              (att, a["L3_gnn_att_vec"].partition_broadcast(P))]
             + [(av[:, n, :], a[f"L3_gnn_av_{m}"].partition_broadcast(P)) for n, m in enumerate(("low", "high", "mlp"))])
        table5 = table("table5", D)
        store([(rows_of(table5), xw)])
        acc = aggregate(2, ew, gather=table5)
        h_all = view(x_all, 5 * KN * D, KN, 3 * D)
        hs = [h_all[:, :, n * D:(n + 1) * D] for n in range(3)]
        dense([acc, xw], [Wlh, Wm], h_all)
        feats = small[:, 0:3 * KN].rearrange("p (n k) -> p n k", n=3)
        logits = small[:, 3 * KN:6 * KN].rearrange("p (n k) -> p n k", n=3)
        extra = view(msg, 0, 2, KN)
        y = node[3]

        def steps(v, ask):
            for m in range(3):
                v[V.tensor_scalar(hs[m], hs[m], 0.0, None, ALU.max)]
                v[V.tensor_tensor(node[4], hs[m], av[:, m:m + 1, :].to_broadcast([P, KN, D]), ALU.mult)]
                v[V.tensor_reduce(feats[:, m, :], node[4], AX, ALU.add)]
            ask()
            for j in range(3):
                v[V.tensor_scalar(logits[:, j, :], feats[:, 0, :], att[:, j:j + 1], None, ALU.mult)]
                for i in range(1, 3):
                    v[V.scalar_tensor_tensor(out=logits[:, j, :], in0=feats[:, i, :], scalar=att[:, 3 * i + j:3 * i + j + 1],
                                             in1=logits[:, j, :], op0=ALU.mult, op1=ALU.add)]
            v[V.tensor_scalar(logits, logits, 1.0 / 3.0, None, ALU.mult)]
            top, tot = extra[:, 0, :], extra[:, 1, :]
            v[V.tensor_tensor(top, logits[:, 0, :], logits[:, 1, :], ALU.max)]
            v[V.tensor_tensor(top, top, logits[:, 2, :], ALU.max)]
            v[V.tensor_tensor(logits, logits, top.unsqueeze(1).to_broadcast([P, 3, KN]), ALU.subtract)]
            ask()
            v[V.tensor_tensor(tot, logits[:, 0, :], logits[:, 1, :], ALU.add)]
            v[V.tensor_tensor(tot, tot, logits[:, 2, :], ALU.add)]
            v[V.reciprocal(tot, tot)]
            v[V.tensor_scalar(tot, tot, 3.0, None, ALU.mult)]
            v[V.tensor_tensor(logits, logits, tot.unsqueeze(1).to_broadcast([P, 3, KN]), ALU.mult)]
            v[V.tensor_copy(y, xw)]
            for m in range(3):
                v[V.tensor_tensor(hs[m], hs[m], logits[:, m, :].unsqueeze(2).to_broadcast([P, KN, D]), ALU.mult)]
                v[V.tensor_tensor(y, y, hs[m], ALU.add)]
        on_vector(steps, [lambda: nc.scalar.activation(feats, feats, ACT.Sigmoid),
                          lambda: nc.scalar.activation(logits, logits, ACT.Exp)])
        layernorm(y, node[4], xw)
        full = N // P
        store([(out[0:full * P, :].rearrange("(k p) d -> p k d", p=P), xs[:, 0:full, 0:D]),
               (out[full * P:N, :], xs[0:N - full * P, full, 0:D])])


def kernel(**inputs):
    import numpy as np
    import concourse.bacc as bacc
    from concourse.bass_utils import run_bass_kernel_spmd

    def padded(x, n, fill=0):
        return np.concatenate([x, np.full((n - len(x),) + x.shape[1:], fill, x.dtype)])

    def tiles(x, fill=0):
        return np.ascontiguousarray(padded(x, EPAD, fill).reshape(T, P).T)

    def biased(w, b):
        return np.ascontiguousarray(np.concatenate([w, b[None]]))

    i = {k: np.asarray(v) for k, v in inputs.items()}
    arrays = {"x": padded(i["x"], NPAD), "src": tiles(i["src"]), "dst": tiles(i["dst"], NPAD - 1)}
    arrays["ea"] = np.ascontiguousarray(padded(i["edge_attr_64"], EPAD).reshape(T, P, D).transpose(0, 2, 1))
    arrays["ew"] = np.ascontiguousarray(np.stack([tiles(i["edge_weight"]), tiles(i["edge_weight_n2"])], 1))
    for k in ("W1", "W2"):
        arrays[f"L0_gnn_{k}"] = i[f"L0_gnn_{k}"]
    for k in ("a1_src", "a1_dst", "a2_src", "a2_dst", "b1", "b2"):
        arrays[f"L0_gnn_{k}"] = i[f"L0_gnn_{k}"].reshape(-1)
    for k, b in (("Wn", "bn"), ("Wc", "bc"), ("Wp", "bp")):
        arrays[f"L1_{k}"] = biased(i[f"L1_gnn_{k}"].T, i[f"L1_gnn_{b}"])
    for k in ("We1", "We2"):
        arrays[f"L1_{k}"] = np.ascontiguousarray(i[f"L1_gnn_{k}"].T)
    for k in ("be1", "be2"):
        arrays[f"L1_gnn_{k}"] = i[f"L1_gnn_{k}"]
    for l in ("l1", "l2"):
        w = {k: biased(i[f"L2_gnn_{l}_w{k}"], i[f"L2_gnn_{l}_b{k}"]) for k in "qkvs"}
        for k in "qk":
            arrays[f"L2_{l}_{k}"] = np.ascontiguousarray(w[k].reshape(X1, 2, D).transpose(2, 1, 0))
        for k in "vs":
            arrays[f"L2_{l}_{k}"] = w[k]
    for k in ("W_low", "W_high", "W_mlp"):
        arrays[f"L3_gnn_{k}"] = i[f"L3_gnn_{k}"]
    for k in ("av_low", "av_high", "av_mlp", "att_vec"):
        arrays[f"L3_gnn_{k}"] = i[f"L3_gnn_{k}"].reshape(-1)

    nc = bacc.Bacc("TRN2", target_bir_lowering=False, num_devices=1)
    arrays = {f"{k}_in": v for k, v in arrays.items()}
    a = {k[:-3]: nc.dram_tensor(k, v.shape, mybir.dt.from_np(v.dtype), kind="ExternalInput").ap()
         for k, v in arrays.items()}
    out = nc.dram_tensor("out", (N, D), F32, kind="ExternalOutput").ap()
    build(nc, a, out)
    r = run_bass_kernel_spmd(nc, [arrays], core_ids=[0])
    return r.results[0]["out"]
```
